# Optimizing a Trainium2 kernel written in Bass

```python
import numpy as np
import jax
import jax.numpy as jnp

def _softmax(x, axis=-1):
    return jax.nn.softmax(x, axis=axis)

def _gelu(x):
    return jax.nn.gelu(x, approximate=True)

def _silu(x):
    return jax.nn.silu(x)

def _sigmoid(x):
    return jax.nn.sigmoid(x)

def _layernorm(x, axis=-1, eps=1e-05):
    m = jnp.mean(x, axis=axis, keepdims=True)
    v = jnp.var(x, axis=axis, keepdims=True)
    return (x - m) / jnp.sqrt(v + eps)

def _scatter_add(tgt, idx, src, axis=0):
    return tgt.at[idx].add(src)

def _segment_sum(src, seg, n):
    return jax.ops.segment_sum(src, seg, n)
kernel_name = 'mk_early_fusion_d1_tok_img1024_r4_6d58b0'

def setup_inputs(seed: int=0):
    np.random.seed(seed)
    _w = jnp.asarray

    def _rec_inputs():
        import jax
        import jax.numpy as jnp
        _rk = jax.random.key(seed)
        x = -0.00016672 + 0.999947 * jax.random.normal(jax.random.fold_in(_rk, 1), (64, 3, 96, 96), jnp.float32)
        txt = 0.00213415 + 1.41303 * jax.random.normal(jax.random.fold_in(_rk, 2), (64, 32, 256), jnp.float32)
        return (x, txt)
    x, txt = _rec_inputs()

    def _L0_tok_setup():
        import jax, jax.numpy as jnp
        import numpy as np
        EMBED_DIM = 256
        IMAGE_SIZE = 96
        CHANNELS = 3
        PATCH = 16
        NUM_PATCHES = (IMAGE_SIZE // PATCH) ** 2
        PATCH_DIM = PATCH * PATCH * CHANNELS

        def _patchify(x, patch):
            B, C, H, W = x.shape
            hp, wp = (H // patch, W // patch)
            x = x.reshape(B, C, hp, patch, wp, patch)
            x = x.transpose(0, 2, 4, 1, 3, 5)
            return x.reshape(B, hp * wp, C * patch * patch)
        key = jax.random.key(seed)
        k_x, k_w, k_b, k_cls, k_pos = jax.random.split(key, 5)
        x = jax.random.normal(k_x, (64, CHANNELS, IMAGE_SIZE, IMAGE_SIZE), dtype=jnp.float32)
        W = jax.random.normal(k_w, (EMBED_DIM, PATCH_DIM), dtype=jnp.float32) / np.sqrt(PATCH_DIM)
        b = jax.random.normal(k_b, (EMBED_DIM,), dtype=jnp.float32) * 0.01
        cls_token = jax.random.normal(k_cls, (1, 1, EMBED_DIM), dtype=jnp.float32)
        pos_embedding = jax.random.normal(k_pos, (1, 1 + NUM_PATCHES, EMBED_DIM), dtype=jnp.float32)
        return {'x': x, 'W': W, 'b': b, 'cls_token': cls_token, 'pos_embedding': pos_embedding}
    _L0_tok_all = _L0_tok_setup()
    _L0_tok_in = {k: v for k, v in _L0_tok_all.items() if k in ('W', 'b', 'cls_token', 'pos_embedding')}
    del _L0_tok_all

    def _L0_attn_setup():
        import jax, jax.numpy as jnp
        import numpy as np
        key = jax.random.key(seed)
        ks = jax.random.split(key, 5)
        B, T, D = (4, 1024, 256)
        x = jax.random.normal(ks[0], (B, T, D), dtype=jnp.float32)
        Wqkv = jax.random.normal(ks[1], (D, 3 * D), dtype=jnp.float32) * D ** (-0.5)
        bqkv = jax.random.normal(ks[2], (3 * D,), dtype=jnp.float32) * 0.02
        Wout = jax.random.normal(ks[3], (D, D), dtype=jnp.float32) * D ** (-0.5)
        bout = jax.random.normal(ks[4], (D,), dtype=jnp.float32) * 0.02
        return {'x': x, 'Wqkv': Wqkv, 'bqkv': bqkv, 'Wout': Wout, 'bout': bout}
    _L0_attn_all = _L0_attn_setup()
    _L0_attn_in = {k: v for k, v in _L0_attn_all.items() if k in ('Wqkv', 'bqkv', 'Wout', 'bout')}
    del _L0_attn_all

    def _L0_ffn_setup():
        import math
        import jax, jax.numpy as jnp
        import numpy as np
        K = 2
        CAP_FACTOR = 1.0
        EPS = 1e-09
        key = jax.random.key(seed)
        ks = jax.random.split(key, 6)
        B, S, D, H, E = (4, 512, 256, 1024, 8)
        x = jax.random.normal(ks[0], (B, S, D), jnp.float32)
        wg = jax.random.normal(ks[1], (D, E), jnp.float32) * 0.02
        w1 = jax.random.normal(ks[2], (E, D, H), jnp.float32) * 0.02
        b1 = jnp.zeros((E, H), jnp.float32)
        w2 = jax.random.normal(ks[3], (E, H, D), jnp.float32) * 0.02
        b2 = jnp.zeros((E, D), jnp.float32)
        return {'x': x, 'wg': wg, 'w1': w1, 'b1': b1, 'w2': w2, 'b2': b2}
    _L0_ffn_all = _L0_ffn_setup()
    _L0_ffn_in = {k: v for k, v in _L0_ffn_all.items() if k in ('wg', 'w1', 'b1', 'w2', 'b2')}
    del _L0_ffn_all
    return {'x': x, 'txt': txt, 'L0_tok_W': _L0_tok_in['W'], 'L0_tok_b': _L0_tok_in['b'], 'L0_tok_cls_token': _L0_tok_in['cls_token'], 'L0_tok_pos_embedding': _L0_tok_in['pos_embedding'], 'L0_attn_Wqkv': _L0_attn_in['Wqkv'], 'L0_attn_bqkv': _L0_attn_in['bqkv'], 'L0_attn_Wout': _L0_attn_in['Wout'], 'L0_attn_bout': _L0_attn_in['bout'], 'L0_ffn_wg': _L0_ffn_in['wg'], 'L0_ffn_w1': _L0_ffn_in['w1'], 'L0_ffn_b1': _L0_ffn_in['b1'], 'L0_ffn_w2': _L0_ffn_in['w2'], 'L0_ffn_b2': _L0_ffn_in['b2']}

def reference(x, txt, L0_tok_W, L0_tok_b, L0_tok_cls_token, L0_tok_pos_embedding, L0_attn_Wqkv, L0_attn_bqkv, L0_attn_Wout, L0_attn_bout, L0_ffn_wg, L0_ffn_w1, L0_ffn_b1, L0_ffn_w2, L0_ffn_b2):
    import jax
    import jax.numpy as jnp

    def _L0_tok_ref(x, W, b, cls_token, pos_embedding):
        import jax, jax.numpy as jnp
        import numpy as np
        EMBED_DIM = 256
        IMAGE_SIZE = 96
        CHANNELS = 3
        PATCH = 16
        NUM_PATCHES = (IMAGE_SIZE // PATCH) ** 2
        PATCH_DIM = PATCH * PATCH * CHANNELS

        def _patchify(x, patch):
            B, C, H, W = x.shape
            hp, wp = (H // patch, W // patch)
            x = x.reshape(B, C, hp, patch, wp, patch)
            x = x.transpose(0, 2, 4, 1, 3, 5)
            return x.reshape(B, hp * wp, C * patch * patch)
        B = x.shape[0]
        patches = _patchify(x, PATCH)
        tokens = jnp.einsum('bnd,ed->bne', patches, W) + b
        cls = jnp.broadcast_to(cls_token, (B, 1, EMBED_DIM))
        out = jnp.concatenate([cls, tokens], axis=1)
        return out + pos_embedding

    def _L0_attn_ref(x, Wqkv, bqkv, Wout, bout):
        import jax, jax.numpy as jnp
        import numpy as np
        qkv = jnp.einsum('btd,de->bte', x, Wqkv) + bqkv
        q, k, v = jnp.split(qkv, 3, axis=-1)
        q = q / jnp.linalg.norm(q, axis=-1, keepdims=True)
        k = k / jnp.linalg.norm(k, axis=-1, keepdims=True)
        kv = jnp.sum(k * v, axis=-2, keepdims=True)
        out = q * kv
        return jnp.einsum('btd,de->bte', out, Wout) + bout

    def _L0_ffn_ref(x, wg, w1, b1, w2, b2):
        import math
        import jax, jax.numpy as jnp
        import numpy as np
        K = 2
        CAP_FACTOR = 1.0
        EPS = 1e-09
        B, S, D = x.shape
        E = wg.shape[1]
        xt = x.reshape(-1, D)
        N = xt.shape[0]
        cap = int(math.ceil(CAP_FACTOR * K * N / E))
        logits = xt.astype(jnp.float32) @ wg.astype(jnp.float32)
        scores = jax.nn.softmax(logits, axis=-1)
        gvals, gidx = jax.lax.top_k(scores, K)
        gvals = gvals / jnp.clip(gvals.sum(-1, keepdims=True), EPS)
        offset = jnp.zeros((E,), jnp.int32)
        pos_l, keep_l = ([], [])
        for kk in range(K):
            m = jax.nn.one_hot(gidx[:, kk], E, dtype=jnp.int32)
            loc = jnp.cumsum(m, axis=0) - 1 + offset[None, :]
            offset = offset + m.sum(axis=0)
            pos = jnp.take_along_axis(loc, gidx[:, kk:kk + 1], axis=1)[:, 0]
            keep = pos < cap
            pos_l.append(jnp.where(keep, pos, 0))
            keep_l.append(keep)
        pos = jnp.stack(pos_l, axis=1)
        keep = jnp.stack(keep_l, axis=1)
        gvals = gvals * keep
        e_flat = gidx.reshape(-1)
        p_flat = pos.reshape(-1)
        kmask = keep.reshape(-1).astype(x.dtype)
        x_rep = jnp.repeat(xt, K, axis=0)
        disp = jnp.zeros((E, cap, D), x.dtype).at[e_flat, p_flat].add(x_rep * kmask[:, None])
        h = jax.nn.gelu(jnp.einsum('ecd,edh->ech', disp, w1) + b1[:, None, :], approximate=False)
        y = jnp.einsum('ech,ehd->ecd', h, w2) + b2[:, None, :]
        yk = y[e_flat, p_flat]
        w = gvals.reshape(-1).astype(x.dtype)
        out = (yk * w[:, None]).reshape(N, K, D).sum(axis=1)
        return out.reshape(B, S, D)
    h = _L0_tok_ref(x, L0_tok_W, L0_tok_b, L0_tok_cls_token, L0_tok_pos_embedding)
    h = jnp.concatenate([h, txt], axis=1)
    h = h + _L0_attn_ref(_layernorm(h, axis=-1), L0_attn_Wqkv, L0_attn_bqkv, L0_attn_Wout, L0_attn_bout)
    h = h + _L0_ffn_ref(_layernorm(h, axis=-1), L0_ffn_wg, L0_ffn_w1, L0_ffn_b1, L0_ffn_w2, L0_ffn_b2)
    return h

_drawn_inputs = setup_inputs


def setup_inputs(seed=0):
    import zlib

    import numpy as np

    out = dict(_drawn_inputs(seed))
    spreads = {'L0_ffn_b1': (0.0, 0.436), 'L0_ffn_b2': (0.0, 0.1)}
    factors = {'L0_tok_b': 8.0, 'L0_attn_bqkv': 37.81, 'L0_attn_bout': 3.678}
    for name, (base, spread) in spreads.items():
        noise = np.random.default_rng([zlib.crc32(name.encode()), seed]).standard_normal(out[name].shape)
        drawn = base * np.exp(spread * noise) if base else spread * noise
        out[name] = jnp.asarray(drawn.astype(out[name].dtype))
    for name, factor in factors.items():
        out[name] = (out[name] * factor).astype(out[name].dtype)
    return out
```

```python
from contextlib import ExitStack

import numpy as np
import concourse.bass as bass
from concourse import mybir

F32 = mybir.dt.float32
F16 = mybir.dt.float16
BF16 = mybir.dt.bfloat16
I32 = mybir.dt.int32
U32 = mybir.dt.uint32
ALU = mybir.AluOpType
ACT = mybir.ActivationFunctionType
AX = mybir.AxisListType.X

P = 128
B, C, IMG, PATCH = 64, 3, 96, 16
HP = IMG // PATCH
NPATCH = HP * HP
D = 256
ND = D // P
KD = C * PATCH * PATCH
NKT = KD // P
TXT = 32
SEQ = 1 + NPATCH + TXT
N = B * SEQ
G = 5
NG = -(-N // (P * G))
NT = NG * G
NPAD = NT * P
LAST = N - (NT - 1) * P
E, TOP, HID = 8, 2, 1024
CAP = -(-TOP * N // E)
NS = -(-CAP // P)
CH = 3
ST = NS // CH
NM = HID // P
XW = D + TOP
EPS = 1e-5
GATE_EPS = 1e-9
SCALE = 64.0
NOWHERE = 1000.0
BIG = 3.0e38
KEY = NS * E


def after(engine, sem, value):
    if not isinstance(value, int) or value > 0:
        engine.wait_ge(sem, value)


def before(i, t):
    return i + 1 - (1 if t == 0 else 3 if t == 1 else 2)


def apart(engine):
    engine.nop(nofuse=True)


class Own:

    def __init__(self, engine, sem):
        self.engine, self.sem, self.base, self.n = engine, sem, 0, 0

    def step(self, base):
        self.base, self.n = base, 0

    def __call__(self, instruction):
        instruction.then_inc(self.sem, 1)
        self.n += 1
        self.engine.wait_ge(self.sem, self.base + self.n)


def build(nc, x, txt, tok_w, tok_b, cls, pos, wqkv, bqkv, wout, bout, wg, w1, b1, w2, b2, out):
    ctx = ExitStack()
    with ctx:
        def sb(name, shape, dt=F32):
            return ctx.enter_context(nc.sbuf_tensor(name, shape, dt))

        def sem(name):
            return ctx.enter_context(nc.semaphore(name))

        h_rows = nc.dram_tensor("h_rows", (NPAD, D), F32, kind="Internal").ap()
        x_rows = nc.dram_tensor("x_rows", (NPAD, XW), F32, kind="Internal").ap()

        region_h = sb("region_h", [P, NT * D])
        region_q = sb("region_q", [P, NT * D])
        region_x = sb("region_x", [P, KD * HP * (HP // 2)])
        region_i = sb("region_i", [P, NPAD // 2 + (NT + 1) * B])

        h_all = region_h[:, :].rearrange("p (i d) -> p i d", d=D)
        q_all = region_q[:, :].rearrange("p (i d) -> p i d", d=D)
        tokw_raw = region_h[:, 0:2 * KD].rearrange("p (t k) -> p t k", t=2)
        qkv_raw = region_h[:, 2 * KD:2 * KD + ND * 3 * D].rearrange("p (k n) -> p k n", k=ND)
        wo_raw = region_h[:, 4 * KD:4 * KD + ND * D].rearrange("p (k n) -> p k n", k=ND)
        bq_raw = region_h[:, 5 * KD:5 * KD + 3 * D]
        tokb_b = region_h[:, 6 * KD:6 * KD + D]
        cls_b = region_h[0:B, 6 * KD + D:6 * KD + 2 * D]
        pos0_b = region_h[0:B, 6 * KD + 2 * D:6 * KD + 3 * D]
        zeros = region_h[0:P, 6 * KD + 3 * D:6 * KD + 4 * D]
        b1_raw = region_h[0:E * NM, 6 * KD + 4 * D:6 * KD + 4 * D + P]
        NTX = HP // 2
        pos_b = region_q[:, 0:NTX * HP * D].rearrange("p (t w d) -> p t w d", t=NTX, w=HP)
        store = region_q[:, NTX * HP * D:(NTX + 2) * HP * D].rearrange("p (s w d) -> p s w d", s=2, w=HP)
        x_sb = region_x[:, :].rearrange("p (t c i w j) -> p t c i w j", t=NTX, c=C, i=PATCH, w=HP)
        ind_t = region_i[:, 0:NPAD // 2].bitcast(F16)
        ind = region_i[:, NPAD // 2:].rearrange("p (i b) -> p i b", b=B)
        WR = ND * HID
        w1_raw = region_x[:, 0:WR].rearrange("p (k n) -> p k n", k=ND)
        w2_raw = region_x[:, WR:2 * WR].rearrange("p (k n) -> p k n", k=NM)
        halves = [region_x[:, 2 * WR + s * 2 * WR:2 * WR + (s + 1) * 2 * WR].bitcast(F16) for s in range(2)]
        w1h = [v[:, 0:WR].rearrange("p (k n) -> p k n", k=ND) for v in halves]
        w1l = [v[:, WR:2 * WR].rearrange("p (k n) -> p k n", k=ND) for v in halves]
        w2h = [v[:, 2 * WR:3 * WR].rearrange("p (k n) -> p k n", k=NM) for v in halves]
        w2l = [v[:, 3 * WR:4 * WR].rearrange("p (k n) -> p k n", k=NM) for v in halves]
        HW = NM * ST * P // 2
        hid_h = [region_q[:, (2 * s) * HW:(2 * s + 1) * HW].bitcast(F16).rearrange("p (m n) -> p m n", m=NM) for s in range(2)]
        hid_l = [region_q[:, (2 * s + 1) * HW:(2 * s + 2) * HW].bitcast(F16).rearrange("p (m n) -> p m n", m=NM) for s in range(2)]
        rows = [region_i[:, 0:NS * XW].rearrange("p (j d) -> p j d", d=XW),
                region_q[:, 4 * HW:4 * HW + NS * XW].rearrange("p (j d) -> p j d", d=XW)]

        tokw_h, tokw_l = (sb(n, [P, NKT, D], F16) for n in ("tokw_h", "tokw_l"))
        qkv_h, qkv_l = (sb(n, [P, ND, 3 * D], F16) for n in ("qkv_h", "qkv_l"))
        wo_h, wo_l = (sb(n, [P, ND, D], F16) for n in ("wo_h", "wo_l"))
        bq_hl = sb("bq_hl", [P, 3 * D], F16)
        wg_sb = sb("wg_sb", [P, ND, E])
        bout_b = sb("bout_b", [P, D])
        b1_cols = sb("b1_cols", [P, E * NM])
        ident = sb("ident", [P, P])
        upper = sb("upper", [P, P], BF16)
        ones_b = sb("ones_b", [P, P], BF16)
        ones_h = sb("ones_h", [P, P], F16)
        zero_h = sb("zero_h", [P, TOP * KEY], F16)
        ones_f = sb("ones_f", [P, 1])
        lane = sb("lane", [P, P])
        keys = sb("keys", [P, KEY])
        slot = sb("slot", [P, KEY])
        token = sb("token", [P, NT])
        trash = sb("trash", [P, 1])
        rev = sb("rev", [P, E])
        half = sb("half", [P, NT])
        pat_h, pat_l = (sb(n, [P, 2, KD], F16) for n in ("pat_h", "pat_l"))
        stats = sb("stats", [P, G, 6])
        mv = sb("mv", [P, G, 2])
        veps = sb("veps", [P, G])
        rstd = sb("rstd", [P, G])
        nmr = sb("nmr", [P, G])
        trio = sb("trio", [P, 6 * D])
        patch = trio[:, :].rearrange("p (s k) -> p s k", s=2)
        xn, sq, vs = (trio[:, 2 * k * D:2 * (k + 1) * D].rearrange("p (s d) -> p s d", s=2) for k in range(3))
        xh, xl = (sb(n, [P, 2, D], F16) for n in ("xh", "xl"))
        junk = sb("junk", [P, D])
        nk = sb("nk", [P, G])
        rk = sb("rk", [P, G])
        kvp = sb("kvp", [P, 2, D])
        nq = sb("nq", [P, NT])
        rq = sb("rq", [P, NT])
        kvt = sb("kvt", [P, ND, P])
        kv_hl = sb("kv_hl", [P, D], F16)
        x2 = sb("x2", [P, G, D])
        w_cols = sb("w_cols", [P, G, TOP])
        lg = sb("lg", [P, G, E])
        lg2 = sb("lg2", [P, G, E])
        same = sb("same", [P, G, E])
        m12 = sb("m12", [P, G, 2])
        er = sb("er", [P, G, TOP])
        pick = sb("pick", [P, G, TOP * E], BF16)
        cum = sb("cum", [P, G + 1, TOP * E], BF16)
        ex = sb("ex", [P, G, E + 1])
        ssum = sb("ssum", [P, G])
        gp = sb("gp", [P, G, TOP])
        gt = sb("gt", [P, G])
        pm = sb("pm", [P, G, TOP * E])
        posn = sb("posn", [P, G, TOP])
        hi_i = sb("hi_i", [P, G, TOP], I32)
        lo_f = sb("lo_f", [P, G, TOP])
        bad = sb("bad", [P, G, TOP])
        key = sb("key", [P, G, TOP])
        hot_lo = sb("hot_lo", [P, G * TOP, P])
        hot_key = sb("hot_key", [P, G * TOP, KEY])
        cnt = sb("cnt", [P, TOP * E])
        t0 = sb("t0", [P, KEY])
        t1 = sb("t1", [P, KEY])
        ids = sb("ids", [P, KEY])
        tmp = sb("tmp", [P, KEY])
        from_i = sb("from_i", [P, KEY], U32)
        to_i = sb("to_i", [P, KEY], U32)
        from_e = sb("from_e", [P, 2, NS], U32)
        to_e = sb("to_e", [P, 2, NS], U32)
        b2_b = sb("b2_b", [P, 2, D])
        ws = sb("ws", [P, 2, NS])
        wtmp = sb("wtmp", [P, 2, NS])
        xt_h, xt_l = (v[:, :, :].rearrange("p s (k n) -> p s k n", k=ND) for v in (pat_h, pat_l))
        hf = hot_lo[:, 0:6, :].rearrange("p (s n) c -> p s (n c)", s=2)
        b2w = sb("b2w", [P, 2, D])
        y_sb = sb("y_sb", [P, 3, D])

        bank = [ctx.enter_context(nc.psum_tensor(f"bank{k}", [P, 512], F32)) for k in range(8)]

        (raw_in, raw2_in, consts, qkv_hi, qkv_lo, pos_in, pos_sum, row0_sum, txt_out, cls_out, pad_out,
         pool_own, dve_own, act_own) = (sem(n) for n in (
             "raw_in", "raw2_in", "consts", "qkv_hi", "qkv_lo", "pos_in", "pos_sum", "row0_sum", "txt_out", "cls_out",
             "pad_out", "pool_own", "dve_own", "act_own"))
        patch_out = [sem(f"patch_out{t}") for t in range(NTX)]
        x_in = [sem(f"x_in{t}") for t in range(NTX)]
        tk_patch, tk_turned, tk_hi, tk_lo, tk_prod, tk_row, b1_turned, b1_ok = (sem(n) for n in (
            "tk_patch", "tk_turned", "tk_hi", "tk_lo", "tk_prod", "tk_row", "b1_turned", "b1_ok"))
        (h_in, a_var, a_rstd, a_xn, a_turned, a_hi, a_lo, a_q, a_kv, a_qsq, a_v, a_rk, a_kvp, a_nq, a_acc, a_nqc) = (
            sem(n) for n in ("h_in", "a_var", "a_rstd", "a_xn", "a_turned", "a_hi", "a_lo", "a_q", "a_kv", "a_qsq",
                             "a_v", "a_rk", "a_kvp", "a_nq", "a_acc", "a_nqc"))
        kv_copied, kv_turned, kv_hi, kv_ready, rq_ready = (sem(n) for n in (
            "kv_copied", "kv_turned", "kv_hi", "kv_ready", "rq_ready"))
        (b_kvb, b_qk, b_qhi, b_qlo, b_prod, b_hb, b_h2, b_var, b_rstd, b_xn, b_turned, b_xt, b_logit, b_lg, b_pick,
         b_rank, b_ex_in, b_ex, b_w, b_hot, b_inv, out_in, rows_out) = (sem(n) for n in (
             "b_kvb", "b_qk", "b_qhi", "b_qlo", "b_prod", "b_hb", "b_h2", "b_var", "b_rstd", "b_xn", "b_turned",
             "b_xt", "b_logit", "b_lg", "b_pick", "b_rank", "b_ex_in", "b_ex", "b_w", "b_hot", "b_inv",
             "out_in", "rows_out"))
        w_out = sem("w_out")
        pad2_out = sem("pad2_out")
        counted, tables = sem("counted"), sem("tables")
        w1_in, w2_in, w1_hi, w1_lo, w2_hi, w2_lo, b2_in = (sem(n) for n in (
            "w1_in", "w2_in", "w1_hi", "w1_lo", "w2_hi", "w2_lo", "b2_in"))
        got = [[sem(f"got{s}_{g}") for g in range(CH)] for s in range(2)]
        (idx_ok, e_turned, e_xhi, e_xlo, e_up, e_gelu, e_hhi, e_hlo, e_down, e_y, added) = (sem(n) for n in (
            "idx_ok", "e_turned", "e_xhi", "e_xlo", "e_up", "e_gelu", "e_hhi", "e_hlo", "e_down", "e_y", "added"))

        def tile(region, i):
            return region[:, i, :] if isinstance(i, int) else region[:, bass.ds(i, 1), :].rearrange("p a d -> p (a d)")

        def gathered(e, s):
            return ((e - s) // 2 + 1) * ST * 16 if isinstance(e, int) else (e - s + 2) * (ST * 8)

        block = ctx.enter_context(nc.Block())
        NF = 2 * (2 + NTX * HP)
        NX = NTX * HP

        @block.sync
        def _(sp):
            sp.dma_start(tokw_raw, tok_w.rearrange("(t p) k -> p t k", p=P)).then_inc(raw_in, 16)
            for t in range(NTX):
                for hh in range(2):
                    src = x[:, :, (2 * t + hh) * PATCH:(2 * t + hh + 1) * PATCH, :].rearrange("b c i w -> b c (i w)")
                    dst = x_sb[hh * B:(hh + 1) * B, t].rearrange("p c i w j -> p c (i w j)")
                    sp.dma_start(dst, src).then_inc(x_in[t], 16)
            for k, v in ((qkv_raw, wqkv), (wo_raw, wout), (wg_sb[:, :, :], wg)):
                sp.dma_start(k, v.rearrange("(k p) n -> p k n", p=P)).then_inc(raw2_in, 16)
            h_seq = h_rows[0:N, :].rearrange("(b s) d -> b s d", s=SEQ)
            sp.dma_start(h_seq[:, 1 + NPATCH:, :], txt).then_inc(txt_out, 16)
            sp.wait_ge(row0_sum, 1)
            sp.dma_start(h_seq[:, 0, :], cls_b).then_inc(cls_out, 16)
            sp.wait_ge(consts, 1)
            sp.dma_start(h_rows[N:, :], zeros[0:NPAD - N, :]).then_inc(pad_out, 16)
            sp.dma_start(out[NPAD:, :], zeros[0:N + P - NPAD, :]).then_inc(pad2_out, 16)
            for t in range(NTX):
                sp.wait_ge(tk_row, HP * (t + 1))
                for hh in range(2):
                    first = 1 + (2 * t + hh) * HP
                    sp.dma_start(h_seq[:, first:first + HP, :], store[hh * B:(hh + 1) * B, t % 2, :, :]).then_inc(patch_out[t], 16)
            for done, n in ((txt_out, 1), (cls_out, 1), (pad_out, 1), (pad2_out, 1), *((v, 2) for v in patch_out)):
                sp.wait_ge(done, 16 * n)
            sp.wait_ge(b1_ok, 1)
            sp.wait_ge(qkv_hi, 1)
            sp.wait_ge(qkv_lo, 2)
            sp.wait_ge(pos_sum, 1)
            h_src = h_rows.rearrange("(i p) d -> p i d", p=P)
            with sp.Fori(0, NG) as c:
                sp.dma_start(h_all[:, bass.ds(c * G, G), :], h_src[:, bass.ds(c * G, G), :]).then_inc(h_in, 16)
                sp.wait_ge(h_in, c * 16 + 16)
                apart(sp)
            def one(v, e):
                return v[e] if isinstance(e, int) else v[bass.ds(e, 1)].squeeze(0)

            def w1_of(e):
                return one(w1, e).rearrange("(k p) n -> p k n", p=P)

            def w2_of(e):
                return one(w2, e).rearrange("(k p) n -> p k n", p=P)

            def b2_of(e):
                return one(b2, e)

            sp.wait_ge(tk_turned, NF)
            sp.dma_start(w1_raw, w1_of(0)).then_inc(w1_in, 16)
            sp.dma_start(w2_raw, w2_of(0)).then_inc(w2_in, 16)
            sp.dma_start(b2_b[:, 0, :], b2_of(0).partition_broadcast(P)).then_inc(b2_in, 16)
            o_dst = out[0:NPAD, :].rearrange("(i p) d -> p i d", p=P)
            x_dst = x_rows.rearrange("(i p) d -> p i d", p=P)
            with sp.Fori(0, NG) as c:
                sp.wait_ge(b_h2, c * G + G)
                sp.dma_start(o_dst[:, bass.ds(c * G, G), :], h_all[:, bass.ds(c * G, G), :]).then_inc(out_in, 16)
                sp.wait_ge(b_xn, c * G + G)
                sp.dma_start(x_dst[:, bass.ds(c * G, G), 0:D], x2[:, :, :]).then_inc(rows_out, 16)
                sp.wait_ge(b_w, c + 1)
                sp.dma_start(x_dst[:, bass.ds(c * G, G), D:XW], w_cols[:, :, :]).then_inc(w_out, 16)
            def feed(e, s):
                sp.wait_ge(w1_hi, e)
                sp.wait_ge(w1_lo, e)
                sp.dma_start(w1_raw, w1_of(e)).then_inc(w1_in, 16)
                sp.wait_ge(w2_hi, e)
                sp.wait_ge(w2_lo, e)
                sp.dma_start(w2_raw, w2_of(e)).then_inc(w2_in, 16)
                after(sp, e_y, e * NS - NS)
                apart(sp)
                sp.wait_ge(b2_in, e * 16)
                apart(sp)
                sp.dma_start(b2_b[:, s, :], b2_of(e).partition_broadcast(P)).then_inc(b2_in, 16)

            feed(1, 1)
            with sp.Fori(0, (E - 2) // 2) as k:
                feed(k * 2 + 2, 0)
                feed(k * 2 + 3, 1)

        @block.gpsimd
        def _(pool):
            own = Own(pool, pool_own)
            pool.memset(zeros, 0.0).then_inc(consts, 1)
            own(pool.memset(ident[:, :], 0.0))
            own(pool.affine_select(out=ident[:, :], in_=ident[:, :], compare_op=ALU.not_equal, fill=1.0,
                                   base=0, pattern=[[-1, P]], channel_multiplier=1))
            pool.memset(ones_h[:, :], 1.0)
            pool.memset(zero_h[:, :], 0.0)
            pool.memset(ones_f[:, :], 1.0)
            pool.memset(half[:, :], -0.5)
            own(pool.memset(ones_b[:, :], 1.0))
            own(pool.affine_select(out=upper[:, :], in_=ones_b[:, :], compare_op=ALU.is_gt, fill=0.0,
                                   base=0, pattern=[[1, P]], channel_multiplier=-1))
            pool.iota(lane[:, :], [[1, P]], base=0, channel_multiplier=0, allow_small_or_imprecise_dtypes=True)
            pool.iota(keys[:, :], [[1, KEY]], base=-KEY, channel_multiplier=0, allow_small_or_imprecise_dtypes=True)
            pool.iota(slot[:, :].rearrange("p (e j) -> p e j", e=E), [[0, E], [P, NS]], base=0, channel_multiplier=1,
                      allow_small_or_imprecise_dtypes=True)
            pool.iota(token[:, :], [[P, NT]], base=0, channel_multiplier=1, allow_small_or_imprecise_dtypes=True)
            pool.iota(trash[:, :], [[1, 1]], base=N, channel_multiplier=1, allow_small_or_imprecise_dtypes=True)
            pool.iota(rev[:, :], [[-1, E]], base=E, channel_multiplier=0,
                      allow_small_or_imprecise_dtypes=True)
            pool.memset(cum[:, :, :], 0.0).then_inc(consts, 1)
            pool.wait_ge(pos_in, 16 * 5)
            for t in range(NTX):
                last = pool.tensor_tensor(pos_b[:, t], pos_b[:, t], tokb_b.unsqueeze(1).to_broadcast([P, HP, D]), ALU.add)
            last.then_inc(pos_sum, 1)
            pool.tensor_tensor(cls_b, cls_b, pos0_b, ALU.add).then_inc(row0_sum, 1)
            pool.memset(ind, 1.0)
            own(pool.memset(ind_t, 1.0))
            own(pool.affine_select(out=ind, in_=ind, compare_op=ALU.is_ge, fill=0.0, base=-P,
                                   pattern=[[P, NT + 1], [-SEQ, B]], channel_multiplier=1))
            own(pool.affine_select(out=ind, in_=ind, compare_op=ALU.is_ge, fill=0.0, base=P + SEQ - 1,
                                   pattern=[[-P, NT + 1], [SEQ, B]], channel_multiplier=-1))
            for s in range(2):
                part = ind_t[s * B:(s + 1) * B, :]
                own(pool.affine_select(out=part, in_=part, compare_op=ALU.is_ge, fill=0.0, base=0,
                                       pattern=[[1, NPAD]], channel_multiplier=-SEQ))
                own(pool.affine_select(out=part, in_=part, compare_op=ALU.is_ge, fill=0.0, base=SEQ - 1,
                                       pattern=[[-1, NPAD]], channel_multiplier=SEQ))
            pool.nop().then_inc(consts, 1)

            n0 = own.n
            with pool.Fori(0, NG) as c:
                pool.wait_ge(a_var, c + 1)
                pool.tensor_tensor(rstd[:, :], veps[:, :], half[:, 0:G], ALU.pow).then_inc(a_rstd, 1)
                for t in range(G):
                    pool.wait_ge(a_v, c * G + t + 1)
                    pool.tensor_tensor(rk[:, t:t + 1], nk[:, t:t + 1], half[:, 0:1], ALU.pow).then_inc(a_rk, 1)
            pool.wait_ge(a_nqc, NG)
            own.step(n0)
            own(pool.tensor_tensor(rq[:, :], nq[:, :], half[:, :], ALU.pow))
            pool.tensor_scalar(rq[:, :], rq[:, :], 1.0 / SCALE, None, ALU.mult).then_inc(rq_ready, 1)

            n1 = n0 + own.n
            with pool.Fori(0, NG) as c:
                pool.tensor_tensor(h_all[:, bass.ds(c * G, G), :], h_all[:, bass.ds(c * G, G), :],
                                   bout_b[:, :].unsqueeze(1).to_broadcast([P, G, D]), ALU.add).then_inc(b_hb, 1)
                for t in range(G):
                    pool.wait_ge(b_qhi, c * G + t + 1)
                    pool.tensor_tensor(xl[:, t % 2, :], sq[:, t % 2, :], xh[:, t % 2, :], ALU.subtract).then_inc(b_qlo, 1)
                pool.wait_ge(b_var, c + 1)
                pool.tensor_tensor(rstd[:, :], veps[:, :], half[:, 0:G], ALU.pow).then_inc(b_rstd, 1)

            def pull(e, s):
                apart(pool)
                for j in range(NS):
                    m = min(P, CAP - j * P)
                    pool.indirect_dma_start(out=rows[s][0:m, j, :], out_offset=None, in_=x_rows,
                                            in_offset=bass.IndirectOffsetOnAxis(ap=from_e[0:m, s, j:j + 1], axis=0)
                                            ).then_inc(got[s][j // ST], 16)

            pool.wait_ge(tables, 1)
            pool.tensor_copy(from_e[:, 0, :], from_i[:, 0:NS])
            own.step(n1)
            own(pool.tensor_copy(to_e[:, 0, :], to_i[:, 0:NS]))
            pool.wait_ge(rows_out, 16 * NG)
            pool.wait_ge(w_out, 16 * NG)
            pull(0, 0)
            pool.wait_ge(out_in, 16 * NG)
            pool.wait_ge(pad2_out, 16)
            n2 = n1 + own.n

            def expert(e, s, last):
                if not last:
                    after(pool, e_turned, e * NS)
                    after(pool, added, e * NS * 16)
                    pool.tensor_copy(from_e[:, 1 - s, :], from_i[:, bass.ds((e + 1) * NS, NS)])
                    own(pool.tensor_copy(to_e[:, 1 - s, :], to_i[:, bass.ds((e + 1) * NS, NS)]))
                    pull(e + 1, 1 - s)
                for j in range(NS):
                    m = min(P, CAP - j * P)
                    pool.wait_ge(e_y, e * NS + j + 1)
                    after(pool, added, (e * NS + j) * 16)
                    apart(pool)
                    pool.indirect_dma_start(out=out, out_offset=bass.IndirectOffsetOnAxis(ap=to_e[0:m, s, j:j + 1], axis=0),
                                            in_=y_sb[0:m, j % 3, :], in_offset=None, compute_op=ALU.add
                                            ).then_inc(added, 16)

            own.step(n2)
            expert(0, 0, False)
            n3 = n2 + own.n
            with pool.Fori(0, (E - 2) // 2) as k:
                own.step(k * 2 + n3)
                expert(k * 2 + 1, 1, False)
                expert(k * 2 + 2, 0, False)
            expert(E - 1, 1, True)
            pool.wait_ge(added, 16 * NS * E)

        @block.scalar
        def _(act):
            p_all = pos[0, 1:, :].rearrange("(t hh w) d -> hh t w d", hh=2, w=HP)
            for hh in range(2):
                act.dma_start(pos_b[hh * B:(hh + 1) * B].rearrange("p t w d -> p t (w d)"),
                              p_all[hh].rearrange("t w d -> t (w d)").partition_broadcast(B)).then_inc(pos_in, 16)
            act.dma_start(tokb_b, tok_b.partition_broadcast(P)).then_inc(pos_in, 16)
            act.dma_start(cls_b, cls[0, 0, :].partition_broadcast(B)).then_inc(pos_in, 16)
            act.dma_start(pos0_b, pos[0, 0, :].partition_broadcast(B)).then_inc(pos_in, 16)
            act.dma_start(bout_b[:, :], bout.partition_broadcast(P)).then_inc(raw2_in, 16)
            act.dma_start(b1_raw, b1.rearrange("e (m p) -> (e m) p", p=P)).then_inc(raw2_in, 16)
            act.wait_ge(qkv_lo, 1)
            for r in (0, 32):
                act.dma_start(bq_raw[r:r + 1, :], bqkv.unsqueeze(0)).then_inc(raw2_in, 16)

            def gather_patches(s):
                if s % HP == 0:
                    act.wait_ge(x_in[s // HP], 32)
                if s >= 2:
                    act.wait_ge(tk_turned, 4 + 2 * (s - 1))
                act.activation(patch[:, s % 2, :].rearrange("p (r j) -> p r j", j=PATCH),
                               x_sb[:, s // HP, :, :, s % HP, :].rearrange("p c i j -> p (c i) j"), ACT.Copy).then_inc(tk_patch, 1)

            def high(f):
                act.wait_ge(tk_turned, f + 1)
                step, part = f // 2, f % 2
                src = bank[f % 4][:, 0:3 * P]
                if step < 2:
                    dst = tokw_h[:, 3 * part:3 * part + 3, step * P:(step + 1) * P]
                    act.activation(dst, src.rearrange("p (k n) -> p k n", k=3), ACT.Copy, scale=SCALE).then_inc(tk_hi, 1)
                else:
                    s = step - 2
                    after(act, tk_prod, s - 1)
                    act.activation(pat_h[:, s % 2, part * 3 * P:(part + 1) * 3 * P], src, ACT.Copy).then_inc(tk_hi, 1)
            gather_patches(0)
            gather_patches(1)
            for f in range(8):
                high(f)
                if f >= 5 and f % 2 == 1:
                    gather_patches(f // 2)
            act.wait_ge(raw2_in, 16 * 7)
            act.activation(qkv_h[:, :, :], qkv_raw, ACT.Copy, scale=SCALE)
            act.activation(wo_h[:, :, :], wo_raw, ACT.Copy, scale=SCALE)
            act.activation(bq_hl[:, :], bq_raw, ACT.Copy, scale=SCALE).then_inc(qkv_hi, 1)
            for f in range(8, NF):
                high(f)
                if f % 2 == 1 and f // 2 < NX:
                    gather_patches(f // 2)
            act.wait_ge(b1_turned, 1)
            act.activation(b1_cols[:, :], bank[0][:, 0:E * NM], ACT.Copy).then_inc(b1_ok, 1)

            def project(c):
                for t in range(G):
                    i = c * G + t
                    s = t % 2
                    act.wait_ge(a_turned, i + 1)
                    after(act, a_kv, before(i, t))
                    act.activation(xh[:, s, :], bank[s][:, 0:D], ACT.Copy).then_inc(a_hi, 1)
                    act.wait_ge(a_q, i + 1)
                    after(act, a_nq, before(i, t))
                    apart(act)
                    act.activation(tile(q_all, i), bank[2 + s][:, 0:D], ACT.Copy)
                    act.activation(sq[:, s, :], bank[2 + s][:, 0:D], ACT.Square).then_inc(a_qsq, 1)
                    act.wait_ge(a_kv, i + 1)
                    after(act, a_kvp, before(i, t))
                    act.activation(vs[:, s, :], bank[4 + s][:, D:2 * D], ACT.Copy)
                    act.activation(junk[:, :], bank[4 + s][:, 0:D], ACT.Square, accum_out=nk[:, t:t + 1]).then_inc(a_v, 1)
            project(0)
            with act.Fori(1, NG) as c:
                project(c)
            act.wait_ge(a_acc, NT)
            for r in range(2):
                last = act.activation(kvt[:, :, r * B:(r + 1) * B], bank[6][:, 0:ND * B].rearrange("p (k b) -> p k b", k=ND),
                                      ACT.Copy, scale=1.0 / SCALE)
            last.then_inc(kv_copied, 1)
            act.wait_ge(kv_turned, 1)
            act.activation(kv_hl[:, :], bank[7][:, 0:D], ACT.Copy).then_inc(kv_hi, 1)

            def attend(c):
                for t in range(G):
                    i = c * G + t
                    act.wait_ge(b_qk, i + 1)
                    after(act, b_prod, before(i, t))
                    act.activation(xh[:, t % 2, :], sq[:, t % 2, :], ACT.Copy).then_inc(b_qhi, 1)
                if not (isinstance(c, int) and c == 0):
                    gate_exp(c - 1)
                for t in range(G):
                    i = c * G + t
                    act.wait_ge(b_turned, i + 1)
                    after(act, b_logit, before(i, t))
                    act.activation(xn[:, t % 2, :], bank[4 + t % 2][:, 0:D], ACT.Copy).then_inc(b_xt, 1)
                act.wait_ge(b_logit, c * G + G)
                after(act, b_w, c)
                act.activation(lg[:, :, :], bank[6][:, 0:G * E].rearrange("p (t e) -> p t e", e=E), ACT.Copy).then_inc(b_lg, 1)

            def gate_exp(c):
                act.wait_ge(b_ex_in, c + 1)
                act.activation(ex[:, :, :], ex[:, :, :], ACT.Exp).then_inc(b_ex, 1)

            attend(0)
            with act.Fori(1, NG) as c:
                attend(c)
            gate_exp(NG - 1)

            def split_w1(e, s):
                act.wait_ge(w1_in, e * 16 + 16)
                act.activation(w1h[s], w1_raw, ACT.Copy, scale=SCALE).then_inc(w1_hi, 1)

            def split_w2(e, s):
                act.wait_ge(w2_in, e * 16 + 16)
                act.activation(w2h[s], w2_raw, ACT.Copy, scale=SCALE).then_inc(w2_hi, 1)

            split_w1(0, 0)
            split_w2(0, 0)

            def expert(e, s, last):
                for g in range(CH):
                    w = min(ST * P, CAP - g * ST * P)
                    u = e * CH + g
                    v = (s + g) % 2
                    for j in range(ST):
                        m = min(P, w - j * P)
                        k = u * ST + j
                        act.wait_ge(e_turned, k + 1)
                        if j == 0:
                            after(act, e_up, (u - 1) * NM)
                        act.activation(xt_h[:, v, :, j * P:j * P + m],
                                       bank[(s + g * ST + j) % 2][:, 0:D].rearrange("p (k n) -> p k n", k=ND)[:, :, 0:m],
                                       ACT.Copy).then_inc(e_xhi, 1)
                    for m in range(NM):
                        k = u * NM + m
                        act.wait_ge(e_up, k + 1)
                        after(act, e_hlo, k - 1)
                        apart(act)
                        bcol = b1_cols[:, m:m + 1] if isinstance(e, int) and e == 0 else b1_cols[:, bass.ds(e * NM + m, 1)]
                        act.activation(hf[:, m % 2, 0:w], bank[2 + m % 4 if m % 4 < 3 else 7][:, 0:w], ACT.Gelu,
                                       bias=bcol, scale=1.0 / SCALE).then_inc(e_gelu, 1)
                    if g == 0 and not last:
                        split_w1(e + 1, 1 - s)
                    if g == 1 and not last:
                        after(act, e_down, e * NS)
                        split_w2(e + 1, 1 - s)

            expert(0, 0, False)
            with act.Fori(0, (E - 2) // 2) as k:
                expert(k * 2 + 1, 1, False)
                expert(k * 2 + 2, 0, False)
            expert(E - 1, 1, True)

        @block.vector
        def _(dve):
            own = Own(dve, dve_own)
            own(dve.memset(bq_raw, 0.0))
            dve.nop().then_inc(qkv_lo, 1)

            def low(f):
                act_done = f + 1
                dve.wait_ge(tk_hi, act_done)
                step, part = f // 2, f % 2
                src = bank[f % 4][:, 0:3 * P]
                if step < 2:
                    o = tokw_l[:, 3 * part:3 * part + 3, step * P:(step + 1) * P]
                    i1 = tokw_h[:, 3 * part:3 * part + 3, step * P:(step + 1) * P]
                    dve.scalar_tensor_tensor(o, src.rearrange("p (k n) -> p k n", k=3), SCALE, i1,
                                             ALU.mult, ALU.subtract).then_inc(tk_lo, 1)
                else:
                    s = step - 2
                    after(dve, tk_prod, s - 1)
                    cut = slice(part * 3 * P, (part + 1) * 3 * P)
                    dve.tensor_tensor(pat_l[:, s % 2, cut], src, pat_h[:, s % 2, cut], ALU.subtract).then_inc(tk_lo, 1)

            def row(s):
                t, w = s // HP, s % HP
                dve.wait_ge(tk_prod, s + 1)
                if s == 0:
                    dve.wait_ge(pos_sum, 1)
                if t == 2 and w == 0:
                    dve.wait_ge(patch_out[0], 32)
                dve.scalar_tensor_tensor(store[:, t % 2, w, :], bank[4 + s % 2][:, 0:D], 1.0 / SCALE, pos_b[:, t, w, :],
                                         ALU.mult, ALU.add).then_inc(tk_row, 1)

            for f in range(8):
                low(f)
            dve.wait_ge(qkv_hi, 1)
            dve.scalar_tensor_tensor(qkv_l[:, :, :], qkv_raw, SCALE, qkv_h[:, :, :], ALU.mult, ALU.subtract)
            dve.scalar_tensor_tensor(wo_l[:, :, :], wo_raw, SCALE, wo_h[:, :, :], ALU.mult, ALU.subtract)
            dve.scalar_tensor_tensor(bq_hl[32:33, :], bq_raw[32:33, :], SCALE, bq_hl[32:33, :],
                                     ALU.mult, ALU.subtract).then_inc(qkv_lo, 1)
            for s in range(NX):
                if s + 2 < NX:
                    low(2 * (s + 2) + 4)
                    low(2 * (s + 2) + 5)
                row(s)

            PP = 2

            def project(c, base):
                own.step(base)
                dve.wait_ge(h_in, c * 16 + 16)
                for t in range(G):
                    last = dve.bn_stats(stats[:, t, :], tile(h_all, c * G + t))
                own(last)
                apart(dve)
                for t in range(G):
                    last = dve.bn_aggr(mv[:, t, :], stats[:, t, :])
                own(last)
                dve.tensor_scalar(veps[:, :], mv[:, :, 1], EPS, None, ALU.add).then_inc(a_var, 1)
                dve.wait_ge(a_rstd, c + 1)

                def normal(t):
                    i = c * G + t
                    after(dve, a_turned, before(i, t))
                    dve.tensor_scalar(xn[:, t % 2, :], tile(h_all, i), mv[:, t, 0:1], rstd[:, t:t + 1],
                                      ALU.subtract, ALU.mult).then_inc(a_xn, 1)

                normal(0)
                for t in range(G):
                    i = c * G + t
                    s = t % 2
                    if t + 1 < G:
                        normal(t + 1)
                    dve.wait_ge(a_hi, i + 1)
                    after(dve, a_kv, before(i, t))
                    dve.tensor_tensor(xl[:, s, :], bank[s][:, 0:D], xh[:, s, :], ALU.subtract).then_inc(a_lo, 1)
                    if t > 0:
                        product(c, t - 1)
                product(c, G - 1)
                dve.wait_ge(a_nq, c * G + G)
                dve.tensor_copy(nq[:, c * G:c * G + G] if isinstance(c, int) else nq[:, bass.ds(c * G, G)],
                                bank[7][:, 0:G]).then_inc(a_nqc, 1)

            def product(c, t):
                i = c * G + t
                s = t % 2
                dve.wait_ge(a_rk, i + 1)
                after(dve, a_acc, before(i, t))
                dve.scalar_tensor_tensor(kvp[:, s, :], bank[4 + s][:, 0:D], rk[:, t:t + 1], vs[:, s, :],
                                         ALU.mult, ALU.mult).then_inc(a_kvp, 1)

            n0 = own.n
            project(0, n0)
            with dve.Fori(1, NG) as c:
                project(c, c * PP + n0)
            assert own.n == PP
            n1 = n0 + NG * PP
            dve.wait_ge(kv_hi, 1)
            dve.tensor_tensor(kv_hl[B:2 * B, :], bank[7][B:2 * B, 0:D], kv_hl[B:2 * B, :], ALU.subtract).then_inc(kv_ready, 1)
            dve.wait_ge(rq_ready, 1)

            def attend(c, base):
                own.step(base)
                for t in range(G + 1):
                    if t < G:
                        i = c * G + t
                        dve.wait_ge(b_kvb, i + 1)
                        after(dve, b_qlo, before(i, t))
                        dve.tensor_tensor(sq[:, t % 2, :], bank[t % 2][:, 0:D], tile(q_all, i), ALU.mult).then_inc(b_qk, 1)
                    if t > 0:
                        i = c * G + t - 1
                        if t == 1:
                            dve.wait_ge(b_hb, c + 1)
                        dve.wait_ge(b_prod, i + 1)
                        own(dve.scalar_tensor_tensor(tile(h_all, i), bank[2 + (t - 1) % 2][:, 0:D],
                                                     rq[:, i:i + 1] if isinstance(i, int) else rq[:, bass.ds(i, 1)],
                                                     tile(h_all, i), ALU.mult, ALU.add))
                        apart(dve)
                        last = dve.bn_stats(stats[:, t - 1, :], tile(h_all, i))
                        last.then_inc(b_h2, 1)
                dve.wait_ge(b_h2, c * G + G)
                apart(dve)
                for t in range(G):
                    last = dve.bn_aggr(mv[:, t, :], stats[:, t, :])
                own(last)
                dve.tensor_scalar(veps[:, :], mv[:, :, 1], EPS, None, ALU.add).then_inc(b_var, 1)
                if not (isinstance(c, int) and c == 0):
                    gate(c - 1, False)
                dve.wait_ge(b_rstd, c + 1)
                after(dve, rows_out, c * 16)
                for t in range(G):
                    i = c * G + t
                    dve.tensor_scalar(x2[:, t, :], tile(h_all, i), mv[:, t, 0:1], rstd[:, t:t + 1],
                                      ALU.subtract, ALU.mult).then_inc(b_xn, 1)

            def top(src, at):
                own(dve.tensor_reduce(m12[:, :, at:at + 1], src, AX, ALU.max))
                own(dve.tensor_tensor(same[:, :, :], src, m12[:, :, at:at + 1].to_broadcast([P, G, E]), ALU.is_equal))
                own(dve.tensor_tensor(same[:, :, :], same[:, :, :], rev[:, :].unsqueeze(1).to_broadcast([P, G, E]), ALU.mult))
                own(dve.tensor_reduce(er[:, :, at:at + 1], same[:, :, :], AX, ALU.max))
                own(dve.tensor_tensor(pick[:, :, at * E:(at + 1) * E], same[:, :, :],
                                      er[:, :, at:at + 1].to_broadcast([P, G, E]), ALU.is_equal))

            def gate(c, last_group):
                dve.wait_ge(b_lg, c + 1)
                after(dve, b_rank, c)
                top(lg[:, :, :], 0)
                own(dve.scalar_tensor_tensor(lg2[:, :, :], pick[:, :, 0:E], -BIG, lg[:, :, :], ALU.mult, ALU.add))
                top(lg2[:, :, :], 1)
                if last_group:
                    own(dve.memset(pick[LAST:P, G - 1, :], 0.0))
                own(dve.tensor_copy(cum[:, 0, :], cum[:, G, :]))
                for t in range(G):
                    add = dve.tensor_tensor(cum[:, t + 1, :], cum[:, t, :], pick[:, t, :], ALU.add)
                    if t + 1 < G:
                        own(add)
                add.then_inc(b_pick, 1)
                dve.tensor_tensor(ex[:, :, 0:E], lg[:, :, :], m12[:, :, 0:1].to_broadcast([P, G, E]), ALU.subtract)
                dve.tensor_tensor(ex[:, :, E:E + 1], m12[:, :, 1:2], m12[:, :, 0:1], ALU.subtract).then_inc(b_ex_in, 1)
                dve.wait_ge(b_rank, c + 1)
                own(dve.tensor_tensor(pm[:, :, :], bank[6][:, 64:64 + G * TOP * E].rearrange("p (t k) -> p t k", t=G),
                                      pick[:, :, :], ALU.mult))
                own(dve.tensor_reduce(posn[:, :, :], pm[:, :, :].rearrange("p t (k e) -> p t k e", k=TOP), AX, ALU.add))
                own(dve.tensor_scalar(posn[:, :, 1:2], posn[:, :, 1:2], -1.0, CAP - 1.0, ALU.mult, ALU.add))
                dve.tensor_scalar(hi_i[:, :, :], posn[:, :, :], -(P - 1) / 2, 1.0 / P, ALU.add, ALU.mult)
                own(dve.tensor_scalar(bad[:, :, :], posn[:, :, :], CAP - 0.5, None, ALU.is_gt))
                own(dve.scalar_tensor_tensor(bad[:, :, :], posn[:, :, :], -0.5, bad[:, :, :], ALU.is_lt, ALU.add))
                own(dve.scalar_tensor_tensor(key[:, :, :], er[:, :, :], -float(NS), hi_i[:, :, :], ALU.mult, ALU.add))
                own(dve.scalar_tensor_tensor(key[:, :, :], bad[:, :, :], NOWHERE, key[:, :, :], ALU.mult, ALU.add))
                if last_group:
                    own(dve.memset(key[LAST:P, G - 1, :], NOWHERE))
                own(dve.scalar_tensor_tensor(lo_f[:, :, :], hi_i[:, :, :], -float(P), posn[:, :, :], ALU.mult, ALU.add))
                after(dve, b_inv, c)
                for t in range(G):
                    for k in range(TOP):
                        n = t * TOP + k
                        dve.tensor_scalar(hot_lo[:, n, :], lane[:, :], lo_f[:, t, k:k + 1], None, ALU.is_equal)
                        i = c * G + t
                        last = dve.tensor_scalar(hot_key[:, n, :], keys[:, :], key[:, t, k:k + 1],
                                                 token[:, i:i + 1] if isinstance(i, int) else token[:, bass.ds(i, 1)],
                                                 ALU.is_equal, ALU.mult)
                last.then_inc(b_hot, 1)
                dve.wait_ge(b_ex, c + 1)
                own(dve.tensor_reduce(ssum[:, :], ex[:, :, 0:E], AX, ALU.add))
                own(dve.reciprocal(gp[:, :, 0], ssum[:, :]))
                own(dve.tensor_tensor(gp[:, :, 1], gp[:, :, 0], ex[:, :, E], ALU.mult))
                own(dve.tensor_tensor(gt[:, :], gp[:, :, 0], gp[:, :, 1], ALU.add))
                own(dve.tensor_scalar(gt[:, :], gt[:, :], GATE_EPS, None, ALU.max))
                own(dve.reciprocal(gt[:, :], gt[:, :]))
                after(dve, w_out, c * 16)
                dve.tensor_tensor(w_cols[:, :, :], gp[:, :, :], gt[:, :].unsqueeze(2).to_broadcast([P, G, TOP]), ALU.mult).then_inc(b_w, 1)

            attend(0, n1)
            A0, n2 = own.n, n1 + own.n
            AG = G + 1 + 30
            attend(1, n2)
            with dve.Fori(2, NG) as c:
                attend(c, (c - 1) * AG + n2)
            assert own.n == AG, own.n
            n3 = n2 + (NG - 1) * AG
            own.step(n3)

            def split_w1(e, s):
                dve.wait_ge(w1_hi, e + 1)
                dve.scalar_tensor_tensor(w1l[s], w1_raw, SCALE, w1h[s], ALU.mult, ALU.subtract).then_inc(w1_lo, 1)

            def split_w2(e, s):
                dve.wait_ge(w2_hi, e + 1)
                dve.scalar_tensor_tensor(w2l[s], w2_raw, SCALE, w2h[s], ALU.mult, ALU.subtract).then_inc(w2_lo, 1)

            gate(NG - 1, True)

            dve.wait_ge(counted, 1)
            own(dve.tensor_copy(cnt[:, :], bank[6][:, 0:TOP * E]))

            def count(k):
                return cnt[:, k * E:(k + 1) * E].unsqueeze(2).to_broadcast([P, E, NS])

            def ej(v):
                return v[:, :].rearrange("p (e j) -> p e j", e=E)

            own(dve.tensor_tensor(ej(t0), ej(slot), count(0), ALU.is_lt))
            own(dve.scalar_tensor_tensor(t0[:, :], slot[:, :], CAP - 0.5, t0[:, :], ALU.is_lt, ALU.mult))
            own(dve.tensor_scalar(tmp[:, :], slot[:, :], -1.0, CAP - 1.0, ALU.mult, ALU.add))
            own(dve.tensor_tensor(ej(t1), ej(tmp), count(1), ALU.is_lt))
            own(dve.scalar_tensor_tensor(t1[:, :], tmp[:, :], -0.5, t1[:, :], ALU.is_gt, ALU.mult))
            own(dve.tensor_tensor(tmp[:, :], t0[:, :], t1[:, :], ALU.mult))
            own(dve.tensor_tensor(t1[:, :], t1[:, :], tmp[:, :], ALU.subtract))
            own(dve.tensor_tensor(ids[:, :], bank[7][:, 0:KEY], t0[:, :], ALU.mult))
            own(dve.tensor_tensor(tmp[:, :], bank[7][:, KEY:2 * KEY], t1[:, :], ALU.mult))
            own(dve.tensor_tensor(ids[:, :], ids[:, :], tmp[:, :], ALU.add))
            own(dve.tensor_copy(from_i[:, :], ids[:, :]))
            own(dve.tensor_tensor(tmp[:, :], t0[:, :], t1[:, :], ALU.add))
            own(dve.tensor_scalar(tmp[:, :], tmp[:, :], -1.0, 1.0, ALU.mult, ALU.add))
            own(dve.scalar_tensor_tensor(ids[:, :], tmp[:, :], trash[:, 0:1], ids[:, :], ALU.mult, ALU.add))
            dve.tensor_copy(to_i[:, :], ids[:, :]).then_inc(tables, 1)
            split_w1(0, 0)
            split_w2(0, 0)
            n4 = own.base + own.n

            def split_rows(e, s, g, js):
                u, v = e * CH + g, (s + g) % 2
                for j in js:
                    m = min(P, CAP - (g * ST + j) * P)
                    dve.wait_ge(e_xhi, u * ST + j + 1)
                    if j == 0:
                        after(dve, e_up, (u - 1) * NM)
                    dve.tensor_tensor(xt_l[:, v, :, j * P:j * P + m],
                                      bank[(s + g * ST + j) % 2][:, 0:D].rearrange("p (k n) -> p k n", k=ND)[:, :, 0:m],
                                      xt_h[:, v, :, j * P:j * P + m], ALU.subtract).then_inc(e_xlo, 1)

            def expert(e, s, last, base):
                own.step(base)
                for g in range(CH):
                    w = min(ST * P, CAP - g * ST * P)
                    u = e * CH + g
                    v = (s + g) % 2
                    nxt = (e, s, g + 1) if g + 1 < CH else None if last else (e + 1, 1 - s, 0)
                    if g == 0:
                        def cols(tab):
                            return tab[:, e * NS:(e + 1) * NS] if isinstance(e, int) else tab[:, bass.ds(e * NS, NS)]
                        for gg in range(CH):
                            dve.wait_ge(got[s][gg], gathered(e, s))
                        own(dve.tensor_tensor(ws[:, s, :], rows[s][:, :, D], cols(t0), ALU.mult))
                        own(dve.tensor_tensor(wtmp[:, s, :], rows[s][:, :, D + 1], cols(t1), ALU.mult))
                        own(dve.tensor_tensor(ws[:, s, :], ws[:, s, :], wtmp[:, s, :], ALU.add))
                        own(dve.tensor_scalar(wtmp[:, s, :], ws[:, s, :], 1.0 / SCALE, None, ALU.mult))
                        dve.wait_ge(b2_in, e * 16 + 16)
                    for m in range(NM):
                        k = u * NM + m
                        dve.wait_ge(e_gelu, k + 1)
                        if m == 0:
                            after(dve, e_down, (u - 1) * ST)
                        dve.tensor_copy(hid_h[v][:, m, 0:w], hf[:, m % 2, 0:w]).then_inc(e_hhi, 1)
                        dve.wait_ge(e_hhi, k + 1)
                        dve.tensor_tensor(hid_l[v][:, m, 0:w], hf[:, m % 2, 0:w], hid_h[v][:, m, 0:w],
                                          ALU.subtract).then_inc(e_hlo, 1)
                    if g == 0 and not last:
                        split_w1(e + 1, 1 - s)
                    if g == 1 and not last:
                        split_w2(e + 1, 1 - s)
                    if nxt:
                        split_rows(*nxt, (0, 1))
                    for j in range(ST):
                        jj = g * ST + j
                        m = min(P, w - j * P)
                        k = u * ST + j
                        own(dve.tensor_scalar(b2w[0:m, jj % 2, :], b2_b[0:m, s, :], ws[0:m, s, jj:jj + 1], None, ALU.mult))
                        dve.wait_ge(e_down, k + 1)
                        after(dve, added, (k - 2) * 16)
                        dve.scalar_tensor_tensor(y_sb[0:m, jj % 3, :], bank[5 + (s + jj) % 2][0:m, 0:D],
                                                 wtmp[0:m, s, jj:jj + 1], b2w[0:m, jj % 2, :],
                                                 ALU.mult, ALU.add).then_inc(e_y, 1)
                        if j == 0 and nxt:
                            split_rows(*nxt, (2,))

            EO = 4 + NS
            split_rows(0, 0, 0, range(ST))
            expert(0, 0, False, n4)
            assert own.n == EO
            with dve.Fori(0, (E - 2) // 2) as k:
                expert(k * 2 + 1, 1, False, k * 2 * EO + (n4 + EO))
                expert(k * 2 + 2, 0, False, k * 2 * EO + (n4 + 2 * EO))
            expert(E - 1, 1, True, n4 + (E - 1) * EO)

        @block.tensor
        def _(pe):
            def three(dst, lh, ll, rh, rl, start, stop):
                pe.matmul(dst, lh, rh, start=start, stop=False)
                pe.matmul(dst, lh, rl, start=False, stop=False)
                return pe.matmul(dst, ll, rh, start=False, stop=stop)

            def add_zeros(dst, n, start):
                return pe.matmul(dst, zero_h[:, 0:P], zero_h[:, 0:n], start=start, stop=not start, skip_group_check=True)

            pe.wait_ge(consts, 2)
            pe.wait_ge(raw_in, 16)

            def turn(f):
                step, part = f // 2, f % 2
                if f >= 4:
                    pe.wait_ge(tk_lo, f - 3)
                for k in range(3):
                    kt = 3 * part + k
                    if step < 2:
                        src = tokw_raw[:, step, kt * P:(kt + 1) * P]
                    else:
                        s = step - 2
                        if k == 0:
                            pe.wait_ge(tk_patch, s + 1)
                        src = patch[:, s % 2, kt * P:(kt + 1) * P]
                    last = pe.transpose(bank[f % 4][:, k * P:(k + 1) * P], src, ident[:, :])
                last.then_inc(tk_turned, 1)

            for f in range(4):
                turn(f)
            turn(4)
            turn(5)
            pe.wait_ge(tk_lo, 4)
            for s in range(NX):
                if s + 1 < NX:
                    turn(2 * (s + 1) + 4)
                    turn(2 * (s + 1) + 5)
                pe.wait_ge(tk_lo, 2 * s + 6)
                if s >= 2:
                    pe.wait_ge(tk_row, s - 1)
                for kt in range(NKT):
                    cut = slice(kt * P, (kt + 1) * P)
                    last = three(bank[4 + s % 2][:, 0:D], pat_h[:, s % 2, cut], pat_l[:, s % 2, cut],
                                 tokw_h[:, kt, :], tokw_l[:, kt, :], kt == 0, kt == NKT - 1)
                last.then_inc(tk_prod, 1)
            pe.wait_ge(raw2_in, 16 * 7)
            pe.transpose(bank[0][:, 0:E * NM], b1_raw, ident[0:E * NM, 0:E * NM]).then_inc(b1_turned, 1)
            pe.wait_ge(b1_ok, 1)
            pe.wait_ge(tk_row, NX)
            pe.wait_ge(qkv_lo, 2)
            pe.wait_ge(consts, 3)

            def turn_x(c, t):
                i = c * G + t
                pe.wait_ge(a_xn, i + 1)
                after(pe, a_lo, before(i, t))
                for k in range(ND):
                    last = pe.transpose(bank[t % 2][:, k * P:(k + 1) * P], xn[:, t % 2, k * P:(k + 1) * P], ident[:, :])
                last.then_inc(a_turned, 1)

            def sums(c, t):
                i = c * G + t
                s = t % 2
                pe.wait_ge(a_qsq, i + 1)
                if t == 0:
                    after(pe, a_nqc, c)
                for k in range(ND):
                    last = pe.matmul(bank[7][:, t:t + 1], sq[:, s, k * P:(k + 1) * P], ones_f[:, :], start=k == 0, stop=k == ND - 1)
                last.then_inc(a_nq, 1)
                pe.wait_ge(a_kvp, i + 1)
                final = isinstance(i, int) and i == NT - 1
                for k in range(ND):
                    rhs = ind[:, i + 1, :] if isinstance(i, int) else ind[:, bass.ds(i + 1, 1), :].rearrange("p a b -> p (a b)")
                    last = pe.matmul(bank[6][:, k * B:(k + 1) * B], kvp[:, s, k * P:(k + 1) * P], rhs,
                                     start=False, stop=False, skip_group_check=True)
                if final:
                    last = add_zeros(bank[6][:, 0:ND * B], ND * B, False)
                last.then_inc(a_acc, 1)

            def project(c):
                turn_x(c, 0)
                for t in range(G):
                    i = c * G + t
                    s = t % 2
                    if t + 1 < G:
                        turn_x(c, t + 1)
                    pe.wait_ge(a_lo, i + 1)
                    after(pe, a_qsq, before(i, t))
                    for dh in range(ND):
                        dst = bank[2 + s][:, dh * P:(dh + 1) * P]
                        pe.matmul(dst, bq_hl[:, dh * P:(dh + 1) * P], ones_h[:, :], start=True, stop=False)
                        for k in range(ND):
                            cut = slice(k * P, (k + 1) * P)
                            last = three(dst, qkv_h[:, k, dh * P:(dh + 1) * P], qkv_l[:, k, dh * P:(dh + 1) * P],
                                         xh[:, s, cut], xl[:, s, cut], False, k == ND - 1)
                    last.then_inc(a_q, 1)
                    after(pe, a_kvp, before(i, t))
                    dst = bank[4 + s][:, 0:2 * D]
                    pe.matmul(dst, ones_h[:, :], bq_hl[:, D:3 * D], start=True, stop=False)
                    for k in range(ND):
                        cut = slice(k * P, (k + 1) * P)
                        last = three(dst, xh[:, s, cut], xl[:, s, cut], qkv_h[:, k, D:3 * D], qkv_l[:, k, D:3 * D],
                                     False, k == ND - 1)
                    last.then_inc(a_kv, 1)
                    if t > 0:
                        sums(c, t - 1)
                sums(c, G - 1)

            add_zeros(bank[6][:, 0:ND * B], ND * B, True)
            project(0)
            with pe.Fori(1, NG - 1) as c:
                project(c)
            project(NG - 1)
            pe.wait_ge(kv_copied, 1)
            pe.wait_ge(a_nqc, NG)
            for k in range(ND):
                last = pe.transpose(bank[7][:, k * P:(k + 1) * P], kvt[:, k, :], ident[:, :])
            last.then_inc(kv_turned, 1)
            pe.wait_ge(kv_ready, 1)

            def spread(c, t):
                i = c * G + t
                after(pe, b_qk, before(i, t))
                rhs = ind_t[:, i * P:(i + 1) * P] if isinstance(i, int) else ind_t[:, bass.ds(i * P, P)]
                for k in range(ND):
                    last = pe.matmul(bank[t % 2][:, k * P:(k + 1) * P], kv_hl[:, k * P:(k + 1) * P], rhs,
                                     start=True, stop=True)
                last.then_inc(b_kvb, 1)

            def ranks(c):
                pe.wait_ge(b_pick, c + 1)
                dst = bank[6][:, 64:64 + G * TOP * E]
                pe.matmul(dst, upper[:, :], pick[:, :, :].rearrange("p t k -> p (t k)"), start=True, stop=False)
                pe.matmul(dst, ones_b[:, :], cum[:, 0:G, :].rearrange("p t k -> p (t k)"),
                          start=False, stop=True).then_inc(b_rank, 1)

            def invert(c, final):
                pe.wait_ge(b_hot, c + 1)
                for n in range(G * TOP):
                    k = n % TOP
                    last = pe.matmul(bank[7][:, k * KEY:(k + 1) * KEY], hot_lo[:, n, :], hot_key[:, n, :],
                                     start=False, stop=False, skip_group_check=True)
                if final:
                    last = add_zeros(bank[7][:, 0:TOP * KEY], TOP * KEY, False)
                last.then_inc(b_inv, 1)

            def attend(c):
                spread(c, 0)
                for t in range(G):
                    i = c * G + t
                    s = t % 2
                    if t + 1 < G:
                        spread(c, t + 1)
                    pe.wait_ge(b_qlo, i + 1)
                    after(pe, b_h2, before(i, t))
                    for k in range(ND):
                        cut = slice(k * P, (k + 1) * P)
                        last = three(bank[2 + s][:, 0:D], xh[:, s, cut], xl[:, s, cut], wo_h[:, k, :], wo_l[:, k, :],
                                     k == 0, k == ND - 1)
                    last.then_inc(b_prod, 1)
                if not (isinstance(c, int) and c == 0):
                    ranks(c - 1)
                    invert(c - 1, False)
                for t in range(G + 1):
                    if t < G:
                        i = c * G + t
                        s = t % 2
                        pe.wait_ge(b_xn, i + 1)
                        after(pe, b_xt, before(i, t))
                        for k in range(ND):
                            last = pe.transpose(bank[4 + s][:, k * P:(k + 1) * P], x2[:, t, k * P:(k + 1) * P], ident[:, :])
                        last.then_inc(b_turned, 1)
                    if t > 0:
                        i = c * G + t - 1
                        pe.wait_ge(b_xt, i + 1)
                        if t == 1:
                            after(pe, b_lg, c)
                        for k in range(ND):
                            last = pe.matmul(bank[6][:, (t - 1) * E:t * E], xn[:, (t - 1) % 2, k * P:(k + 1) * P],
                                             wg_sb[:, k, :], start=k == 0, stop=k == ND - 1)
                        last.then_inc(b_logit, 1)

            add_zeros(bank[7][:, 0:TOP * KEY], TOP * KEY, True)
            attend(0)
            with pe.Fori(1, NG) as c:
                attend(c)
            ranks(NG - 1)
            invert(NG - 1, True)
            pe.matmul(bank[6][:, 0:TOP * E], ones_b[:, :], cum[:, G, :], start=True, stop=True).then_inc(counted, 1)

            pe.wait_ge(tables, 1)
            up = [2, 3, 4, 7]

            def turn_rows(e, s, g, js):
                for j in js:
                    m = min(P, CAP - (g * ST + j) * P)
                    k = (e * CH + g) * ST + j
                    if j == 0:
                        pe.wait_ge(got[s][g], gathered(e, s))
                    after(pe, e_xlo, k - 1)
                    for kk in range(ND):
                        last = pe.transpose(bank[(s + g * ST + j) % 2][:, kk * P:kk * P + m],
                                            rows[s][0:m, g * ST + j, kk * P:(kk + 1) * P], ident[0:m, 0:m])
                    last.then_inc(e_turned, 1)

            def expert(e, s, last_one):
                for g in range(CH):
                    w = min(ST * P, CAP - g * ST * P)
                    u = e * CH + g
                    v = (s + g) % 2
                    if g == 0:
                        pe.wait_ge(w1_lo, e + 1)
                    pe.wait_ge(e_xlo, u * ST + ST)
                    for m in range(NM):
                        after(pe, e_gelu, u * NM + m - 3)
                        for k in range(ND):
                            cut = slice(m * P, (m + 1) * P)
                            last = three(bank[up[m % 4]][:, 0:w], w1h[s][:, k, cut], w1l[s][:, k, cut],
                                         xt_h[:, v, k, 0:w], xt_l[:, v, k, 0:w], k == 0, k == ND - 1)
                        last.then_inc(e_up, 1)
                    nxt = (e, s, g + 1) if g + 1 < CH else None if last_one else (e + 1, 1 - s, 0)
                    if nxt:
                        turn_rows(*nxt, (0, 1))
                    if g == 0:
                        pe.wait_ge(w2_lo, e + 1)
                    for j in range(ST):
                        mj = min(P, w - j * P)
                        kj = u * ST + j
                        after(pe, e_y, kj - 1)
                        dst = bank[5 + (s + g * ST + j) % 2][0:mj, 0:D]
                        for m in range(NM):
                            if j == 0:
                                pe.wait_ge(e_hlo, u * NM + m + 1)
                            cut = slice(j * P, j * P + mj)
                            last = three(dst, hid_h[v][:, m, cut], hid_l[v][:, m, cut], w2h[s][:, m, :], w2l[s][:, m, :],
                                         m == 0, m == NM - 1)
                        last.then_inc(e_down, 1)
                        if j == 0 and nxt:
                            turn_rows(*nxt, (2,))

            turn_rows(0, 0, 0, range(ST))
            expert(0, 0, False)
            with pe.Fori(0, (E - 2) // 2) as k:
                expert(k * 2 + 1, 1, False)
                expert(k * 2 + 2, 0, False)
            expert(E - 1, 1, True)


_INS = ["x", "txt", "L0_tok_W", "L0_tok_b", "L0_tok_cls_token", "L0_tok_pos_embedding", "L0_attn_Wqkv", "L0_attn_bqkv",
        "L0_attn_Wout", "L0_attn_bout", "L0_ffn_wg", "L0_ffn_w1", "L0_ffn_b1", "L0_ffn_w2", "L0_ffn_b2"]


def kernel(**inputs):
    import concourse.bacc as bacc
    from concourse.bass_utils import run_bass_kernel_spmd

    nc = bacc.Bacc("TRN2", target_bir_lowering=False, num_devices=1)
    arrays, args = {}, []
    for name in _INS:
        a = np.ascontiguousarray(inputs[name])
        arrays[f"in_{name}"] = a
        args.append(nc.dram_tensor(f"in_{name}", a.shape, mybir.dt.from_np(a.dtype), kind="ExternalInput").ap())
    out = nc.dram_tensor("out_rows", (N + P, D), F32, kind="ExternalOutput").ap()
    build(nc, *args, out)
    r = run_bass_kernel_spmd(nc, [arrays], core_ids=[0])
    return r.results[0]["out_rows"][0:N].reshape(B, SEQ, D)
```

```python
from contextlib import ExitStack

import numpy as np
import concourse.bass as bass
from concourse import mybir

F32 = mybir.dt.float32
F16 = mybir.dt.float16
BF16 = mybir.dt.bfloat16
I32 = mybir.dt.int32
U32 = mybir.dt.uint32
ALU = mybir.AluOpType
ACT = mybir.ActivationFunctionType
AX = mybir.AxisListType.X

P = 128
B, C, IMG, PATCH = 64, 3, 96, 16
HP = IMG // PATCH
NPATCH = HP * HP
D = 256
ND = D // P
KD = C * PATCH * PATCH
NKT = KD // P
TXT = 32
SEQ = 1 + NPATCH + TXT
N = B * SEQ
G = 5
NG = -(-N // (P * G))
NT = NG * G
NPAD = NT * P
LAST = N - (NT - 1) * P
E, TOP, HID = 8, 2, 1024
CAP = -(-TOP * N // E)
NS = -(-CAP // P)
CH = 3
ST = NS // CH
NM = HID // P
XW = D + TOP
EPS = 1e-5
GATE_EPS = 1e-9
SCALE = 64.0
NOWHERE = 1000.0
BIG = 3.0e38
KEY = NS * E


def after(engine, sem, value):
    if not isinstance(value, int) or value > 0:
        engine.wait_ge(sem, value)


def there(i):
    return not isinstance(i, int) or 0 <= i < NT


def apart(engine):
    engine.nop(nofuse=True)


class Own:

    def __init__(self, engine, sem):
        self.engine, self.sem, self.base, self.n = engine, sem, 0, 0

    def step(self, base):
        self.base, self.n = base, 0

    def __call__(self, instruction):
        instruction.then_inc(self.sem, 1)
        self.n += 1
        self.engine.wait_ge(self.sem, self.base + self.n)


def build(nc, x, txt, tok_w, tok_b, cls, pos, wqkv, bqkv, wout, bout, wg, w1, b1, w2, b2, out):
    ctx = ExitStack()
    with ctx:
        def sb(name, shape, dt=F32):
            return ctx.enter_context(nc.sbuf_tensor(name, shape, dt))

        def sem(name):
            return ctx.enter_context(nc.semaphore(name))

        h_rows = nc.dram_tensor("h_rows", (NPAD, D), F32, kind="Internal").ap()
        x_rows = nc.dram_tensor("x_rows", (NPAD, XW), F32, kind="Internal").ap()

        region_h = sb("region_h", [P, NT * D])
        region_q = sb("region_q", [P, NT * D])
        region_x = sb("region_x", [P, KD * HP * (HP // 2)])
        region_i = sb("region_i", [P, NPAD // 2 + (NT + 1) * B])

        h_all = region_h[:, :].rearrange("p (i d) -> p i d", d=D)
        q_all = region_q[:, :].rearrange("p (i d) -> p i d", d=D)
        tokw_raw = region_h[:, 0:2 * KD].rearrange("p (t k) -> p t k", t=2)
        qkv_raw = region_h[:, 2 * KD:2 * KD + ND * 3 * D].rearrange("p (k n) -> p k n", k=ND)
        wo_raw = region_h[:, 4 * KD:4 * KD + ND * D].rearrange("p (k n) -> p k n", k=ND)
        bq_raw = region_h[:, 5 * KD:5 * KD + 3 * D]
        tokb_b = region_h[:, 6 * KD:6 * KD + D]
        cls_b = region_h[0:B, 6 * KD + D:6 * KD + 2 * D]
        pos0_b = region_h[0:B, 6 * KD + 2 * D:6 * KD + 3 * D]
        zeros = region_h[0:P, 6 * KD + 3 * D:6 * KD + 4 * D]
        b1_raw = region_h[0:E * NM, 6 * KD + 4 * D:6 * KD + 4 * D + P]
        NTX = HP // 2
        pos_b = region_q[:, 0:NTX * HP * D].rearrange("p (t w d) -> p t w d", t=NTX, w=HP)
        store = region_q[:, NTX * HP * D:(NTX + 2) * HP * D].rearrange("p (s w d) -> p s w d", s=2, w=HP)
        x_sb = region_x[:, :].rearrange("p (t c i w j) -> p t c i w j", t=NTX, c=C, i=PATCH, w=HP)
        ind_t = region_i[:, 0:NPAD // 2].bitcast(F16)
        ind = region_i[:, NPAD // 2:].rearrange("p (i b) -> p i b", b=B)
        WR = ND * HID
        w1_raw = region_x[:, 0:WR].rearrange("p (k n) -> p k n", k=ND)
        w2_raw = region_x[:, WR:2 * WR].rearrange("p (k n) -> p k n", k=NM)
        halves = [region_x[:, 2 * WR + s * 2 * WR:2 * WR + (s + 1) * 2 * WR].bitcast(F16) for s in range(2)]
        w1h = [v[:, 0:WR].rearrange("p (k n) -> p k n", k=ND) for v in halves]
        w1l = [v[:, WR:2 * WR].rearrange("p (k n) -> p k n", k=ND) for v in halves]
        w2h = [v[:, 2 * WR:3 * WR].rearrange("p (k n) -> p k n", k=NM) for v in halves]
        w2l = [v[:, 3 * WR:4 * WR].rearrange("p (k n) -> p k n", k=NM) for v in halves]
        HW = NM * ST * P // 2
        hid_h = [region_q[:, (2 * s) * HW:(2 * s + 1) * HW].bitcast(F16).rearrange("p (m n) -> p m n", m=NM) for s in range(2)]
        hid_l = [region_q[:, (2 * s + 1) * HW:(2 * s + 2) * HW].bitcast(F16).rearrange("p (m n) -> p m n", m=NM) for s in range(2)]
        rows = [region_i[:, 0:NS * XW].rearrange("p (j d) -> p j d", d=XW),
                region_q[:, 4 * HW:4 * HW + NS * XW].rearrange("p (j d) -> p j d", d=XW)]

        tokw_h, tokw_l = (sb(n, [P, NKT, D], F16) for n in ("tokw_h", "tokw_l"))
        qkv_h, qkv_l = (sb(n, [P, ND, 3 * D], F16) for n in ("qkv_h", "qkv_l"))
        wo_h, wo_l = (sb(n, [P, ND, D], F16) for n in ("wo_h", "wo_l"))
        bq_hl = sb("bq_hl", [P, 3 * D], F16)
        wg_sb = sb("wg_sb", [P, ND, E])
        bout_b = sb("bout_b", [P, D])
        b1_cols = sb("b1_cols", [P, E * NM])
        ident = sb("ident", [P, P])
        upper = sb("upper", [P, P], BF16)
        ones_b = sb("ones_b", [P, P], BF16)
        ones_h = sb("ones_h", [P, P], F16)
        zero_h = sb("zero_h", [P, TOP * KEY], F16)
        ones_f = sb("ones_f", [P, 1])
        lane = sb("lane", [P, P])
        keys = sb("keys", [P, KEY])
        slot = sb("slot", [P, KEY])
        token = sb("token", [P, NT])
        trash = sb("trash", [P, 1])
        rev = sb("rev", [P, E])
        half = sb("half", [P, NT])
        minus = sb("minus", [P, 1])
        eps = sb("eps", [P, 1])
        pat = sb("pat", [P, 2 * KD])
        pat_h, pat_l = (pat[:, k * KD:(k + 1) * KD].bitcast(F16).rearrange("p (s k) -> p s k", s=2) for k in range(2))
        stats = sb("stats", [P, G, 6])
        mv = sb("mv", [P, G, 2])
        veps = sb("veps", [P, G])
        rstd = sb("rstd", [P, G])
        nmr = sb("nmr", [P, G])
        trio = sb("trio", [P, 6 * D])
        patch = trio[:, :].rearrange("p (s k) -> p s k", s=2)
        xn, sq, vs = (trio[:, 2 * k * D:2 * (k + 1) * D].rearrange("p (s d) -> p s d", s=2) for k in range(3))
        xh, xl = (sb(n, [P, 2, D], F16) for n in ("xh", "xl"))
        junk = sb("junk", [P, 2, D])
        nk = sb("nk", [P, G])
        rk = sb("rk", [P, G])
        kvp = sb("kvp", [P, 2, D])
        nq = sb("nq", [P, NT])
        rq = sb("rq", [P, NT])
        kvt = sb("kvt", [P, ND, P])
        kv_hl = sb("kv_hl", [P, D], F16)
        x2_even = sb("x2", [P, G, D])
        x2 = [x2_even[:, :, :], pat[:, 0:G * D].rearrange("p (t d) -> p t d", d=D)]
        w_cols = sb("w_cols", [P, G, TOP])
        lg = sb("lg", [P, G, E])
        lg2 = sb("lg2", [P, G, E])
        same = sb("same", [P, G, E])
        m12 = sb("m12", [P, G, 2])
        er = sb("er", [P, G, TOP])
        pick = sb("pick", [P, G, TOP * E], BF16)
        cum = sb("cum", [P, G + 1, TOP * E], BF16)
        ex = sb("ex", [P, G, E + 1])
        ssum = sb("ssum", [P, G])
        gp = sb("gp", [P, G, TOP])
        gt = sb("gt", [P, G])
        pm = sb("pm", [P, G, TOP * E])
        posn = sb("posn", [P, G, TOP])
        hi_i = sb("hi_i", [P, G, TOP], I32)
        lo_f = sb("lo_f", [P, G, TOP])
        bad = sb("bad", [P, G, TOP])
        key = sb("key", [P, G, TOP])
        hot_lo = sb("hot_lo", [P, G * TOP, P])
        hot_key = sb("hot_key", [P, G * TOP, KEY])
        cnt = sb("cnt", [P, TOP * E])
        t0 = sb("t0", [P, KEY])
        t1 = sb("t1", [P, KEY])
        ids = sb("ids", [P, KEY])
        tmp = sb("tmp", [P, KEY])
        from_i = sb("from_i", [P, KEY], U32)
        to_i = sb("to_i", [P, KEY], U32)
        from_e = sb("from_e", [P, 2, NS], U32)
        to_e = sb("to_e", [P, 2, NS], U32)
        b2_b = sb("b2_b", [P, 2, D])
        ws = sb("ws", [P, 2, NS])
        wtmp = sb("wtmp", [P, 2, NS])
        xt_h, xt_l = (v.rearrange("p s (k n) -> p s k n", k=ND) for v in (pat_h, pat_l))
        hf = hot_lo[:, 0:6, :].rearrange("p (s n) c -> p s (n c)", s=2)
        b2w = sb("b2w", [P, 2, D])
        y_sb = sb("y_sb", [P, 3, D])

        bank = [ctx.enter_context(nc.psum_tensor(f"bank{k}", [P, 512], F32)) for k in range(8)]

        (raw_in, raw2_in, consts, qkv_hi, qkv_lo, pos_in, pos_sum, row0_sum, txt_out, cls_out, pad_out,
         pool_own, dve_own, act_own) = (sem(n) for n in (
             "raw_in", "raw2_in", "consts", "qkv_hi", "qkv_lo", "pos_in", "pos_sum", "row0_sum", "txt_out", "cls_out",
             "pad_out", "pool_own", "dve_own", "act_own"))
        patch_out = [sem(f"patch_out{t}") for t in range(NTX)]
        x_in = [sem(f"x_in{t}") for t in range(NTX)]
        tk_patch, tk_turned, tk_hi, tk_lo, tk_prod, tk_row, b1_turned, b1_ok = (sem(n) for n in (
            "tk_patch", "tk_turned", "tk_hi", "tk_lo", "tk_prod", "tk_row", "b1_turned", "b1_ok"))
        (h_in, a_var, a_rstd, a_xn, a_turned, a_hi, a_lo, a_q, a_kv, a_qsq, a_v, a_rk, a_kvp, a_nq, a_acc, a_nqc) = (
            sem(n) for n in ("h_in", "a_var", "a_rstd", "a_xn", "a_turned", "a_hi", "a_lo", "a_q", "a_kv", "a_qsq",
                             "a_v", "a_rk", "a_kvp", "a_nq", "a_acc", "a_nqc"))
        kv_copied, kv_turned, kv_hi, kv_ready, rq_ready = (sem(n) for n in (
            "kv_copied", "kv_turned", "kv_hi", "kv_ready", "rq_ready"))
        (b_kvb, b_qk, b_qhi, b_qlo, b_prod, b_hb, b_h2, b_var, b_rstd, b_xn, b_turned, b_xt, b_logit, b_lg, b_pick,
         b_rank, b_ex_in, b_ex, b_w, b_hot, b_inv, out_in, rows_out_a) = (sem(n) for n in (
             "b_kvb", "b_qk", "b_qhi", "b_qlo", "b_prod", "b_hb", "b_h2", "b_var", "b_rstd", "b_xn", "b_turned",
             "b_xt", "b_logit", "b_lg", "b_pick", "b_rank", "b_ex_in", "b_ex", "b_w", "b_hot", "b_inv",
             "out_in", "rows_out_a"))
        w_out = sem("w_out")
        rows_out = [rows_out_a, sem("rows_out_b")]
        pad2_out = sem("pad2_out")
        counted, tables = sem("counted"), sem("tables")
        w1_in, w2_in, w1_hi, w1_lo, w2_hi, w2_lo, b2_in = (sem(n) for n in (
            "w1_in", "w2_in", "w1_hi", "w1_lo", "w2_hi", "w2_lo", "b2_in"))
        got = [[sem(f"got{s}_{g}") for g in range(CH)] for s in range(2)]
        (idx_ok, e_turned, e_xhi, e_xlo, e_up, e_gelu, e_hhi, e_hlo, e_down, e_y, added) = (sem(n) for n in (
            "idx_ok", "e_turned", "e_xhi", "e_xlo", "e_up", "e_gelu", "e_hhi", "e_hlo", "e_down", "e_y", "added"))

        def tile(region, i):
            return region[:, i, :] if isinstance(i, int) else region[:, bass.ds(i, 1), :].rearrange("p a d -> p (a d)")

        def gathered(e, s):
            return ((e - s) // 2 + 1) * ST * 16 if isinstance(e, int) else (e - s + 2) * (ST * 8)

        block = ctx.enter_context(nc.Block())
        NF = 2 * (2 + NTX * HP)
        NX = NTX * HP

        @block.sync
        def _(sp):
            sp.dma_start(tokw_raw, tok_w.rearrange("(t p) k -> p t k", p=P)).then_inc(raw_in, 16)
            for t in range(NTX):
                for hh in range(2):
                    src = x[:, :, (2 * t + hh) * PATCH:(2 * t + hh + 1) * PATCH, :].rearrange("b c i w -> b c (i w)")
                    dst = x_sb[hh * B:(hh + 1) * B, t].rearrange("p c i w j -> p c (i w j)")
                    sp.dma_start(dst, src).then_inc(x_in[t], 16)
            for k, v in ((qkv_raw, wqkv), (wo_raw, wout), (wg_sb[:, :, :], wg)):
                sp.dma_start(k, v.rearrange("(k p) n -> p k n", p=P)).then_inc(raw2_in, 16)
            h_seq = h_rows[0:N, :].rearrange("(b s) d -> b s d", s=SEQ)
            sp.dma_start(h_seq[:, 1 + NPATCH:, :], txt).then_inc(txt_out, 16)
            sp.wait_ge(row0_sum, 1)
            sp.dma_start(h_seq[:, 0, :], cls_b).then_inc(cls_out, 16)
            sp.wait_ge(consts, 1)
            sp.dma_start(h_rows[N:, :], zeros[0:NPAD - N, :]).then_inc(pad_out, 16)
            sp.dma_start(out[NPAD:, :], zeros[0:N + P - NPAD, :]).then_inc(pad2_out, 16)
            for t in range(NTX):
                sp.wait_ge(tk_row, HP * (t + 1))
                for hh in range(2):
                    first = 1 + (2 * t + hh) * HP
                    sp.dma_start(h_seq[:, first:first + HP, :], store[hh * B:(hh + 1) * B, t % 2, :, :]).then_inc(patch_out[t], 16)
            for done, n in ((txt_out, 1), (cls_out, 1), (pad_out, 1), (pad2_out, 1), *((v, 2) for v in patch_out)):
                sp.wait_ge(done, 16 * n)
            sp.wait_ge(b1_ok, 1)
            sp.wait_ge(qkv_hi, 1)
            sp.wait_ge(qkv_lo, 2)
            sp.wait_ge(pos_sum, 1)
            h_src = h_rows.rearrange("(i p) d -> p i d", p=P)
            with sp.Fori(0, NG) as c:
                sp.dma_start(h_all[:, bass.ds(c * G, G), :], h_src[:, bass.ds(c * G, G), :]).then_inc(h_in, 16)
                sp.wait_ge(h_in, c * 16 + 16)
                apart(sp)
            def one(v, e):
                return v[e] if isinstance(e, int) else v[bass.ds(e, 1)].squeeze(0)

            def w1_of(e):
                return one(w1, e).rearrange("(k p) n -> p k n", p=P)

            def w2_of(e):
                return one(w2, e).rearrange("(k p) n -> p k n", p=P)

            def b2_of(e):
                return one(b2, e)

            sp.wait_ge(tk_turned, NF)
            sp.dma_start(w1_raw, w1_of(0)).then_inc(w1_in, 16)
            sp.dma_start(w2_raw, w2_of(0)).then_inc(w2_in, 16)
            sp.dma_start(b2_b[:, 0, :], b2_of(0).partition_broadcast(P)).then_inc(b2_in, 16)
            o_dst = out[0:NPAD, :].rearrange("(i p) d -> p i d", p=P)
            x_dst = x_rows.rearrange("(i p) d -> p i d", p=P)

            def rows_of(c, half):
                sp.wait_ge(b_h2, c * G + G)
                sp.dma_start(o_dst[:, bass.ds(c * G, G), :], h_all[:, bass.ds(c * G, G), :]).then_inc(out_in, 16)
                sp.wait_ge(b_xn, c * G + G)
                sp.dma_start(x_dst[:, bass.ds(c * G, G), 0:D], x2[half]).then_inc(rows_out[half], 16)

            def weights_of(c):
                sp.wait_ge(b_w, c + 1)
                sp.dma_start(x_dst[:, bass.ds(c * G, G), D:XW], w_cols[:, :, :]).then_inc(w_out, 16)

            rows_of(0, 0)
            with sp.Fori(0, (NG - 1) // 2) as k:
                rows_of(k * 2 + 1, 1)
                weights_of(k * 2)
                rows_of(k * 2 + 2, 0)
                weights_of(k * 2 + 1)
            weights_of(NG - 1)
            def feed(e, s):
                sp.wait_ge(w1_hi, e)
                sp.wait_ge(w1_lo, e)
                sp.dma_start(w1_raw, w1_of(e)).then_inc(w1_in, 16)
                sp.wait_ge(w2_hi, e)
                sp.wait_ge(w2_lo, e)
                sp.dma_start(w2_raw, w2_of(e)).then_inc(w2_in, 16)
                after(sp, e_y, e * NS - NS)
                apart(sp)
                sp.wait_ge(b2_in, e * 16)
                apart(sp)
                sp.dma_start(b2_b[:, s, :], b2_of(e).partition_broadcast(P)).then_inc(b2_in, 16)

            feed(1, 1)
            with sp.Fori(0, (E - 2) // 2) as k:
                feed(k * 2 + 2, 0)
                feed(k * 2 + 3, 1)

        @block.gpsimd
        def _(pool):
            own = Own(pool, pool_own)
            pool.memset(zeros, 0.0).then_inc(consts, 1)
            own(pool.memset(ident[:, :], 0.0))
            own(pool.affine_select(out=ident[:, :], in_=ident[:, :], compare_op=ALU.not_equal, fill=1.0,
                                   base=0, pattern=[[-1, P]], channel_multiplier=1))
            pool.memset(ones_h[:, :], 1.0)
            pool.memset(zero_h[:, :], 0.0)
            pool.memset(ones_f[:, :], 1.0)
            pool.memset(half[:, :], -0.5)
            pool.memset(minus[:, :], -1.0)
            pool.memset(eps[:, :], EPS)
            own(pool.memset(ones_b[:, :], 1.0))
            own(pool.affine_select(out=upper[:, :], in_=ones_b[:, :], compare_op=ALU.is_gt, fill=0.0,
                                   base=0, pattern=[[1, P]], channel_multiplier=-1))
            pool.iota(lane[:, :], [[1, P]], base=0, channel_multiplier=0, allow_small_or_imprecise_dtypes=True)
            pool.iota(keys[:, :], [[1, KEY]], base=-KEY, channel_multiplier=0, allow_small_or_imprecise_dtypes=True)
            pool.iota(slot[:, :].rearrange("p (e j) -> p e j", e=E), [[0, E], [P, NS]], base=0, channel_multiplier=1,
                      allow_small_or_imprecise_dtypes=True)
            pool.iota(token[:, :], [[P, NT]], base=0, channel_multiplier=1, allow_small_or_imprecise_dtypes=True)
            pool.iota(trash[:, :], [[1, 1]], base=N, channel_multiplier=1, allow_small_or_imprecise_dtypes=True)
            pool.iota(rev[:, :], [[-1, E]], base=E, channel_multiplier=0,
                      allow_small_or_imprecise_dtypes=True)
            pool.memset(cum[:, :, :], 0.0).then_inc(consts, 1)
            pool.wait_ge(pos_in, 16 * 5)
            for t in range(NTX):
                last = pool.tensor_tensor(pos_b[:, t], pos_b[:, t], tokb_b.unsqueeze(1).to_broadcast([P, HP, D]), ALU.add)
            last.then_inc(pos_sum, 1)
            pool.tensor_tensor(cls_b, cls_b, pos0_b, ALU.add).then_inc(row0_sum, 1)
            pool.memset(ind, 1.0)
            own(pool.memset(ind_t, 1.0))
            own(pool.affine_select(out=ind, in_=ind, compare_op=ALU.is_ge, fill=0.0, base=-P,
                                   pattern=[[P, NT + 1], [-SEQ, B]], channel_multiplier=1))
            own(pool.affine_select(out=ind, in_=ind, compare_op=ALU.is_ge, fill=0.0, base=P + SEQ - 1,
                                   pattern=[[-P, NT + 1], [SEQ, B]], channel_multiplier=-1))
            for s in range(2):
                part = ind_t[s * B:(s + 1) * B, :]
                own(pool.affine_select(out=part, in_=part, compare_op=ALU.is_ge, fill=0.0, base=0,
                                       pattern=[[1, NPAD]], channel_multiplier=-SEQ))
                own(pool.affine_select(out=part, in_=part, compare_op=ALU.is_ge, fill=0.0, base=SEQ - 1,
                                       pattern=[[-1, NPAD]], channel_multiplier=SEQ))
            pool.nop().then_inc(consts, 1)

            def group_scale(c):
                pool.wait_ge(a_var, c + 1)
                pool.tensor_tensor(rstd[:, :], veps[:, :], half[:, 0:G], ALU.pow).then_inc(a_rstd, 1)

            def project(c, more):
                for t in range(G):
                    pool.wait_ge(a_v, c * G + t + 1)
                    pool.tensor_tensor(rk[:, t:t + 1], nk[:, t:t + 1], half[:, 0:1], ALU.pow).then_inc(a_rk, 1)
                    if t == 2 and more:
                        group_scale(c + 1)
                    pool.wait_ge(a_xn, c * G + t + 1)
                    apart(pool)
                    pool.tensor_tensor(tile(h_all, c * G + t), tile(h_all, c * G + t), bout_b[:, :], ALU.add).then_inc(b_hb, 1)

            n0 = own.n
            group_scale(0)
            with pool.Fori(0, NG - 1) as c:
                project(c, True)
            project(NG - 1, False)
            pool.wait_ge(a_nqc, 1)
            own(pool.tensor_tensor(rq[:, :], nq[:, :], half[:, :], ALU.pow))
            pool.tensor_scalar(rq[:, :], rq[:, :], 1.0 / SCALE, None, ALU.mult).then_inc(rq_ready, 1)

            def low_qk(i, s):
                pool.wait_ge(b_qhi, i + 1)
                after(pool, b_prod, i - 1)
                pool.tensor_tensor(xl[:, s, :], sq[:, s, :], xh[:, s, :], ALU.subtract).then_inc(b_qlo, 1)

            def attend(c, half_0, base):
                own.step(base)
                for t in range(G):
                    i = c * G + t
                    if there(i + 1):
                        low_qk(i + 1, (half_0 + t + 1) % 2)
                    pool.wait_ge(b_var, i + 1)
                    pool.tensor_tensor(nmr[:, t:t + 1], mv[:, t, 0:1], minus[:, :], ALU.mult)
                    own(pool.tensor_tensor(veps[:, t:t + 1], mv[:, t, 1:2], eps[:, :], ALU.add))
                    own(pool.tensor_tensor(rstd[:, t:t + 1], veps[:, t:t + 1], half[:, 0:1], ALU.pow))
                    pool.tensor_tensor(nmr[:, t:t + 1], nmr[:, t:t + 1], rstd[:, t:t + 1], ALU.mult).then_inc(b_rstd, 1)

            PA = 2 * G
            n1 = own.n
            low_qk(0, 0)
            attend(0, 0, n1)
            with pool.Fori(0, (NG - 3) // 2) as k:
                attend(k * 2 + 1, 1, k * 2 * PA + (n1 + PA))
                attend(k * 2 + 2, 0, k * 2 * PA + (n1 + 2 * PA))
            attend(NG - 2, 1, n1 + (NG - 2) * PA)
            attend(NG - 1, 0, n1 + (NG - 1) * PA)
            n1 += NG * PA

            def pull(e, s):
                apart(pool)
                for j in range(NS):
                    m = min(P, CAP - j * P)
                    pool.indirect_dma_start(out=rows[s][0:m, j, :], out_offset=None, in_=x_rows,
                                            in_offset=bass.IndirectOffsetOnAxis(ap=from_e[0:m, s, j:j + 1], axis=0)
                                            ).then_inc(got[s][j // ST], 16)

            pool.wait_ge(tables, 1)
            pool.tensor_copy(from_e[:, 0, :], from_i[:, 0:NS])
            own.step(n1)
            own(pool.tensor_copy(to_e[:, 0, :], to_i[:, 0:NS]))
            pool.wait_ge(rows_out[0], 16 * (NG - NG // 2))
            pool.wait_ge(rows_out[1], 16 * (NG // 2))
            pool.wait_ge(w_out, 16 * NG)
            pull(0, 0)
            pool.wait_ge(out_in, 16 * NG)
            pool.wait_ge(pad2_out, 16)
            n2 = n1 + own.n

            def expert(e, s, last):
                if not last:
                    after(pool, e_turned, e * NS)
                    after(pool, added, e * NS * 16)
                    pool.tensor_copy(from_e[:, 1 - s, :], from_i[:, bass.ds((e + 1) * NS, NS)])
                    own(pool.tensor_copy(to_e[:, 1 - s, :], to_i[:, bass.ds((e + 1) * NS, NS)]))
                    pull(e + 1, 1 - s)
                for j in range(NS):
                    m = min(P, CAP - j * P)
                    pool.wait_ge(e_y, e * NS + j + 1)
                    after(pool, added, (e * NS + j) * 16)
                    apart(pool)
                    pool.indirect_dma_start(out=out, out_offset=bass.IndirectOffsetOnAxis(ap=to_e[0:m, s, j:j + 1], axis=0),
                                            in_=y_sb[0:m, j % 3, :], in_offset=None, compute_op=ALU.add
                                            ).then_inc(added, 16)

            own.step(n2)
            expert(0, 0, False)
            n3 = n2 + own.n
            with pool.Fori(0, (E - 2) // 2) as k:
                own.step(k * 2 + n3)
                expert(k * 2 + 1, 1, False)
                expert(k * 2 + 2, 0, False)
            expert(E - 1, 1, True)
            pool.wait_ge(added, 16 * NS * E)

        @block.scalar
        def _(act):
            p_all = pos[0, 1:, :].rearrange("(t hh w) d -> hh t w d", hh=2, w=HP)
            for hh in range(2):
                act.dma_start(pos_b[hh * B:(hh + 1) * B].rearrange("p t w d -> p t (w d)"),
                              p_all[hh].rearrange("t w d -> t (w d)").partition_broadcast(B)).then_inc(pos_in, 16)
            act.dma_start(tokb_b, tok_b.partition_broadcast(P)).then_inc(pos_in, 16)
            act.dma_start(cls_b, cls[0, 0, :].partition_broadcast(B)).then_inc(pos_in, 16)
            act.dma_start(pos0_b, pos[0, 0, :].partition_broadcast(B)).then_inc(pos_in, 16)
            act.dma_start(bout_b[:, :], bout.partition_broadcast(P)).then_inc(raw2_in, 16)
            act.dma_start(b1_raw, b1.rearrange("e (m p) -> (e m) p", p=P)).then_inc(raw2_in, 16)
            act.wait_ge(qkv_lo, 1)
            for r in (0, 32):
                act.dma_start(bq_raw[r:r + 1, :], bqkv.unsqueeze(0)).then_inc(raw2_in, 16)

            def gather_patches(s):
                if s % HP == 0:
                    act.wait_ge(x_in[s // HP], 32)
                if s >= 2:
                    act.wait_ge(tk_turned, 4 + 2 * (s - 1))
                act.activation(patch[:, s % 2, :].rearrange("p (r j) -> p r j", j=PATCH),
                               x_sb[:, s // HP, :, :, s % HP, :].rearrange("p c i j -> p (c i) j"), ACT.Copy).then_inc(tk_patch, 1)

            def high(f):
                act.wait_ge(tk_turned, f + 1)
                step, part = f // 2, f % 2
                src = bank[f % 4][:, 0:3 * P]
                if step < 2:
                    dst = tokw_h[:, 3 * part:3 * part + 3, step * P:(step + 1) * P]
                    act.activation(dst, src.rearrange("p (k n) -> p k n", k=3), ACT.Copy, scale=SCALE).then_inc(tk_hi, 1)
                else:
                    s = step - 2
                    after(act, tk_prod, s - 1)
                    act.activation(pat_h[:, s % 2, part * 3 * P:(part + 1) * 3 * P], src, ACT.Copy).then_inc(tk_hi, 1)
            gather_patches(0)
            gather_patches(1)
            for f in range(8):
                high(f)
                if f >= 5 and f % 2 == 1:
                    gather_patches(f // 2)
            act.wait_ge(raw2_in, 16 * 7)
            act.activation(qkv_h[:, :, :], qkv_raw, ACT.Copy, scale=SCALE)
            act.activation(wo_h[:, :, :], wo_raw, ACT.Copy, scale=SCALE)
            act.activation(bq_hl[:, :], bq_raw, ACT.Copy, scale=SCALE).then_inc(qkv_hi, 1)
            for f in range(8, NF):
                high(f)
                if f % 2 == 1 and f // 2 < NX:
                    gather_patches(f // 2)
            act.wait_ge(b1_turned, 1)
            act.activation(b1_cols[:, :], bank[0][:, 0:E * NM], ACT.Copy).then_inc(b1_ok, 1)

            def high_x(i, s):
                act.wait_ge(a_turned, i + 1)
                after(act, a_q, i - 1)
                act.activation(xh[:, s, :], bank[s][:, 0:D], ACT.Copy).then_inc(a_hi, 1)

            def project(c, half_0):
                for t in range(G):
                    i = c * G + t
                    s = (half_0 + t) % 2
                    if there(i + 1):
                        high_x(i + 1, 1 - s)
                    act.wait_ge(a_kv, i + 1)
                    after(act, a_kvp, i - 1)
                    act.activation(vs[:, s, :], bank[4 + s][:, D:2 * D], ACT.Copy)
                    act.activation(junk[:, s, :], bank[4 + s][:, 0:D], ACT.Square, accum_out=nk[:, t:t + 1]).then_inc(a_v, 1)
                    act.wait_ge(a_q, i + 1)
                    after(act, a_nq, i - 1)
                    apart(act)
                    act.activation(tile(q_all, i), bank[2 + s][:, 0:D], ACT.Copy)
                    act.activation(sq[:, s, :], bank[2 + s][:, 0:D], ACT.Square).then_inc(a_qsq, 1)

            high_x(0, 0)
            project(0, 0)
            with act.Fori(0, (NG - 3) // 2) as k:
                project(k * 2 + 1, 1)
                project(k * 2 + 2, 0)
            project(NG - 2, 1)
            project(NG - 1, 0)
            act.wait_ge(a_acc, NT)
            for r in range(2):
                last = act.activation(kvt[:, :, r * B:(r + 1) * B], bank[6][:, 0:ND * B].rearrange("p (k b) -> p k b", k=ND),
                                      ACT.Copy, scale=1.0 / SCALE)
            last.then_inc(kv_copied, 1)
            act.wait_ge(kv_turned, 1)
            act.activation(kv_hl[:, :], bank[7][:, 0:D], ACT.Copy).then_inc(kv_hi, 1)

            def high_qk(i, s):
                act.wait_ge(b_qk, i + 1)
                after(act, b_prod, i - 1)
                act.activation(xh[:, s, :], sq[:, s, :], ACT.Copy).then_inc(b_qhi, 1)

            def attend(c, half_0, pairs):
                for t in range(G):
                    i = c * G + t
                    s = (half_0 + t) % 2
                    if there(i + 1):
                        high_qk(i + 1, 1 - s)
                    if t == 3 and there(i - G):
                        act.wait_ge(b_logit, c * G)
                        after(act, b_w, c - 1)
                        act.activation(lg[:, :, :], bank[6][:, 0:G * E].rearrange("p (t e) -> p t e", e=E), ACT.Copy).then_inc(b_lg, 1)
                    if there(i - 1):
                        act.wait_ge(b_rstd, i)
                        if t == 1:
                            after(act, rows_out[half_0], pairs * 16)
                        apart(act)
                        u = (t - 1) % G
                        act.activation(x2[half_0 if t > 0 else 1 - half_0][:, u, :], tile(h_all, i - 1), ACT.Identity,
                                       bias=nmr[:, u:u + 1], scale=rstd[:, u:u + 1]).then_inc(b_xn, 1)
                    if there(i - 2):
                        act.wait_ge(b_turned, i - 1)
                        after(act, b_logit, i - 3)
                        act.activation(xn[:, s, :], bank[4][:, 0:D], ACT.Copy).then_inc(b_xt, 1)
                    if t == 4 and there(i - G):
                        act.wait_ge(b_ex_in, c)
                        act.activation(ex[:, :, :], ex[:, :, :], ACT.Exp).then_inc(b_ex, 1)

            high_qk(0, 0)
            attend(0, 0, 0)
            attend(1, 1, 0)
            with act.Fori(1, (NG - 1) // 2) as k:
                attend(k * 2, 0, k)
                attend(k * 2 + 1, 1, k)
            attend(NG - 1, 0, (NG - 1) // 2)
            attend(NG, 1, NG // 2)

            def split_w1(e, s):
                act.wait_ge(w1_in, e * 16 + 16)
                act.activation(w1h[s], w1_raw, ACT.Copy, scale=SCALE).then_inc(w1_hi, 1)

            def split_w2(e, s):
                act.wait_ge(w2_in, e * 16 + 16)
                act.activation(w2h[s], w2_raw, ACT.Copy, scale=SCALE).then_inc(w2_hi, 1)

            split_w1(0, 0)
            split_w2(0, 0)

            def expert(e, s, last):
                for g in range(CH):
                    w = min(ST * P, CAP - g * ST * P)
                    u = e * CH + g
                    v = (s + g) % 2
                    for j in range(ST):
                        m = min(P, w - j * P)
                        k = u * ST + j
                        act.wait_ge(e_turned, k + 1)
                        if j == 0:
                            after(act, e_up, (u - 1) * NM)
                        act.activation(xt_h[:, v, :, j * P:j * P + m],
                                       bank[(s + g * ST + j) % 2][:, 0:D].rearrange("p (k n) -> p k n", k=ND)[:, :, 0:m],
                                       ACT.Copy).then_inc(e_xhi, 1)
                    for m in range(NM):
                        k = u * NM + m
                        act.wait_ge(e_up, k + 1)
                        after(act, e_hlo, k - 1)
                        apart(act)
                        bcol = b1_cols[:, m:m + 1] if isinstance(e, int) and e == 0 else b1_cols[:, bass.ds(e * NM + m, 1)]
                        act.activation(hf[:, m % 2, 0:w], bank[2 + m % 4 if m % 4 < 3 else 7][:, 0:w], ACT.Gelu,
                                       bias=bcol, scale=1.0 / SCALE).then_inc(e_gelu, 1)
                    if g == 0 and not last:
                        split_w1(e + 1, 1 - s)
                    if g == 1 and not last:
                        after(act, e_down, e * NS)
                        split_w2(e + 1, 1 - s)

            expert(0, 0, False)
            with act.Fori(0, (E - 2) // 2) as k:
                expert(k * 2 + 1, 1, False)
                expert(k * 2 + 2, 0, False)
            expert(E - 1, 1, True)

        @block.vector
        def _(dve):
            own = Own(dve, dve_own)
            own(dve.memset(bq_raw, 0.0))
            dve.nop().then_inc(qkv_lo, 1)

            def low(f):
                act_done = f + 1
                dve.wait_ge(tk_hi, act_done)
                step, part = f // 2, f % 2
                src = bank[f % 4][:, 0:3 * P]
                if step < 2:
                    o = tokw_l[:, 3 * part:3 * part + 3, step * P:(step + 1) * P]
                    i1 = tokw_h[:, 3 * part:3 * part + 3, step * P:(step + 1) * P]
                    dve.scalar_tensor_tensor(o, src.rearrange("p (k n) -> p k n", k=3), SCALE, i1,
                                             ALU.mult, ALU.subtract).then_inc(tk_lo, 1)
                else:
                    s = step - 2
                    after(dve, tk_prod, s - 1)
                    cut = slice(part * 3 * P, (part + 1) * 3 * P)
                    dve.tensor_tensor(pat_l[:, s % 2, cut], src, pat_h[:, s % 2, cut], ALU.subtract).then_inc(tk_lo, 1)

            def row(s):
                t, w = s // HP, s % HP
                dve.wait_ge(tk_prod, s + 1)
                if s == 0:
                    dve.wait_ge(pos_sum, 1)
                if t == 2 and w == 0:
                    dve.wait_ge(patch_out[0], 32)
                dve.scalar_tensor_tensor(store[:, t % 2, w, :], bank[4 + s % 2][:, 0:D], 1.0 / SCALE, pos_b[:, t, w, :],
                                         ALU.mult, ALU.add).then_inc(tk_row, 1)

            for f in range(8):
                low(f)
            dve.wait_ge(qkv_hi, 1)
            dve.scalar_tensor_tensor(qkv_l[:, :, :], qkv_raw, SCALE, qkv_h[:, :, :], ALU.mult, ALU.subtract)
            dve.scalar_tensor_tensor(wo_l[:, :, :], wo_raw, SCALE, wo_h[:, :, :], ALU.mult, ALU.subtract)
            dve.scalar_tensor_tensor(bq_hl[32:33, :], bq_raw[32:33, :], SCALE, bq_hl[32:33, :],
                                     ALU.mult, ALU.subtract).then_inc(qkv_lo, 1)
            for s in range(NX):
                if s + 2 < NX:
                    low(2 * (s + 2) + 4)
                    low(2 * (s + 2) + 5)
                row(s)

            def statistics(c, ts):
                if 0 in ts:
                    dve.wait_ge(h_in, c * 16 + 16)
                    apart(dve)
                for t in ts:
                    last = dve.bn_stats(stats[:, t, :], tile(h_all, c * G + t))
                return last

            def variance(last):
                own(last)
                apart(dve)
                for t in range(G):
                    last = dve.bn_aggr(mv[:, t, :], stats[:, t, :])
                own(last)
                dve.tensor_scalar(veps[:, :], mv[:, :, 1], EPS, None, ALU.add).then_inc(a_var, 1)

            def normal(i, t, s):
                after(dve, a_turned, i - 1)
                dve.tensor_scalar(xn[:, s, :], tile(h_all, i), mv[:, t, 0:1], rstd[:, t:t + 1],
                                  ALU.subtract, ALU.mult).then_inc(a_xn, 1)

            def low_x(i, s):
                dve.wait_ge(a_hi, i + 1)
                after(dve, a_q, i - 1)
                dve.tensor_tensor(xl[:, s, :], bank[s][:, 0:D], xh[:, s, :], ALU.subtract).then_inc(a_lo, 1)

            def project(c, half_0, base):
                own.step(base)
                for t in range(G):
                    i = c * G + t
                    s = (half_0 + t) % 2
                    if there(i + 1):
                        low_x(i + 1, 1 - s)
                    if there(i + 2):
                        if t == 3:
                            dve.wait_ge(a_rstd, c + 2)
                        normal(i + 2, (t + 2) % G, s)
                    dve.wait_ge(a_rk, i + 1)
                    after(dve, a_acc, i - 1)
                    dve.scalar_tensor_tensor(kvp[:, s, :], bank[4 + s][:, 0:D], rk[:, t:t + 1], vs[:, s, :],
                                             ALU.mult, ALU.mult).then_inc(a_kvp, 1)
                    if t < 3 and there(i + G):
                        last = statistics(c + 1, ((0, 1), (2, 3), (4,))[t])
                        if t == 2:
                            variance(last)

            variance(statistics(0, range(G)))
            dve.wait_ge(a_rstd, 1)
            normal(0, 0, 0)
            normal(1, 1, 1)
            low_x(0, 0)
            n0 = own.n
            PP = 2
            project(0, 0, n0)
            with dve.Fori(0, (NG - 3) // 2) as k:
                project(k * 2 + 1, 1, k * 2 * PP + (n0 + PP))
                project(k * 2 + 2, 0, k * 2 * PP + (n0 + 2 * PP))
            project(NG - 2, 1, n0 + (NG - 2) * PP)
            project(NG - 1, 0, n0 + (NG - 1) * PP)
            dve.wait_ge(a_nq, NT)
            dve.tensor_copy(nq[:, :], bank[7][:, 0:NT]).then_inc(a_nqc, 1)
            n1 = n0 + (NG - 1) * PP
            dve.wait_ge(kv_hi, 1)
            dve.tensor_tensor(kv_hl[B:2 * B, :], bank[7][B:2 * B, 0:D], kv_hl[B:2 * B, :], ALU.subtract).then_inc(kv_ready, 1)
            dve.wait_ge(rq_ready, 1)

            def multiply_qk(i, s):
                dve.wait_ge(b_kvb, i + 1)
                after(dve, b_qlo, i - 1)
                dve.tensor_tensor(sq[:, s, :], bank[s][:, 0:D], tile(q_all, i), ALU.mult).then_inc(b_qk, 1)

            def attend(c, half_0, base):
                own.step(base)
                for t in range(G):
                    i = c * G + t
                    s = (half_0 + t) % 2
                    if there(i + 1):
                        multiply_qk(i + 1, 1 - s)
                    if there(i):
                        dve.wait_ge(b_prod, i + 1)
                        own(dve.scalar_tensor_tensor(tile(h_all, i), bank[2 + s][:, 0:D],
                                                     rq[:, i:i + 1] if isinstance(i, int) else rq[:, bass.ds(i, 1)],
                                                     tile(h_all, i), ALU.mult, ALU.add))
                        apart(dve)
                        dve.bn_stats(stats[:, t, :], tile(h_all, i)).then_inc(b_h2, 1)
                        dve.wait_ge(b_h2, i + 1)
                        apart(dve)
                        dve.bn_aggr(mv[:, t, :], stats[:, t, :]).then_inc(b_var, 1)
                    if t < 3 and there(i - 2 * G):
                        hots(c - 2, ((0, 1), (2,), (3, 4))[t])
                    if t == 3 and there(i - G):
                        picks(c - 1)
                    if t == 4 and there(i - G):
                        places(c - 1)

            def top(src, at):
                own(dve.tensor_reduce(m12[:, :, at:at + 1], src, AX, ALU.max))
                own(dve.tensor_tensor(same[:, :, :], src, m12[:, :, at:at + 1].to_broadcast([P, G, E]), ALU.is_equal))
                own(dve.tensor_tensor(same[:, :, :], same[:, :, :], rev[:, :].unsqueeze(1).to_broadcast([P, G, E]), ALU.mult))
                own(dve.tensor_reduce(er[:, :, at:at + 1], same[:, :, :], AX, ALU.max))
                own(dve.tensor_tensor(pick[:, :, at * E:(at + 1) * E], same[:, :, :],
                                      er[:, :, at:at + 1].to_broadcast([P, G, E]), ALU.is_equal))

            def is_last(c):
                return isinstance(c, int) and c == NG - 1

            def picks(c):
                dve.wait_ge(b_lg, c + 1)
                after(dve, b_rank, c)
                top(lg[:, :, :], 0)
                own(dve.scalar_tensor_tensor(lg2[:, :, :], pick[:, :, 0:E], -BIG, lg[:, :, :], ALU.mult, ALU.add))
                top(lg2[:, :, :], 1)
                if is_last(c):
                    own(dve.memset(pick[LAST:P, G - 1, :], 0.0))
                own(dve.tensor_copy(cum[:, 0, :], cum[:, G, :]))
                for t in range(G):
                    add = dve.tensor_tensor(cum[:, t + 1, :], cum[:, t, :], pick[:, t, :], ALU.add)
                    if t + 1 < G:
                        own(add)
                add.then_inc(b_pick, 1)
                dve.tensor_tensor(ex[:, :, 0:E], lg[:, :, :], m12[:, :, 0:1].to_broadcast([P, G, E]), ALU.subtract)
                dve.tensor_tensor(ex[:, :, E:E + 1], m12[:, :, 1:2], m12[:, :, 0:1], ALU.subtract).then_inc(b_ex_in, 1)

            def places(c):
                dve.wait_ge(b_rank, c + 1)
                own(dve.tensor_tensor(pm[:, :, :], bank[5][:, 0:G * TOP * E].rearrange("p (t k) -> p t k", t=G),
                                      pick[:, :, :], ALU.mult))
                own(dve.tensor_reduce(posn[:, :, :], pm[:, :, :].rearrange("p t (k e) -> p t k e", k=TOP), AX, ALU.add))
                own(dve.tensor_scalar(posn[:, :, 1:2], posn[:, :, 1:2], -1.0, CAP - 1.0, ALU.mult, ALU.add))
                dve.tensor_scalar(hi_i[:, :, :], posn[:, :, :], -(P - 1) / 2, 1.0 / P, ALU.add, ALU.mult)
                own(dve.tensor_scalar(bad[:, :, :], posn[:, :, :], CAP - 0.5, None, ALU.is_gt))
                own(dve.scalar_tensor_tensor(bad[:, :, :], posn[:, :, :], -0.5, bad[:, :, :], ALU.is_lt, ALU.add))
                own(dve.scalar_tensor_tensor(key[:, :, :], er[:, :, :], -float(NS), hi_i[:, :, :], ALU.mult, ALU.add))
                own(dve.scalar_tensor_tensor(key[:, :, :], bad[:, :, :], NOWHERE, key[:, :, :], ALU.mult, ALU.add))
                if is_last(c):
                    own(dve.memset(key[LAST:P, G - 1, :], NOWHERE))
                own(dve.scalar_tensor_tensor(lo_f[:, :, :], hi_i[:, :, :], -float(P), posn[:, :, :], ALU.mult, ALU.add))
                dve.wait_ge(b_ex, c + 1)
                own(dve.tensor_reduce(ssum[:, :], ex[:, :, 0:E], AX, ALU.add))
                own(dve.reciprocal(gp[:, :, 0], ssum[:, :]))
                own(dve.tensor_tensor(gp[:, :, 1], gp[:, :, 0], ex[:, :, E], ALU.mult))
                own(dve.tensor_tensor(gt[:, :], gp[:, :, 0], gp[:, :, 1], ALU.add))
                own(dve.tensor_scalar(gt[:, :], gt[:, :], GATE_EPS, None, ALU.max))
                own(dve.reciprocal(gt[:, :], gt[:, :]))
                after(dve, w_out, c * 16)
                dve.tensor_tensor(w_cols[:, :, :], gp[:, :, :], gt[:, :].unsqueeze(2).to_broadcast([P, G, TOP]), ALU.mult).then_inc(b_w, 1)

            def hots(c, ts):
                if 0 in ts:
                    dve.wait_ge(b_inv, c * G + 1)
                for t in ts:
                    for k in range(TOP):
                        n = t * TOP + k
                        dve.tensor_scalar(hot_lo[:, n, :], lane[:, :], lo_f[:, t, k:k + 1], None, ALU.is_equal)
                        i = c * G + t
                        last = dve.tensor_scalar(hot_key[:, n, :], keys[:, :], key[:, t, k:k + 1],
                                                 token[:, i:i + 1] if isinstance(i, int) else token[:, bass.ds(i, 1)],
                                                 ALU.is_equal, ALU.mult)
                    last.then_inc(b_hot, 1)

            dve.wait_ge(b_hb, NT)
            multiply_qk(0, 0)
            n2 = n1 + own.n
            attend(0, 0, n2)
            n2 += own.n
            attend(1, 1, n2)
            AG = own.n
            with dve.Fori(1, (NG - 1) // 2) as k:
                attend(k * 2, 0, (k - 1) * 2 * AG + (n2 + AG))
                attend(k * 2 + 1, 1, (k - 1) * 2 * AG + (n2 + 2 * AG))
            assert own.n == AG, own.n
            n3 = n2 + (NG - 2) * AG
            attend(NG - 1, 0, n3)
            n3 += own.n
            attend(NG, 1, n3)
            n3 += own.n
            own.step(n3)

            def split_w1(e, s):
                dve.wait_ge(w1_hi, e + 1)
                dve.scalar_tensor_tensor(w1l[s], w1_raw, SCALE, w1h[s], ALU.mult, ALU.subtract).then_inc(w1_lo, 1)

            def split_w2(e, s):
                dve.wait_ge(w2_hi, e + 1)
                dve.scalar_tensor_tensor(w2l[s], w2_raw, SCALE, w2h[s], ALU.mult, ALU.subtract).then_inc(w2_lo, 1)

            hots(NG - 1, range(G))

            dve.wait_ge(counted, 1)
            own(dve.tensor_copy(cnt[:, :], bank[6][:, 0:TOP * E]))

            def count(k):
                return cnt[:, k * E:(k + 1) * E].unsqueeze(2).to_broadcast([P, E, NS])

            def ej(v):
                return v[:, :].rearrange("p (e j) -> p e j", e=E)

            own(dve.tensor_tensor(ej(t0), ej(slot), count(0), ALU.is_lt))
            own(dve.scalar_tensor_tensor(t0[:, :], slot[:, :], CAP - 0.5, t0[:, :], ALU.is_lt, ALU.mult))
            own(dve.tensor_scalar(tmp[:, :], slot[:, :], -1.0, CAP - 1.0, ALU.mult, ALU.add))
            own(dve.tensor_tensor(ej(t1), ej(tmp), count(1), ALU.is_lt))
            own(dve.scalar_tensor_tensor(t1[:, :], tmp[:, :], -0.5, t1[:, :], ALU.is_gt, ALU.mult))
            own(dve.tensor_tensor(tmp[:, :], t0[:, :], t1[:, :], ALU.mult))
            own(dve.tensor_tensor(t1[:, :], t1[:, :], tmp[:, :], ALU.subtract))
            own(dve.tensor_tensor(ids[:, :], bank[7][:, 0:KEY], t0[:, :], ALU.mult))
            own(dve.tensor_tensor(tmp[:, :], bank[7][:, KEY:2 * KEY], t1[:, :], ALU.mult))
            own(dve.tensor_tensor(ids[:, :], ids[:, :], tmp[:, :], ALU.add))
            own(dve.tensor_copy(from_i[:, :], ids[:, :]))
            own(dve.tensor_tensor(tmp[:, :], t0[:, :], t1[:, :], ALU.add))
            own(dve.tensor_scalar(tmp[:, :], tmp[:, :], -1.0, 1.0, ALU.mult, ALU.add))
            own(dve.scalar_tensor_tensor(ids[:, :], tmp[:, :], trash[:, 0:1], ids[:, :], ALU.mult, ALU.add))
            dve.tensor_copy(to_i[:, :], ids[:, :]).then_inc(tables, 1)
            split_w1(0, 0)
            split_w2(0, 0)
            n4 = own.base + own.n

            def split_rows(e, s, g, js):
                u, v = e * CH + g, (s + g) % 2
                for j in js:
                    m = min(P, CAP - (g * ST + j) * P)
                    dve.wait_ge(e_xhi, u * ST + j + 1)
                    if j == 0:
                        after(dve, e_up, (u - 1) * NM)
                    dve.tensor_tensor(xt_l[:, v, :, j * P:j * P + m],
                                      bank[(s + g * ST + j) % 2][:, 0:D].rearrange("p (k n) -> p k n", k=ND)[:, :, 0:m],
                                      xt_h[:, v, :, j * P:j * P + m], ALU.subtract).then_inc(e_xlo, 1)

            def expert(e, s, last, base):
                own.step(base)
                for g in range(CH):
                    w = min(ST * P, CAP - g * ST * P)
                    u = e * CH + g
                    v = (s + g) % 2
                    nxt = (e, s, g + 1) if g + 1 < CH else None if last else (e + 1, 1 - s, 0)
                    if g == 0:
                        def cols(tab):
                            return tab[:, e * NS:(e + 1) * NS] if isinstance(e, int) else tab[:, bass.ds(e * NS, NS)]
                        for gg in range(CH):
                            dve.wait_ge(got[s][gg], gathered(e, s))
                        own(dve.tensor_tensor(ws[:, s, :], rows[s][:, :, D], cols(t0), ALU.mult))
                        own(dve.tensor_tensor(wtmp[:, s, :], rows[s][:, :, D + 1], cols(t1), ALU.mult))
                        own(dve.tensor_tensor(ws[:, s, :], ws[:, s, :], wtmp[:, s, :], ALU.add))
                        own(dve.tensor_scalar(wtmp[:, s, :], ws[:, s, :], 1.0 / SCALE, None, ALU.mult))
                        dve.wait_ge(b2_in, e * 16 + 16)
                    for m in range(NM):
                        k = u * NM + m
                        dve.wait_ge(e_gelu, k + 1)
                        if m == 0:
                            after(dve, e_down, (u - 1) * ST)
                        dve.tensor_copy(hid_h[v][:, m, 0:w], hf[:, m % 2, 0:w]).then_inc(e_hhi, 1)
                        dve.wait_ge(e_hhi, k + 1)
                        dve.tensor_tensor(hid_l[v][:, m, 0:w], hf[:, m % 2, 0:w], hid_h[v][:, m, 0:w],
                                          ALU.subtract).then_inc(e_hlo, 1)
                    if g == 0 and not last:
                        split_w1(e + 1, 1 - s)
                    if g == 1 and not last:
                        split_w2(e + 1, 1 - s)
                    if nxt:
                        split_rows(*nxt, (0, 1))
                    for j in range(ST):
                        jj = g * ST + j
                        m = min(P, w - j * P)
                        k = u * ST + j
                        own(dve.tensor_scalar(b2w[0:m, jj % 2, :], b2_b[0:m, s, :], ws[0:m, s, jj:jj + 1], None, ALU.mult))
                        dve.wait_ge(e_down, k + 1)
                        after(dve, added, (k - 2) * 16)
                        dve.scalar_tensor_tensor(y_sb[0:m, jj % 3, :], bank[5 + (s + jj) % 2][0:m, 0:D],
                                                 wtmp[0:m, s, jj:jj + 1], b2w[0:m, jj % 2, :],
                                                 ALU.mult, ALU.add).then_inc(e_y, 1)
                        if j == 0 and nxt:
                            split_rows(*nxt, (2,))

            EO = 4 + NS
            split_rows(0, 0, 0, range(ST))
            expert(0, 0, False, n4)
            assert own.n == EO
            with dve.Fori(0, (E - 2) // 2) as k:
                expert(k * 2 + 1, 1, False, k * 2 * EO + (n4 + EO))
                expert(k * 2 + 2, 0, False, k * 2 * EO + (n4 + 2 * EO))
            expert(E - 1, 1, True, n4 + (E - 1) * EO)

        @block.tensor
        def _(pe):
            def three(dst, lh, ll, rh, rl, start, stop):
                pe.matmul(dst, lh, rh, start=start, stop=False)
                pe.matmul(dst, lh, rl, start=False, stop=False)
                return pe.matmul(dst, ll, rh, start=False, stop=stop)

            def add_zeros(dst, n, start):
                return pe.matmul(dst, zero_h[:, 0:P], zero_h[:, 0:n], start=start, stop=not start, skip_group_check=True)

            pe.wait_ge(consts, 2)
            pe.wait_ge(raw_in, 16)

            def turn(f):
                step, part = f // 2, f % 2
                if f >= 4:
                    pe.wait_ge(tk_lo, f - 3)
                for k in range(3):
                    kt = 3 * part + k
                    if step < 2:
                        src = tokw_raw[:, step, kt * P:(kt + 1) * P]
                    else:
                        s = step - 2
                        if k == 0:
                            pe.wait_ge(tk_patch, s + 1)
                        src = patch[:, s % 2, kt * P:(kt + 1) * P]
                    last = pe.transpose(bank[f % 4][:, k * P:(k + 1) * P], src, ident[:, :])
                last.then_inc(tk_turned, 1)

            for f in range(4):
                turn(f)
            turn(4)
            turn(5)
            pe.wait_ge(tk_lo, 4)
            for s in range(NX):
                if s + 1 < NX:
                    turn(2 * (s + 1) + 4)
                    turn(2 * (s + 1) + 5)
                pe.wait_ge(tk_lo, 2 * s + 6)
                if s >= 2:
                    pe.wait_ge(tk_row, s - 1)
                for kt in range(NKT):
                    cut = slice(kt * P, (kt + 1) * P)
                    last = three(bank[4 + s % 2][:, 0:D], pat_h[:, s % 2, cut], pat_l[:, s % 2, cut],
                                 tokw_h[:, kt, :], tokw_l[:, kt, :], kt == 0, kt == NKT - 1)
                last.then_inc(tk_prod, 1)
            pe.wait_ge(raw2_in, 16 * 7)
            pe.transpose(bank[0][:, 0:E * NM], b1_raw, ident[0:E * NM, 0:E * NM]).then_inc(b1_turned, 1)
            pe.wait_ge(b1_ok, 1)
            pe.wait_ge(tk_row, NX)
            pe.wait_ge(qkv_lo, 2)
            pe.wait_ge(consts, 3)

            def turn_x(i, s):
                pe.wait_ge(a_xn, i + 1)
                after(pe, a_lo, i - 1)
                for k in range(ND):
                    last = pe.transpose(bank[s][:, k * P:(k + 1) * P], xn[:, s, k * P:(k + 1) * P], ident[:, :])
                last.then_inc(a_turned, 1)

            def sums(i, s):
                pe.wait_ge(a_qsq, i + 1)
                dst = bank[7][:, i:i + 1] if isinstance(i, int) else bank[7][:, bass.ds(i, 1)]
                for k in range(ND):
                    last = pe.matmul(dst, sq[:, s, k * P:(k + 1) * P], ones_f[:, :], start=k == 0, stop=k == ND - 1)
                last.then_inc(a_nq, 1)
                pe.wait_ge(a_kvp, i + 1)
                for k in range(ND):
                    rhs = ind[:, i + 1, :] if isinstance(i, int) else ind[:, bass.ds(i + 1, 1), :].rearrange("p a b -> p (a b)")
                    last = pe.matmul(bank[6][:, k * B:(k + 1) * B], kvp[:, s, k * P:(k + 1) * P], rhs,
                                     start=False, stop=False, skip_group_check=True)
                if isinstance(i, int) and i == NT - 1:
                    last = add_zeros(bank[6][:, 0:ND * B], ND * B, False)
                last.then_inc(a_acc, 1)

            def project(c, half_0):
                for t in range(G):
                    i = c * G + t
                    s = (half_0 + t) % 2
                    pe.wait_ge(a_lo, i + 1)
                    after(pe, a_kvp, i - 1)
                    dst = bank[4 + s][:, 0:2 * D]
                    pe.matmul(dst, ones_h[:, :], bq_hl[:, D:3 * D], start=True, stop=False)
                    for k in range(ND):
                        cut = slice(k * P, (k + 1) * P)
                        last = three(dst, xh[:, s, cut], xl[:, s, cut], qkv_h[:, k, D:3 * D], qkv_l[:, k, D:3 * D],
                                     False, k == ND - 1)
                    last.then_inc(a_kv, 1)
                    after(pe, a_qsq, i - 1)
                    for dh in range(ND):
                        dst = bank[2 + s][:, dh * P:(dh + 1) * P]
                        pe.matmul(dst, bq_hl[:, dh * P:(dh + 1) * P], ones_h[:, :], start=True, stop=False)
                        for k in range(ND):
                            cut = slice(k * P, (k + 1) * P)
                            last = three(dst, qkv_h[:, k, dh * P:(dh + 1) * P], qkv_l[:, k, dh * P:(dh + 1) * P],
                                         xh[:, s, cut], xl[:, s, cut], False, k == ND - 1)
                    last.then_inc(a_q, 1)
                    if there(i + 2):
                        turn_x(i + 2, s)
                    if there(i - 1):
                        sums(i - 1, 1 - s)

            add_zeros(bank[6][:, 0:ND * B], ND * B, True)
            turn_x(0, 0)
            turn_x(1, 1)
            project(0, 0)
            with pe.Fori(0, (NG - 3) // 2) as k:
                project(k * 2 + 1, 1)
                project(k * 2 + 2, 0)
            project(NG - 2, 1)
            project(NG - 1, 0)
            sums(NT - 1, (NT - 1) % 2)
            pe.wait_ge(kv_copied, 1)
            pe.wait_ge(a_nqc, 1)
            for k in range(ND):
                last = pe.transpose(bank[7][:, k * P:(k + 1) * P], kvt[:, k, :], ident[:, :])
            last.then_inc(kv_turned, 1)
            pe.wait_ge(kv_ready, 1)

            def spread(i, s):
                after(pe, b_qk, i - 1)
                rhs = ind_t[:, i * P:(i + 1) * P] if isinstance(i, int) else ind_t[:, bass.ds(i * P, P)]
                for k in range(ND):
                    last = pe.matmul(bank[s][:, k * P:(k + 1) * P], kv_hl[:, k * P:(k + 1) * P], rhs,
                                     start=True, stop=True)
                last.then_inc(b_kvb, 1)

            def ranks(c):
                pe.wait_ge(b_pick, c + 1)
                dst = bank[5][:, 0:G * TOP * E]
                pe.matmul(dst, upper[:, :], pick[:, :, :].rearrange("p t k -> p (t k)"), start=True, stop=False)
                pe.matmul(dst, ones_b[:, :], cum[:, 0:G, :].rearrange("p t k -> p (t k)"),
                          start=False, stop=True).then_inc(b_rank, 1)

            def invert(c, ts):
                for t in ts:
                    pe.wait_ge(b_hot, c * G + t + 1)
                    for n in range(t * TOP, (t + 1) * TOP):
                        k = n % TOP
                        last = pe.matmul(bank[7][:, k * KEY:(k + 1) * KEY], hot_lo[:, n, :], hot_key[:, n, :],
                                         start=False, stop=False, skip_group_check=True)
                    if isinstance(c, int) and c == NG - 1 and t == G - 1:
                        last = add_zeros(bank[7][:, 0:TOP * KEY], TOP * KEY, False)
                    last.then_inc(b_inv, 1)

            def attend(c, half_0):
                for t in range(G):
                    i = c * G + t
                    s = (half_0 + t) % 2
                    if there(i):
                        pe.wait_ge(b_qlo, i + 1)
                        after(pe, b_h2, i - 1)
                        for k in range(ND):
                            cut = slice(k * P, (k + 1) * P)
                            last = three(bank[2 + s][:, 0:D], xh[:, s, cut], xl[:, s, cut], wo_h[:, k, :], wo_l[:, k, :],
                                         k == 0, k == ND - 1)
                        last.then_inc(b_prod, 1)
                    if there(i + 2):
                        spread(i + 2, s)
                    if t == 4 and there(i - G):
                        ranks(c - 1)
                    if there(i - 2):
                        pe.wait_ge(b_xn, i - 1)
                        after(pe, b_xt, i - 2)
                        src = x2[half_0 if t >= 2 else 1 - half_0]
                        for k in range(ND):
                            last = pe.transpose(bank[4][:, k * P:(k + 1) * P], src[:, (t - 2) % G, k * P:(k + 1) * P], ident[:, :])
                        last.then_inc(b_turned, 1)
                    if there(i - 3):
                        u = (t - 3) % G
                        pe.wait_ge(b_xt, i - 2)
                        if u == 0:
                            after(pe, b_lg, c)
                        for k in range(ND):
                            last = pe.matmul(bank[6][:, u * E:(u + 1) * E], xn[:, 1 - s, k * P:(k + 1) * P],
                                             wg_sb[:, k, :], start=k == 0, stop=k == ND - 1)
                        last.then_inc(b_logit, 1)
                    if 1 <= t <= 3 and there(i - 2 * G):
                        invert(c - 2, ((0, 1), (2,), (3, 4))[t - 1])

            add_zeros(bank[7][:, 0:TOP * KEY], TOP * KEY, True).then_inc(b_inv, 1)
            spread(0, 0)
            spread(1, 1)
            attend(0, 0)
            attend(1, 1)
            with pe.Fori(1, (NG - 1) // 2) as k:
                attend(k * 2, 0)
                attend(k * 2 + 1, 1)
            attend(NG - 1, 0)
            attend(NG, 1)
            invert(NG - 1, range(G))
            pe.matmul(bank[6][:, 0:TOP * E], ones_b[:, :], cum[:, G, :], start=True, stop=True).then_inc(counted, 1)

            pe.wait_ge(tables, 1)
            up = [2, 3, 4, 7]

            def turn_rows(e, s, g, js):
                for j in js:
                    m = min(P, CAP - (g * ST + j) * P)
                    k = (e * CH + g) * ST + j
                    if j == 0:
                        pe.wait_ge(got[s][g], gathered(e, s))
                    after(pe, e_xlo, k - 1)
                    for kk in range(ND):
                        last = pe.transpose(bank[(s + g * ST + j) % 2][:, kk * P:kk * P + m],
                                            rows[s][0:m, g * ST + j, kk * P:(kk + 1) * P], ident[0:m, 0:m])
                    last.then_inc(e_turned, 1)

            def expert(e, s, last_one):
                for g in range(CH):
                    w = min(ST * P, CAP - g * ST * P)
                    u = e * CH + g
                    v = (s + g) % 2
                    if g == 0:
                        pe.wait_ge(w1_lo, e + 1)
                    pe.wait_ge(e_xlo, u * ST + ST)
                    for m in range(NM):
                        after(pe, e_gelu, u * NM + m - 3)
                        for k in range(ND):
                            cut = slice(m * P, (m + 1) * P)
                            last = three(bank[up[m % 4]][:, 0:w], w1h[s][:, k, cut], w1l[s][:, k, cut],
                                         xt_h[:, v, k, 0:w], xt_l[:, v, k, 0:w], k == 0, k == ND - 1)
                        last.then_inc(e_up, 1)
                    nxt = (e, s, g + 1) if g + 1 < CH else None if last_one else (e + 1, 1 - s, 0)
                    if nxt:
                        turn_rows(*nxt, (0, 1))
                    if g == 0:
                        pe.wait_ge(w2_lo, e + 1)
                    for j in range(ST):
                        mj = min(P, w - j * P)
                        kj = u * ST + j
                        after(pe, e_y, kj - 1)
                        dst = bank[5 + (s + g * ST + j) % 2][0:mj, 0:D]
                        for m in range(NM):
                            if j == 0:
                                pe.wait_ge(e_hlo, u * NM + m + 1)
                            cut = slice(j * P, j * P + mj)
                            last = three(dst, hid_h[v][:, m, cut], hid_l[v][:, m, cut], w2h[s][:, m, :], w2l[s][:, m, :],
                                         m == 0, m == NM - 1)
                        last.then_inc(e_down, 1)
                        if j == 0 and nxt:
                            turn_rows(*nxt, (2,))

            turn_rows(0, 0, 0, range(ST))
            expert(0, 0, False)
            with pe.Fori(0, (E - 2) // 2) as k:
                expert(k * 2 + 1, 1, False)
                expert(k * 2 + 2, 0, False)
            expert(E - 1, 1, True)


_INS = ["x", "txt", "L0_tok_W", "L0_tok_b", "L0_tok_cls_token", "L0_tok_pos_embedding", "L0_attn_Wqkv", "L0_attn_bqkv",
        "L0_attn_Wout", "L0_attn_bout", "L0_ffn_wg", "L0_ffn_w1", "L0_ffn_b1", "L0_ffn_w2", "L0_ffn_b2"]


def kernel(**inputs):
    import concourse.bacc as bacc
    from concourse.bass_utils import run_bass_kernel_spmd

    nc = bacc.Bacc("TRN2", target_bir_lowering=False, num_devices=1)
    arrays, args = {}, []
    for name in _INS:
        a = np.ascontiguousarray(inputs[name])
        arrays[f"in_{name}"] = a
        args.append(nc.dram_tensor(f"in_{name}", a.shape, mybir.dt.from_np(a.dtype), kind="ExternalInput").ap())
    out = nc.dram_tensor("out_rows", (N + P, D), F32, kind="ExternalOutput").ap()
    build(nc, *args, out)
    r = run_bass_kernel_spmd(nc, [arrays], core_ids=[0])
    return r.results[0]["out_rows"][0:N].reshape(B, SEQ, D)
```

```python
from contextlib import ExitStack

import numpy as np
import concourse.bass as bass
from concourse import mybir

F32 = mybir.dt.float32
F16 = mybir.dt.float16
BF16 = mybir.dt.bfloat16
I32 = mybir.dt.int32
U32 = mybir.dt.uint32
ALU = mybir.AluOpType
ACT = mybir.ActivationFunctionType
AX = mybir.AxisListType.X

P = 128
B, C, IMG, PATCH = 64, 3, 96, 16
HP = IMG // PATCH
NPATCH = HP * HP
D = 256
ND = D // P
ROOT_D = 16
KD = C * PATCH * PATCH
NKT = KD // P
TXT = 32
SEQ = 1 + NPATCH + TXT
N = B * SEQ
G = 5
NG = -(-N // (P * G))
NT = NG * G
NPAD = NT * P
assert ROOT_D * ROOT_D == D
LAST = N - (NT - 1) * P
E, TOP, HID = 8, 2, 1024
CAP = -(-TOP * N // E)
NS = -(-CAP // P)
CH = 3
ST = NS // CH
NM = HID // P
XW = D + TOP
EPS = 1e-5
GATE_EPS = 1e-9
SCALE = 64.0
NOWHERE = 1000.0
BIG = 3.0e38
KEY = NS * E


def after(engine, sem, value):
    if not isinstance(value, int) or value > 0:
        engine.wait_ge(sem, value)


def there(i):
    return not isinstance(i, int) or 0 <= i < NT


def group_there(c):
    return not isinstance(c, int) or 0 <= c < NG


def apart(engine):
    engine.nop(nofuse=True)


class Own:

    def __init__(self, engine, sem):
        self.engine, self.sem, self.base, self.n = engine, sem, 0, 0

    def step(self, base):
        self.base, self.n = base, 0

    def __call__(self, instruction):
        self.mark(instruction)
        self.wait()

    def mark(self, instruction):
        instruction.then_inc(self.sem, 1)
        self.n += 1

    def wait(self):
        self.engine.wait_ge(self.sem, self.base + self.n)


def build(nc, x, txt, tok_w, tok_b, cls, pos, wqkv, bqkv, wout, bout, wg, w1, b1, w2, b2, out):
    ctx = ExitStack()
    with ctx:
        def sb(name, shape, dt=F32):
            return ctx.enter_context(nc.sbuf_tensor(name, shape, dt))

        def sem(name):
            return ctx.enter_context(nc.semaphore(name))

        h_rows = nc.dram_tensor("h_rows", (NPAD, D), F32, kind="Internal").ap()
        x_rows = nc.dram_tensor("x_rows", (NPAD, XW), F32, kind="Internal").ap()

        region_h = sb("region_h", [P, NT * D])
        region_q = sb("region_q", [P, NT * D])
        region_x = sb("region_x", [P, KD * HP * (HP // 2)])
        region_i = sb("region_i", [P, NPAD // 2 + (NT + 1) * B])

        h_all = region_h[:, :].rearrange("p (i d) -> p i d", d=D)
        q_all = region_q[:, :].rearrange("p (i d) -> p i d", d=D)
        tokw_raw = region_h[:, 0:2 * KD].rearrange("p (t k) -> p t k", t=2)
        qkv_raw = region_h[:, 2 * KD:2 * KD + ND * 3 * D].rearrange("p (k n) -> p k n", k=ND)
        wo_raw = region_h[:, 4 * KD:4 * KD + ND * D].rearrange("p (k n) -> p k n", k=ND)
        bq_raw = region_h[:, 5 * KD:5 * KD + D]
        tokb_b = region_h[:, 6 * KD:6 * KD + D]
        cls_b = region_h[0:B, 6 * KD + D:6 * KD + 2 * D]
        pos0_b = region_h[0:B, 6 * KD + 2 * D:6 * KD + 3 * D]
        zeros = region_h[0:P, 6 * KD + 3 * D:6 * KD + 4 * D]
        b1_raw = region_h[0:E * NM, 6 * KD + 4 * D:6 * KD + 4 * D + P]
        NTX = HP // 2
        pos_b = region_q[:, 0:NTX * HP * D].rearrange("p (t w d) -> p t w d", t=NTX, w=HP)
        store = region_q[:, NTX * HP * D:(NTX + 2) * HP * D].rearrange("p (s w d) -> p s w d", s=2, w=HP)
        x_sb = region_x[:, :].rearrange("p (t c i w j) -> p t c i w j", t=NTX, c=C, i=PATCH, w=HP)
        ind_t = region_i[:, 0:NPAD // 2].bitcast(F16)
        ind = region_i[:, NPAD // 2:].bitcast(F16).rearrange("p (i b) -> p i b", b=2 * B)
        WR = ND * HID
        w1_raw = region_x[:, 0:WR].rearrange("p (k n) -> p k n", k=ND)
        w2_raw = region_x[:, WR:2 * WR].rearrange("p (k n) -> p k n", k=NM)
        XT = region_x.shape[1] // NTX
        halves = [region_x[:, (s + 1) * XT:(s + 1) * XT + 2 * WR].bitcast(F16) for s in range(2)]
        w1h = [v[:, 0:WR].rearrange("p (k n) -> p k n", k=ND) for v in halves]
        w1l = [v[:, WR:2 * WR].rearrange("p (k n) -> p k n", k=ND) for v in halves]
        w2h = [v[:, 2 * WR:3 * WR].rearrange("p (k n) -> p k n", k=NM) for v in halves]
        w2l = [v[:, 3 * WR:4 * WR].rearrange("p (k n) -> p k n", k=NM) for v in halves]
        HW = NM * ST * P // 2
        hid_h = [region_q[:, (2 * s) * HW:(2 * s + 1) * HW].bitcast(F16).rearrange("p (m n) -> p m n", m=NM) for s in range(2)]
        hid_l = [region_q[:, (2 * s + 1) * HW:(2 * s + 2) * HW].bitcast(F16).rearrange("p (m n) -> p m n", m=NM) for s in range(2)]
        rows = [region_i[:, 0:NS * XW].rearrange("p (j d) -> p j d", d=XW),
                region_q[:, 4 * HW:4 * HW + NS * XW].rearrange("p (j d) -> p j d", d=XW)]

        tokw_h, tokw_l = (sb(n, [P, NKT, D], F16) for n in ("tokw_h", "tokw_l"))
        qkv_h, qkv_l = (sb(n, [P, ND, 3 * D], F16) for n in ("qkv_h", "qkv_l"))
        wo_h, wo_l = (sb(n, [P, ND, D], F16) for n in ("wo_h", "wo_l"))
        bq_hl = sb("bq_hl", [P, D], F16)
        wg_sb = sb("wg_sb", [P, ND, E])
        bout_b = sb("bout_b", [P, D])
        b1_cols = sb("b1_cols", [P, E * NM])
        ident = sb("ident", [P, P])
        upper = sb("upper", [P, P], BF16)
        ones_b = sb("ones_b", [P, P], BF16)
        ones_h = sb("ones_h", [P, P], F16)
        zero_h = sb("zero_h", [P, 2 * TOP * KEY], F16)
        ones_f = sb("ones_f", [P, 1])
        lane = sb("lane", [P, P])
        keys = sb("keys", [P, KEY])
        slot = sb("slot", [P, KEY])
        tile_no = sb("tile_no", [P, NT])
        number = sb("number", [P, 1])
        trash = sb("trash", [P, 1])
        rev = sb("rev", [P, E])
        half = sb("half", [P, NT])
        minus = sb("minus", [P, 1])
        minus_r = sb("minus_r", [P, 1])
        sums, offset, var_2 = (sb(n, [P, G]) for n in ("sums", "offset", "var_2"))
        eps = sb("eps", [P, 1])
        pat = sb("pat", [P, 2 * KD])
        pat_h, pat_l = (pat[:, k * KD:(k + 1) * KD].bitcast(F16).rearrange("p (s k) -> p s k", s=2) for k in range(2))
        stats = sb("stats", [P, G, 6])
        mv_2 = sb("mv_2", [P, 2, G, 2])
        mv = mv_2[:, 0]
        veps = sb("veps", [P, G])
        rstd_2 = sb("rstd_2", [P, 2, G])
        rstd = rstd_2[:, 0]
        nmr = sb("nmr", [P, G])
        trio = sb("trio", [P, 6 * D])
        patch = trio[:, :].rearrange("p (s k) -> p s k", s=2)
        xn, sq = (trio[:, 2 * k * D:2 * (k + 1) * D].rearrange("p (s d) -> p s d", s=2) for k in range(2))
        vs_flat = trio[:, 4 * D:6 * D]
        xh, xl = (sb(n, [P, 2, D], F16) for n in ("xh", "xl"))
        junk = sb("junk", [P, 2, D])
        nk = sb("nk", [P, G])
        rk = sb("rk", [P, G])
        kvp = sb("kvp", [P, 2, D])
        kvp_h, kvp_l = (sb(n, [P, 2, D], F16) for n in ("kvp_h", "kvp_l"))
        nq = sb("nq", [P, NT])
        rq = sb("rq", [P, NT])
        kv_hl = sb("kv_hl", [P, D], F16)
        x2_even = sb("x2", [P, G, D])
        x2 = [x2_even[:, :, :], pat[:, 0:G * D].rearrange("p (t d) -> p t d", d=D)]
        w_cols = sb("w_cols", [P, G, TOP])
        lg = sb("lg", [P, G, E])
        lg2 = sb("lg2", [P, G, E])
        same = sb("same", [P, G, E])
        m12 = sb("m12", [P, G, 2])
        er = sb("er", [P, G, TOP])
        pick = sb("pick", [P, G, TOP * E], BF16)
        cum = sb("cum", [P, G + 1, TOP * E], BF16)
        ex = sb("ex", [P, G, E + 1])
        ssum = sb("ssum", [P, G])
        gp = sb("gp", [P, G, TOP])
        gt = sb("gt", [P, G])
        pm = sb("pm", [P, G, TOP * E])
        posn = sb("posn", [P, G, TOP])
        hi_i = sb("hi_i", [P, G, TOP], I32)
        lo_f = sb("lo_f", [P, G, TOP])
        bad = sb("bad", [P, G, TOP])
        key = sb("key", [P, G, TOP])
        hot_lo = sb("hot_lo", [P, G * TOP, P], BF16)
        hot_key = sb("hot_key", [P, G * TOP, KEY], BF16)
        hot_token = sb("hot_token", [P, G * TOP, 2, KEY], BF16)
        bkv_b = hot_lo[:, :, :].rearrange("p n c -> p (n c)").bitcast(F32)[:, 0:2 * D]
        kvb = [vs_flat, hot_token[:, :, :, :].rearrange("p n a k -> p (n a k)").bitcast(F32)[:, 0:2 * D]]
        t01 = sb("t01", [P, TOP, KEY])
        t0, t1 = t01[:, 0, :], t01[:, 1, :]
        in_cap = sb("in_cap", [P, KEY])
        slot_r = sb("slot_r", [P, KEY])
        spill = sb("spill", [P, KEY])
        ids = sb("ids", [P, KEY])
        tmp = sb("tmp", [P, KEY])
        tok2 = sb("tok2", [P, TOP, KEY])
        from_i = sb("from_i", [P, KEY], U32)
        to_i = sb("to_i", [P, KEY], U32)
        from_e = sb("from_e", [P, 2, NS], U32)
        to_e = sb("to_e", [P, 2, NS], U32)
        b2_b = sb("b2_b", [P, 2, D])
        ws = sb("ws", [P, 2, NS])
        wtmp = sb("wtmp", [P, 2, NS])
        xt_h, xt_l = (v.rearrange("p s (k n) -> p s k n", k=ND) for v in (pat_h, pat_l))
        hf = x2_even[:, 0:3, :].rearrange("p t d -> p (t d)").rearrange("p (s n) -> p s n", s=2)
        b2w = sb("b2w", [P, 2, D])
        y_sb = sb("y_sb", [P, 3, D])

        bank = [ctx.enter_context(nc.psum_tensor(f"bank{k}", [P, 512], F32)) for k in range(8)]

        (raw_in, raw2_in, consts, qkv_hi, qkv_lo, pos_sum, row0_sum, txt_out, cls_out, pad_out,
         pool_own, dve_own) = (sem(n) for n in (
             "raw_in", "raw2_in", "consts", "qkv_hi", "qkv_lo", "pos_sum", "row0_sum", "txt_out", "cls_out",
             "pad_out", "pool_own", "dve_own"))
        pos_in = [sem(f"pos_in{t}") for t in range(NTX)]
        row0_in = sem("row0_in")
        patch_out = [sem(f"patch_out{t}") for t in range(NTX)]
        x_in = [sem(f"x_in{t}") for t in range(NTX)]
        tk_patch, tk_turned, tk_hi, tk_lo, tk_prod, tk_row, b1_turned, b1_ok = (sem(n) for n in (
            "tk_patch", "tk_turned", "tk_hi", "tk_lo", "tk_prod", "tk_row", "b1_turned", "b1_ok"))
        (h_in, a_var, a_rstd, a_xn, a_turned, a_hi, a_lo, a_q, a_kv, a_qsq, a_v, a_rk, a_kvp, a_nq, a_acc, a_nqc) = (
            sem(n) for n in ("h_in", "a_var", "a_rstd", "a_xn", "a_turned", "a_hi", "a_lo", "a_q", "a_kv", "a_qsq",
                             "a_v", "a_rk", "a_kvp", "a_nq", "a_acc", "a_nqc"))
        kv_hi, kv_ready, rq_ready = (sem(n) for n in ("kv_hi", "kv_ready", "rq_ready"))
        (b_kvb, b_qk, b_qhi, b_qlo, b_prod, b_hb, b_h2, b_var, b_rstd, b_xn, b_turned, b_xt, b_logit, b_lg, b_pick,
         b_rank, b_ex_in, b_ex, b_w, b_hot, b_inv, out_in, rows_out_a) = (sem(n) for n in (
             "b_kvb", "b_qk", "b_qhi", "b_qlo", "b_prod", "b_hb", "b_h2", "b_var", "b_rstd", "b_xn", "b_turned",
             "b_xt", "b_logit", "b_lg", "b_pick", "b_rank", "b_ex_in", "b_ex", "b_w", "b_hot", "b_inv",
             "out_in", "rows_out_a"))
        w_out = sem("w_out")
        b_key = sem("b_key")
        rows_out = [rows_out_a, sem("rows_out_b")]
        pad2_out = sem("pad2_out")
        h_first, b_mean = sem("h_first"), sem("b_mean")
        a_kvb, a_kvh, a_kvl = sem("a_kvb"), sem("a_kvh"), sem("a_kvl")
        counts_ok, masks_ok = sem("counts_ok"), sem("masks_ok")
        counted, tables = sem("counted"), sem("tables")
        w1_in, w2_in, w1_hi, w1_lo, w2_hi, w2_lo, b2_in = (sem(n) for n in (
            "w1_in", "w2_in", "w1_hi", "w1_lo", "w2_hi", "w2_lo", "b2_in"))
        got = [[sem(f"got{s}_{g}") for g in range(CH)] for s in range(2)]
        (e_turned, e_xhi, e_xlo, e_up, e_gelu, e_hhi, e_hlo, e_down, e_y, added) = (sem(n) for n in (
            "e_turned", "e_xhi", "e_xlo", "e_up", "e_gelu", "e_hhi", "e_hlo", "e_down", "e_y", "added"))

        def tile(region, i):
            return region[:, i, :] if isinstance(i, int) else region[:, bass.ds(i, 1), :].rearrange("p a d -> p (a d)")

        def gathered(e, s):
            return ((e - s) // 2 + 1) * ST * 16 if isinstance(e, int) else (e - s + 2) * (ST * 8)

        block = ctx.enter_context(nc.Block())
        NF = 2 * (2 + NTX * HP)
        NX = NTX * HP

        @block.sync
        def _(sp):
            def load_x(t):
                for hh in range(2):
                    src = x[:, :, (2 * t + hh) * PATCH:(2 * t + hh + 1) * PATCH, :].rearrange("b c i w -> b c (i w)")
                    dst = x_sb[hh * B:(hh + 1) * B, t].rearrange("p c i w j -> p c (i w j)")
                    sp.dma_start(dst, src).then_inc(x_in[t], 16)

            def load_pos(t):
                for hh in range(2):
                    first = 1 + (2 * t + hh) * HP
                    sp.dma_start(pos_b[hh * B:(hh + 1) * B, t].rearrange("p w d -> p (w d)"),
                                 pos[0, first:first + HP, :].rearrange("w d -> (w d)").partition_broadcast(B)).then_inc(pos_in[t], 16)

            def one(v, e):
                return v[e] if isinstance(e, int) else v[bass.ds(e, 1)].squeeze(0)

            def w1_of(e):
                return one(w1, e).rearrange("(k p) n -> p k n", p=P)

            def w2_of(e):
                return one(w2, e).rearrange("(k p) n -> p k n", p=P)

            def b2_of(e):
                return one(b2, e)

            sp.dma_start(tokw_raw, tok_w.rearrange("(t p) k -> p t k", p=P)).then_inc(raw_in, 16)
            load_x(0)
            sp.dma_start(tokb_b, tok_b.partition_broadcast(P)).then_inc(pos_in[0], 16)
            load_pos(0)
            load_x(1)
            load_pos(1)
            load_x(2)
            load_pos(2)
            for k, v in ((qkv_raw, wqkv), (wo_raw, wout), (wg_sb[:, :, :], wg)):
                sp.dma_start(k, v.rearrange("(k p) n -> p k n", p=P)).then_inc(raw2_in, 16)
            h_seq = h_rows[0:N, :].rearrange("(b s) d -> b s d", s=SEQ)
            sp.dma_start(h_seq[:, 1 + NPATCH:, :], txt).then_inc(txt_out, 16)
            sp.wait_ge(row0_sum, 1)
            sp.dma_start(h_seq[:, 0, :], cls_b).then_inc(cls_out, 16)
            sp.wait_ge(consts, 1)
            sp.dma_start(h_rows[N:, :], zeros[0:NPAD - N, :]).then_inc(pad_out, 16)
            sp.dma_start(out[NPAD:, :], zeros[0:N + P - NPAD, :]).then_inc(pad2_out, 16)

            def store_rows(t, ws):
                sp.wait_ge(tk_row, HP * t + ws.stop)
                for hh in range(2):
                    first = 1 + (2 * t + hh) * HP
                    sp.dma_start(h_seq[:, first + ws.start:first + ws.stop, :],
                                 store[hh * B:(hh + 1) * B, t % 2, ws, :]).then_inc(patch_out[t], 16)

            sp.wait_ge(tk_patch, HP)
            sp.dma_start(w1_raw, w1_of(0)).then_inc(w1_in, 16)
            sp.dma_start(w2_raw, w2_of(0)).then_inc(w2_in, 16)
            sp.dma_start(b2_b[:, 0, :], b2_of(0).partition_broadcast(P)).then_inc(b2_in, 16)
            for t in range(NTX - 1):
                store_rows(t, slice(0, HP))
            for w in range(0, HP, 2):
                store_rows(NTX - 1, slice(w, w + 2))
            for done, n in ((txt_out, 1), (cls_out, 1), (pad_out, 1), (pad2_out, 1),
                            *((v, 2) for v in patch_out[:-1]), (patch_out[-1], HP)):
                sp.wait_ge(done, 16 * n)
            sp.wait_ge(b1_ok, 1)
            sp.wait_ge(qkv_hi, 1)
            sp.wait_ge(qkv_lo, 2)
            sp.wait_ge(pos_sum, NTX)
            h_src = h_rows.rearrange("(i p) d -> p i d", p=P)
            sp.dma_start(h_all[:, 0:2, :], h_src[:, 0:2, :]).then_inc(h_first, 16)
            sp.dma_start(h_all[:, 2:G, :], h_src[:, 2:G, :]).then_inc(h_in, 16)
            sp.wait_ge(h_in, 16)
            with sp.Fori(1, NG) as c:
                sp.dma_start(h_all[:, bass.ds(c * G, G), :], h_src[:, bass.ds(c * G, G), :]).then_inc(h_in, 16)
                sp.wait_ge(h_in, c * 16 + 16)
                apart(sp)
            o_dst = out[0:NPAD, :].rearrange("(i p) d -> p i d", p=P)
            x_dst = x_rows.rearrange("(i p) d -> p i d", p=P)

            def rows_of(c, half):
                sp.wait_ge(b_h2, c * G + G)
                sp.dma_start(o_dst[:, bass.ds(c * G, G), :], h_all[:, bass.ds(c * G, G), :]).then_inc(out_in, 16)
                sp.wait_ge(b_xn, c * G + G)
                sp.dma_start(x_dst[:, bass.ds(c * G, G), 0:D], x2[half]).then_inc(rows_out[half], 16)

            def weights_of(c):
                sp.wait_ge(b_w, c + 1)
                sp.dma_start(x_dst[:, bass.ds(c * G, G), D:XW], w_cols[:, :, :]).then_inc(w_out, 16)

            sp.nop().then_inc(w_out, 1)
            rows_of(0, 0)
            with sp.Fori(0, (NG - 1) // 2) as k:
                rows_of(k * 2 + 1, 1)
                weights_of(k * 2)
                rows_of(k * 2 + 2, 0)
                weights_of(k * 2 + 1)
            weights_of(NG - 1)
            def feed(e, s):
                sp.wait_ge(w1_hi, e)
                sp.wait_ge(w1_lo, e)
                sp.dma_start(w1_raw, w1_of(e)).then_inc(w1_in, 16)
                sp.wait_ge(w2_hi, e)
                sp.wait_ge(w2_lo, e)
                sp.dma_start(w2_raw, w2_of(e)).then_inc(w2_in, 16)
                after(sp, e_y, e * NS - NS)
                apart(sp)
                sp.wait_ge(b2_in, e * 16)
                apart(sp)
                sp.dma_start(b2_b[:, s, :], b2_of(e).partition_broadcast(P)).then_inc(b2_in, 16)

            feed(1, 1)
            with sp.Fori(0, (E - 2) // 2) as k:
                feed(k * 2 + 2, 0)
                feed(k * 2 + 3, 1)

        @block.gpsimd
        def _(pool):
            own = Own(pool, pool_own)
            pool.memset(zeros, 0.0).then_inc(consts, 1)
            own(pool.memset(ident[:, :], 0.0))
            own(pool.affine_select(out=ident[:, :], in_=ident[:, :], compare_op=ALU.not_equal, fill=1.0,
                                   base=0, pattern=[[-1, P]], channel_multiplier=1))
            pool.memset(ones_h[:, :], 1.0)
            pool.memset(zero_h[:, :], 0.0)
            pool.memset(ones_f[:, :], 1.0)
            pool.memset(half[:, :], -0.5)
            pool.memset(minus[:, :], -1.0 / D)
            pool.memset(minus_r[:, :], -1.0 / (D * ROOT_D))
            pool.memset(eps[:, :], EPS)
            own(pool.memset(ones_b[:, :], 1.0))
            own(pool.affine_select(out=upper[:, :], in_=ones_b[:, :], compare_op=ALU.is_gt, fill=0.0,
                                   base=0, pattern=[[1, P]], channel_multiplier=-1))
            pool.iota(lane[:, :], [[1, P]], base=0, channel_multiplier=0, allow_small_or_imprecise_dtypes=True)
            pool.iota(keys[:, :], [[1, KEY]], base=-KEY, channel_multiplier=0, allow_small_or_imprecise_dtypes=True)
            own(pool.iota(slot[:, :].rearrange("p (e j) -> p e j", e=E), [[0, E], [P, NS]], base=0, channel_multiplier=1,
                          allow_small_or_imprecise_dtypes=True))
            pool.iota(tile_no[:, :], [[1, NT]], base=0, channel_multiplier=0, allow_small_or_imprecise_dtypes=True)
            pool.iota(number[:, :], [[1, 1]], base=0, channel_multiplier=1, allow_small_or_imprecise_dtypes=True)
            own(pool.tensor_scalar(in_cap[:, :], slot[:, :], CAP - 0.5, None, ALU.is_lt))
            own(pool.tensor_scalar(slot_r[:, :], slot[:, :], -1.0, CAP - 1.0, ALU.mult, ALU.add))
            pool.iota(trash[:, :], [[1, 1]], base=N, channel_multiplier=1, allow_small_or_imprecise_dtypes=True)
            pool.iota(rev[:, :], [[-1, E]], base=E, channel_multiplier=0,
                      allow_small_or_imprecise_dtypes=True)
            pool.memset(cum[:, :, :], 0.0).then_inc(consts, 1)
            for t in range(NTX):
                pool.wait_ge(pos_in[t], 48 if t == 0 else 32)
                pool.tensor_tensor(pos_b[:, t], pos_b[:, t], tokb_b.unsqueeze(1).to_broadcast([P, HP, D]), ALU.add).then_inc(pos_sum, 1)
                if t == 0:
                    pool.wait_ge(row0_in, 32)
                    pool.tensor_tensor(cls_b, cls_b, pos0_b, ALU.add).then_inc(row0_sum, 1)
            ind_2 = ind.rearrange("p i (r b) -> p i r b", r=2)
            pool.memset(ind, 1.0)
            own(pool.memset(ind_t, 1.0))
            own(pool.affine_select(out=ind_2, in_=ind_2, compare_op=ALU.is_ge, fill=0.0, base=-P,
                                   pattern=[[P, NT + 1], [0, 2], [-SEQ, B]], channel_multiplier=1))
            own(pool.affine_select(out=ind_2, in_=ind_2, compare_op=ALU.is_ge, fill=0.0, base=P + SEQ - 1,
                                   pattern=[[-P, NT + 1], [0, 2], [SEQ, B]], channel_multiplier=-1))
            for s in range(2):
                part = ind_t[s * B:(s + 1) * B, :]
                own(pool.affine_select(out=part, in_=part, compare_op=ALU.is_ge, fill=0.0, base=0,
                                       pattern=[[1, NPAD]], channel_multiplier=-SEQ))
                own(pool.affine_select(out=part, in_=part, compare_op=ALU.is_ge, fill=0.0, base=SEQ - 1,
                                       pattern=[[-1, NPAD]], channel_multiplier=SEQ))
            pool.nop().then_inc(consts, 1)

            def group_scale(c, h, ts=slice(0, G)):
                pool.wait_ge(a_var, c + 2 if ts.stop == G else 1)
                pool.tensor_tensor(rstd_2[:, h, ts], veps[:, ts], half[:, ts], ALU.pow).then_inc(a_rstd, 1)

            def low_kvp(i, s):
                pool.wait_ge(a_kvh, i + 1)
                after(pool, a_acc, i - 1)
                pool.tensor_tensor(kvp_l[:, s, :], kvp[:, s, :], kvp_h[:, s, :], ALU.subtract).then_inc(a_kvl, 1)

            def project(c, half_0):
                for t in range(G):
                    i = c * G + t
                    if t == 2 and there(i + G):
                        group_scale(c + 1, 1 - half_0)
                    if there(i - 1):
                        low_kvp(i - 1, (half_0 + t + 1) % 2)
                    pool.wait_ge(a_v, i + 1)
                    pool.tensor_tensor(rk[:, t:t + 1], nk[:, t:t + 1], half[:, 0:1], ALU.pow).then_inc(a_rk, 1)
                    pool.wait_ge(a_xn, i + 1)
                    apart(pool)
                    pool.tensor_tensor(tile(h_all, i), tile(h_all, i), bout_b[:, :], ALU.add).then_inc(b_hb, 1)

            group_scale(0, 0, slice(0, 2))
            group_scale(0, 0, slice(2, G))
            project(0, 0)
            with pool.Fori(0, (NG - 3) // 2) as k:
                project(k * 2 + 1, 1)
                project(k * 2 + 2, 0)
            project(NG - 2, 1)
            project(NG - 1, 0)
            low_kvp(NT - 1, (NT - 1) % 2)
            pool.wait_ge(a_nqc, 1)
            own(pool.tensor_tensor(rq[:, :], nq[:, :], half[:, :], ALU.pow))
            pool.tensor_scalar(rq[:, :], rq[:, :], 1.0 / SCALE, None, ALU.mult).then_inc(rq_ready, 1)

            def low_qk(i, s):
                pool.wait_ge(b_qhi, i + 1)
                after(pool, b_prod, i - 1)
                pool.tensor_tensor(xl[:, s, :], sq[:, s, :], xh[:, s, :], ALU.subtract).then_inc(b_qlo, 1)

            def attend(c, half_0, base):
                own.step(base)
                for t in range(G):
                    i = c * G + t
                    pool.wait_ge(b_h2, i + 1)
                    pool.tensor_tensor(offset[:, t:t + 1], sums[:, t:t + 1], minus_r[:, :], ALU.mult).then_inc(b_mean, 1)
                    pool.tensor_tensor(nmr[:, t:t + 1], sums[:, t:t + 1], minus[:, :], ALU.mult)
                    if there(i + 2):
                        low_qk(i + 2, (half_0 + t) % 2)
                    pool.wait_ge(b_var, i + 1)
                    own(pool.tensor_tensor(veps[:, t:t + 1], var_2[:, t:t + 1], eps[:, :], ALU.add))
                    own(pool.tensor_tensor(rstd[:, t:t + 1], veps[:, t:t + 1], half[:, 0:1], ALU.pow))
                    pool.tensor_tensor(nmr[:, t:t + 1], nmr[:, t:t + 1], rstd[:, t:t + 1], ALU.mult).then_inc(b_rstd, 1)

            PA = 2 * G
            n1 = own.n
            low_qk(0, 0)
            low_qk(1, 1)
            attend(0, 0, n1)
            with pool.Fori(0, (NG - 3) // 2) as k:
                attend(k * 2 + 1, 1, k * 2 * PA + (n1 + PA))
                attend(k * 2 + 2, 0, k * 2 * PA + (n1 + 2 * PA))
            attend(NG - 2, 1, n1 + (NG - 2) * PA)
            attend(NG - 1, 0, n1 + (NG - 1) * PA)
            n1 += NG * PA

            def pull(e, s):
                apart(pool)
                for j in range(NS):
                    m = min(P, CAP - j * P)
                    pool.indirect_dma_start(out=rows[s][0:m, j, :], out_offset=None, in_=x_rows,
                                            in_offset=bass.IndirectOffsetOnAxis(ap=from_e[0:m, s, j:j + 1], axis=0)
                                            ).then_inc(got[s][j // ST], 16)

            pool.wait_ge(counts_ok, 1)
            own.step(n1)
            for k in range(TOP):
                own(pool.tensor_tensor(t01[:, k, :], t01[:, k, :], in_cap[:, :], ALU.mult))
            own(pool.tensor_tensor(tmp[:, :], t0, t1, ALU.mult))
            own(pool.tensor_tensor(t1, t1, tmp[:, :], ALU.subtract))
            own(pool.tensor_tensor(tmp[:, :], t0, t1, ALU.add))
            own(pool.tensor_tensor(tmp[:, :], tmp[:, :], trash[:, :].to_broadcast([P, KEY]), ALU.mult))
            own(pool.tensor_tensor(spill[:, :], trash[:, :].to_broadcast([P, KEY]), tmp[:, :], ALU.subtract))
            pool.nop().then_inc(masks_ok, 1)
            pool.wait_ge(tables, 1)
            own(pool.tensor_copy(from_e[:, 0, :], from_i[:, 0:NS]))
            pool.wait_ge(rows_out[0], 16 * (NG - NG // 2))
            pool.wait_ge(rows_out[1], 16 * (NG // 2))
            pool.wait_ge(w_out, 16 * NG + 1)
            pull(0, 0)
            pool.wait_ge(tables, 2)
            own(pool.tensor_copy(to_e[:, 0, :], to_i[:, 0:NS]))
            pool.wait_ge(out_in, 16 * NG)
            pool.wait_ge(pad2_out, 16)
            n2 = n1 + own.n

            def expert(e, s, last):
                if not last:
                    after(pool, e_turned, e * NS)
                    after(pool, added, e * NS * 16)
                    pool.tensor_copy(from_e[:, 1 - s, :], from_i[:, bass.ds((e + 1) * NS, NS)])
                    own(pool.tensor_copy(to_e[:, 1 - s, :], to_i[:, bass.ds((e + 1) * NS, NS)]))
                    pull(e + 1, 1 - s)
                for j in range(NS):
                    m = min(P, CAP - j * P)
                    pool.wait_ge(e_y, e * NS + j + 1)
                    after(pool, added, (e * NS + j) * 16)
                    apart(pool)
                    pool.indirect_dma_start(out=out, out_offset=bass.IndirectOffsetOnAxis(ap=to_e[0:m, s, j:j + 1], axis=0),
                                            in_=y_sb[0:m, j % 3, :], in_offset=None, compute_op=ALU.add
                                            ).then_inc(added, 16)

            own.step(n2)
            expert(0, 0, False)
            n3 = n2 + own.n
            with pool.Fori(0, (E - 2) // 2) as k:
                own.step(k * 2 + n3)
                expert(k * 2 + 1, 1, False)
                expert(k * 2 + 2, 0, False)
            expert(E - 1, 1, True)
            pool.wait_ge(added, 16 * NS * E)

        @block.scalar
        def _(act):
            act.dma_start(cls_b, cls[0, 0, :].partition_broadcast(B)).then_inc(row0_in, 16)
            act.dma_start(pos0_b, pos[0, 0, :].partition_broadcast(B)).then_inc(row0_in, 16)
            act.dma_start(bout_b[:, :], bout.partition_broadcast(P)).then_inc(raw2_in, 16)
            act.dma_start(bkv_b, bqkv[D:3 * D].partition_broadcast(P)).then_inc(raw2_in, 16)
            act.dma_start(b1_raw, b1.rearrange("e (m p) -> (e m) p", p=P)).then_inc(raw2_in, 16)
            act.wait_ge(qkv_lo, 1)
            for r in (0, 32):
                act.dma_start(bq_raw[r:r + 1, :], bqkv[0:D].unsqueeze(0)).then_inc(raw2_in, 16)

            def gather_patches(s):
                if s % HP == 0:
                    act.wait_ge(x_in[s // HP], 32)
                if s >= 2:
                    act.wait_ge(tk_turned, 4 + 2 * (s - 1))
                act.activation(patch[:, s % 2, :].rearrange("p (r j) -> p r j", j=PATCH),
                               x_sb[:, s // HP, :, :, s % HP, :].rearrange("p c i j -> p (c i) j"), ACT.Copy).then_inc(tk_patch, 1)

            def high(f):
                act.wait_ge(tk_turned, f + 1)
                step, part = f // 2, f % 2
                src = bank[f % 4][:, 0:3 * P]
                if step < 2:
                    dst = tokw_h[:, 3 * part:3 * part + 3, step * P:(step + 1) * P]
                    act.activation(dst, src.rearrange("p (k n) -> p k n", k=3), ACT.Copy, scale=SCALE).then_inc(tk_hi, 1)
                else:
                    s = step - 2
                    after(act, tk_prod, s - 1)
                    act.activation(pat_h[:, s % 2, part * 3 * P:(part + 1) * 3 * P], src, ACT.Copy).then_inc(tk_hi, 1)
            gather_patches(0)
            gather_patches(1)
            for f in range(8):
                high(f)
                if f >= 5 and f % 2 == 1:
                    gather_patches(f // 2)
            def other_weights():
                act.wait_ge(raw2_in, 16 * 8)
                act.activation(bkv_b, bkv_b, ACT.Copy, scale=SCALE)
                act.activation(qkv_h[:, :, :], qkv_raw, ACT.Copy, scale=SCALE)
                act.activation(wo_h[:, :, :], wo_raw, ACT.Copy, scale=SCALE)
                act.activation(bq_hl[:, :], bq_raw, ACT.Copy, scale=SCALE).then_inc(qkv_hi, 1)

            for f in range(8, NF):
                if f == 2 * NX - 8:
                    other_weights()
                high(f)
                if f % 2 == 1 and f // 2 < NX:
                    gather_patches(f // 2)
            act.wait_ge(b1_turned, 1)
            act.activation(b1_cols[:, :], bank[0][:, 0:E * NM], ACT.Copy).then_inc(b1_ok, 1)

            def split_w1(e, s):
                act.wait_ge(w1_in, e * 16 + 16)
                act.activation(w1h[s], w1_raw, ACT.Copy, scale=SCALE).then_inc(w1_hi, 1)

            def split_w2(e, s):
                act.wait_ge(w2_in, e * 16 + 16)
                act.activation(w2h[s], w2_raw, ACT.Copy, scale=SCALE).then_inc(w2_hi, 1)

            split_w1(0, 0)
            split_w2(0, 0)

            def high_x(i, s):
                act.wait_ge(a_turned, i + 1)
                after(act, a_q, i - 1)
                act.activation(xh[:, s, :], bank[s][:, 0:D], ACT.Copy).then_inc(a_hi, 1)

            def project(c, half_0):
                for t in range(G):
                    i = c * G + t
                    s = (half_0 + t) % 2
                    if there(i + 1):
                        high_x(i + 1, 1 - s)
                    if there(i - 1):
                        high_kvp(i - 1, 1 - s)
                    act.wait_ge(a_kvb, i + 1)
                    act.activation(junk[:, s, :], kvb[s][:, 0:D], ACT.Square, accum_out=nk[:, t:t + 1]).then_inc(a_v, 1)
                    act.wait_ge(a_q, i + 1)
                    after(act, a_nq, i - 1)
                    apart(act)
                    act.activation(tile(q_all, i), bank[2 + s][:, 0:D], ACT.Copy)
                    act.activation(sq[:, s, :], bank[2 + s][:, 0:D], ACT.Square).then_inc(a_qsq, 1)

            def high_kvp(i, s):
                act.wait_ge(a_kvp, i + 1)
                after(act, a_acc, i - 1)
                act.activation(kvp_h[:, s, :], kvp[:, s, :], ACT.Copy).then_inc(a_kvh, 1)

            high_x(0, 0)
            project(0, 0)
            with act.Fori(0, (NG - 3) // 2) as k:
                project(k * 2 + 1, 1)
                project(k * 2 + 2, 0)
            project(NG - 2, 1)
            project(NG - 1, 0)
            high_kvp(NT - 1, (NT - 1) % 2)
            act.wait_ge(a_acc, NT)
            act.activation(kv_hl[:, :], bank[6][:, 0:D], ACT.Copy, scale=1.0 / SCALE).then_inc(kv_hi, 1)

            def high_qk(i, s):
                act.wait_ge(b_qk, i + 1)
                after(act, b_prod, i - 1)
                act.activation(xh[:, s, :], sq[:, s, :], ACT.Copy).then_inc(b_qhi, 1)

            def times_token(c, ts):
                for t in ts:
                    i = c * G + t
                    act.wait_ge(b_hot, i + 1)
                    apart(act)
                    two = slice(t * TOP, (t + 1) * TOP)
                    act.activation(hot_token[:, two, 0, :], hot_key[:, two, :], ACT.Copy,
                                   scale=tile_no[:, i:i + 1] if isinstance(i, int) else tile_no[:, bass.ds(i, 1)])
                    act.activation(hot_token[:, two, 1, :], hot_key[:, two, :], ACT.Copy,
                                   scale=number[:, :]).then_inc(b_key, 1)

            def attend(c, half_0, pairs):
                for t in range(G):
                    i = c * G + t
                    s = (half_0 + t) % 2
                    if t >= 3 and group_there(c - 2):
                        times_token(c - 2, (0, 1) if t == 3 else (2, 3, 4))
                    if there(i + 2):
                        high_qk(i + 2, s)
                    if t == 3 and group_there(c - 1):
                        act.wait_ge(b_logit, c * G)
                        after(act, b_ex_in, c - 1)
                        act.activation(lg[:, :, :], bank[6][:, 0:G * E].rearrange("p (t e) -> p t e", e=E), ACT.Copy).then_inc(b_lg, 1)
                    if there(i):
                        act.wait_ge(b_mean, i + 1)
                        apart(act)
                        act.activation(junk[:, s, :], tile(h_all, i), ACT.Square, bias=offset[:, t:t + 1], scale=1.0 / ROOT_D,
                                       accum_out=var_2[:, t:t + 1]).then_inc(b_var, 1)
                    if there(i - 1):
                        act.wait_ge(b_rstd, i)
                        if t == 1:
                            after(act, rows_out[half_0], pairs * 16)
                        apart(act)
                        u = (t - 1) % G
                        act.activation(x2[half_0 if t > 0 else 1 - half_0][:, u, :], tile(h_all, i - 1), ACT.Identity,
                                       bias=nmr[:, u:u + 1], scale=rstd[:, u:u + 1]).then_inc(b_xn, 1)
                    if there(i - 2):
                        act.wait_ge(b_turned, i - 1)
                        after(act, b_logit, i - 3)
                        act.activation(xn[:, s, :], bank[4][:, 0:D], ACT.Copy).then_inc(b_xt, 1)
                    if t == 1 and group_there(c - 2):
                        act.wait_ge(b_ex_in, c - 1)
                        act.activation(ex[:, :, :], ex[:, :, :], ACT.Exp).then_inc(b_ex, 1)

            high_qk(0, 0)
            high_qk(1, 1)
            attend(0, 0, 0)
            attend(1, 1, 0)
            with act.Fori(1, (NG - 1) // 2) as k:
                attend(k * 2, 0, k)
                attend(k * 2 + 1, 1, k)
            for c in range(NG - 1, NG + 2):
                attend(c, c % 2, c // 2)

            act.activation(junk[:, 0, 0:1], ones_f[:, :], ACT.Gelu)

            def expert(e, s, last):
                for g in range(CH):
                    w = min(ST * P, CAP - g * ST * P)
                    u = e * CH + g
                    v = (s + g) % 2
                    for j in range(ST):
                        m = min(P, w - j * P)
                        k = u * ST + j
                        act.wait_ge(e_turned, k + 1)
                        if j == 0:
                            after(act, e_up, (u - 1) * NM)
                        act.activation(xt_h[:, v, :, j * P:j * P + m],
                                       bank[(s + g * ST + j) % 2][:, 0:D].rearrange("p (k n) -> p k n", k=ND)[:, :, 0:m],
                                       ACT.Copy).then_inc(e_xhi, 1)
                        if j == 1 and g == 1 and not last:
                            split_w1(e + 1, 1 - s)
                        if j == 1 and g == 2 and not last:
                            after(act, e_down, e * NS)
                            split_w2(e + 1, 1 - s)
                    for m in range(NM):
                        k = u * NM + m
                        act.wait_ge(e_up, k + 1)
                        after(act, e_hlo, k - 1)
                        apart(act)
                        bcol = b1_cols[:, m:m + 1] if isinstance(e, int) and e == 0 else b1_cols[:, bass.ds(e * NM + m, 1)]
                        act.activation(hf[:, m % 2, 0:w], bank[2 + m % 4 if m % 4 < 3 else 7][:, 0:w], ACT.Gelu,
                                       bias=bcol, scale=1.0 / SCALE).then_inc(e_gelu, 1)

            expert(0, 0, False)
            with act.Fori(0, (E - 2) // 2) as k:
                expert(k * 2 + 1, 1, False)
                expert(k * 2 + 2, 0, False)
            expert(E - 1, 1, True)

        @block.vector
        def _(dve):
            own = Own(dve, dve_own)
            own(dve.memset(bq_raw, 0.0))
            dve.nop().then_inc(qkv_lo, 1)

            def low(f):
                act_done = f + 1
                dve.wait_ge(tk_hi, act_done)
                step, part = f // 2, f % 2
                src = bank[f % 4][:, 0:3 * P]
                if step < 2:
                    o = tokw_l[:, 3 * part:3 * part + 3, step * P:(step + 1) * P]
                    i1 = tokw_h[:, 3 * part:3 * part + 3, step * P:(step + 1) * P]
                    dve.scalar_tensor_tensor(o, src.rearrange("p (k n) -> p k n", k=3), SCALE, i1,
                                             ALU.mult, ALU.subtract).then_inc(tk_lo, 1)
                else:
                    s = step - 2
                    after(dve, tk_prod, s - 1)
                    cut = slice(part * 3 * P, (part + 1) * 3 * P)
                    dve.tensor_tensor(pat_l[:, s % 2, cut], src, pat_h[:, s % 2, cut], ALU.subtract).then_inc(tk_lo, 1)

            def row(s):
                t, w = s // HP, s % HP
                dve.wait_ge(tk_prod, s + 1)
                if w == 0:
                    dve.wait_ge(pos_sum, t + 1)
                if t == 2 and w == 0:
                    dve.wait_ge(patch_out[0], 32)
                dve.scalar_tensor_tensor(store[:, t % 2, w, :], bank[4 + s % 2][:, 0:D], 1.0 / SCALE, pos_b[:, t, w, :],
                                         ALU.mult, ALU.add).then_inc(tk_row, 1)

            for f in range(8):
                low(f)
            for s in range(NX):
                if s == NX - 6:
                    dve.wait_ge(qkv_hi, 1)
                    dve.scalar_tensor_tensor(qkv_l[:, :, :], qkv_raw, SCALE, qkv_h[:, :, :], ALU.mult, ALU.subtract)
                if s == NX - 5:
                    dve.scalar_tensor_tensor(wo_l[:, :, :], wo_raw, SCALE, wo_h[:, :, :], ALU.mult, ALU.subtract)
                    dve.scalar_tensor_tensor(bq_hl[32:33, :], bq_raw[32:33, :], SCALE, bq_hl[32:33, :],
                                             ALU.mult, ALU.subtract).then_inc(qkv_lo, 1)
                if s + 2 < NX:
                    low(2 * (s + 2) + 4)
                    low(2 * (s + 2) + 5)
                row(s)

            def split_w1(e, s):
                dve.wait_ge(w1_hi, e + 1)
                dve.scalar_tensor_tensor(w1l[s], w1_raw, SCALE, w1h[s], ALU.mult, ALU.subtract).then_inc(w1_lo, 1)

            def split_w2(e, s):
                dve.wait_ge(w2_hi, e + 1)
                dve.scalar_tensor_tensor(w2l[s], w2_raw, SCALE, w2h[s], ALU.mult, ALU.subtract).then_inc(w2_lo, 1)

            split_w1(0, 0)
            split_w2(0, 0)

            def statistics(c, ts):
                if ts[0] == 0:
                    dve.wait_ge(h_in, c * 16 + 16)
                    apart(dve)
                for t in ts:
                    last = dve.bn_stats(stats[:, t, :], tile(h_all, c * G + t))
                return last

            def variance(last, h, ts=slice(0, G)):
                own(last)
                apart(dve)
                for t in range(ts.start, ts.stop):
                    last = dve.bn_aggr(mv_2[:, h, t, :], stats[:, t, :])
                own(last)
                dve.tensor_scalar(veps[:, ts], mv_2[:, h, ts, 1], EPS, None, ALU.add).then_inc(a_var, 1)

            def normal(i, t, s, h):
                after(dve, a_turned, i - 1)
                dve.tensor_scalar(xn[:, s, :], tile(h_all, i), mv_2[:, h, t, 0:1], rstd_2[:, h, t:t + 1],
                                  ALU.subtract, ALU.mult).then_inc(a_xn, 1)

            def low_x(i, s):
                dve.wait_ge(a_hi, i + 1)
                after(dve, a_q, i - 1)
                dve.tensor_tensor(xl[:, s, :], bank[s][:, 0:D], xh[:, s, :], ALU.subtract).then_inc(a_lo, 1)

            def project(c, half_0, base):
                own.step(base)
                for t in range(G):
                    i = c * G + t
                    s = (half_0 + t) % 2
                    if there(i + 2):
                        if isinstance(i, int) and i == 0:
                            dve.wait_ge(a_rstd, 2)
                        if t == 3:
                            dve.wait_ge(a_rstd, c + 3)
                        normal(i + 2, (t + 2) % G, s, half_0 if t < 3 else 1 - half_0)
                    if there(i + 1):
                        low_x(i + 1, 1 - s)
                    if there(i - 1):
                        product(i - 1, (t - 1) % G, 1 - s)
                    dve.wait_ge(a_kv, i + 1)
                    after(dve, a_kvp, i - 1)
                    dve.tensor_tensor(kvb[s], bank[4 + s][:, 0:2 * D], bkv_b, ALU.add).then_inc(a_kvb, 1)
                    if t < 2 and there(i + G):
                        last = statistics(c + 1, ((0, 1), (2, 3, 4))[t])
                        if t == 1:
                            variance(last, 1 - half_0)

            def product(i, t, s):
                dve.wait_ge(a_rk, i + 1)
                after(dve, a_kvl, i - 1)
                dve.scalar_tensor_tensor(kvp[:, s, :], kvb[s][:, 0:D], rk[:, t:t + 1], kvb[s][:, D:2 * D],
                                         ALU.mult, ALU.mult).then_inc(a_kvp, 1)

            dve.wait_ge(h_first, 16)
            for t in range(2):
                last = dve.bn_stats(stats[:, t, :], tile(h_all, t))
            variance(last, 0, slice(0, 2))
            dve.wait_ge(a_rstd, 1)
            normal(0, 0, 0, 0)
            normal(1, 1, 1, 0)
            dve.wait_ge(h_in, 16)
            variance(statistics(0, (2, 3, 4)), 0, slice(2, G))
            low_x(0, 0)
            n0 = own.n
            PP = 2
            project(0, 0, n0)
            with dve.Fori(0, (NG - 3) // 2) as k:
                project(k * 2 + 1, 1, k * 2 * PP + (n0 + PP))
                project(k * 2 + 2, 0, k * 2 * PP + (n0 + 2 * PP))
            project(NG - 2, 1, n0 + (NG - 2) * PP)
            project(NG - 1, 0, n0 + (NG - 1) * PP)
            product(NT - 1, G - 1, (NT - 1) % 2)
            dve.wait_ge(a_nq, NT)
            dve.tensor_copy(nq[:, :], bank[7][:, 0:NT]).then_inc(a_nqc, 1)
            n1 = n0 + (NG - 1) * PP
            dve.wait_ge(kv_hi, 1)
            dve.scalar_tensor_tensor(kv_hl[B:2 * B, :], bank[6][B:2 * B, 0:D], 1.0 / SCALE, kv_hl[B:2 * B, :],
                                     ALU.mult, ALU.subtract).then_inc(kv_ready, 1)
            dve.wait_ge(rq_ready, 1)

            def multiply_qk(i, s):
                dve.wait_ge(b_kvb, i + 1)
                after(dve, b_qlo, i - 1)
                dve.tensor_tensor(sq[:, s, :], bank[s][:, 0:D], tile(q_all, i), ALU.mult).then_inc(b_qk, 1)

            def attend(c, half_0, base):
                own.step(base)
                for t in range(G):
                    i = c * G + t
                    s = (half_0 + t) % 2
                    if there(i):
                        dve.wait_ge(b_prod, i + 1)
                        dve.scalar_tensor_tensor(tile(h_all, i), bank[2 + s][:, 0:D],
                                                 rq[:, i:i + 1] if isinstance(i, int) else rq[:, bass.ds(i, 1)],
                                                 tile(h_all, i), ALU.mult, ALU.add,
                                                 accum_out=sums[:, t:t + 1]).then_inc(b_h2, 1)
                    if there(i + 2):
                        multiply_qk(i + 2, s)
                    if t == 3 and group_there(c - 1):
                        first_choice(c - 1)
                    if t == 4 and group_there(c - 1):
                        second_choice(c - 1)
                    if t == 0 and group_there(c - 2):
                        count_choices(c - 2)
                    if t == 1 and group_there(c - 2):
                        places(c - 2)
                    if t == 2 and group_there(c - 2):
                        gate_weights(c - 2)

            def one_hots(n, c):
                if not group_there(c):
                    return
                t = n // 2
                if n == 0:
                    dve.wait_ge(b_inv, c * G + 1)
                two = slice(t * TOP, (t + 1) * TOP)
                if n % 2 == 0:
                    dve.tensor_tensor(hot_lo[:, two, :], lane[:, :].unsqueeze(1).to_broadcast([P, TOP, P]),
                                      lo_f[:, t, :].unsqueeze(2).to_broadcast([P, TOP, P]), ALU.is_equal)
                else:
                    dve.tensor_tensor(hot_key[:, two, :], keys[:, :].unsqueeze(1).to_broadcast([P, TOP, KEY]),
                                      key[:, t, :].unsqueeze(2).to_broadcast([P, TOP, KEY]), ALU.is_equal).then_inc(b_hot, 1)

            def own_and(instruction, n, c):
                own.mark(instruction)
                one_hots(n, c)
                own.wait()

            def is_last(c):
                return isinstance(c, int) and c == NG - 1

            def first_choice(c):
                dve.wait_ge(b_lg, c + 1)
                own_and(dve.tensor_reduce(m12[:, :, 0:1], lg[:, :, :], AX, ALU.max), 5, c - 1)
                own_and(dve.tensor_tensor(same[:, :, :], lg[:, :, :], m12[:, :, 0:1].to_broadcast([P, G, E]), ALU.is_equal), 6, c - 1)
                own_and(dve.tensor_tensor(same[:, :, :], same[:, :, :], rev[:, :].unsqueeze(1).to_broadcast([P, G, E]), ALU.mult), 7, c - 1)
                own_and(dve.tensor_reduce(er[:, :, 0:1], same[:, :, :], AX, ALU.max), 8, c - 1)
                own_and(dve.tensor_tensor(pick[:, :, 0:E], same[:, :, :], er[:, :, 0:1].to_broadcast([P, G, E]), ALU.is_equal), 9, c - 1)

            def second_choice(c):
                own(dve.scalar_tensor_tensor(lg2[:, :, :], pick[:, :, 0:E], -BIG, lg[:, :, :], ALU.mult, ALU.add))
                own(dve.tensor_reduce(m12[:, :, 1:2], lg2[:, :, :], AX, ALU.max))
                own(dve.tensor_tensor(same[:, :, :], lg2[:, :, :], m12[:, :, 1:2].to_broadcast([P, G, E]), ALU.is_equal))
                own(dve.tensor_tensor(same[:, :, :], same[:, :, :], rev[:, :].unsqueeze(1).to_broadcast([P, G, E]), ALU.mult))
                own(dve.tensor_reduce(er[:, :, 1:2], same[:, :, :], AX, ALU.max))
                own(dve.tensor_tensor(pick[:, :, E:2 * E], same[:, :, :], er[:, :, 1:2].to_broadcast([P, G, E]), ALU.is_equal))

            def count_choices(c):
                if is_last(c):
                    own(dve.memset(pick[LAST:P, G - 1, :], 0.0))
                own.mark(dve.tensor_copy(cum[:, 0, :], cum[:, G, :]))
                dve.tensor_tensor(ex[:, :, 0:E], lg[:, :, :], m12[:, :, 0:1].to_broadcast([P, G, E]), ALU.subtract)
                own.wait()
                for t in range(G):
                    add = dve.tensor_tensor(cum[:, t + 1, :], cum[:, t, :], pick[:, t, :], ALU.add)
                    if t == 0:
                        own.mark(add)
                        dve.tensor_tensor(ex[:, :, E:E + 1], m12[:, :, 1:2], m12[:, :, 0:1], ALU.subtract).then_inc(b_ex_in, 1)
                        own.wait()
                    elif t + 1 < G:
                        own(add)
                add.then_inc(b_pick, 1)

            def places(c):
                dve.wait_ge(b_rank, c + 1)
                if is_last(c):
                    dve.wait_ge(counted, 1)
                own(dve.tensor_tensor(pm[:, :, :], bank[5][:, 0:G * TOP * E].rearrange("p (t k) -> p t k", t=G),
                                      pick[:, :, :], ALU.mult))
                own(dve.tensor_reduce(posn[:, :, :], pm[:, :, :].rearrange("p t (k e) -> p t k e", k=TOP), AX, ALU.add))
                if is_last(c):
                    for k, number_of in ((0, slot), (1, slot_r)):
                        of = bank[5][:, (G * TOP + k) * E:(G * TOP + k + 1) * E]
                        last = dve.tensor_tensor(t01[:, k, :].rearrange("p (e j) -> p e j", e=E),
                                                 number_of[:, :].rearrange("p (e j) -> p e j", e=E),
                                                 of.unsqueeze(2).to_broadcast([P, E, NS]), ALU.is_lt)
                    last.then_inc(counts_ok, 1)
                own(dve.tensor_scalar(posn[:, :, 1:2], posn[:, :, 1:2], -1.0, CAP - 1.0, ALU.mult, ALU.add))
                dve.tensor_scalar(hi_i[:, :, :], posn[:, :, :], -(P - 1) / 2, 1.0 / P, ALU.add, ALU.mult)
                own(dve.tensor_scalar(bad[:, :, :], posn[:, :, :], CAP - 0.5, None, ALU.is_gt))
                dve.scalar_tensor_tensor(lo_f[:, :, :], hi_i[:, :, :], -float(P), posn[:, :, :], ALU.mult, ALU.add)
                own(dve.scalar_tensor_tensor(key[:, :, :], er[:, :, :], -float(NS), hi_i[:, :, :], ALU.mult, ALU.add))
                own(dve.scalar_tensor_tensor(bad[:, :, :], posn[:, :, :], -0.5, bad[:, :, :], ALU.is_lt, ALU.add))
                own(dve.scalar_tensor_tensor(key[:, :, :], bad[:, :, :], NOWHERE, key[:, :, :], ALU.mult, ALU.add))
                if is_last(c):
                    own(dve.memset(key[LAST:P, G - 1, :], NOWHERE))

            def gate_weights(c):
                dve.wait_ge(b_ex, c + 1)
                own_and(dve.tensor_reduce(ssum[:, :], ex[:, :, 0:E], AX, ALU.add), 0, c)
                own_and(dve.reciprocal(gp[:, :, 0], ssum[:, :]), 1, c)
                own_and(dve.tensor_tensor(gp[:, :, 1], gp[:, :, 0], ex[:, :, E], ALU.mult), 2, c)
                own_and(dve.tensor_tensor(gt[:, :], gp[:, :, 0], gp[:, :, 1], ALU.add), 3, c)
                own_and(dve.tensor_scalar(gt[:, :], gt[:, :], GATE_EPS, None, ALU.max), 4, c)
                own(dve.reciprocal(gt[:, :], gt[:, :]))
                dve.wait_ge(w_out, c * 16 + 1)
                dve.tensor_tensor(w_cols[:, :, :], gp[:, :, :], gt[:, :].unsqueeze(2).to_broadcast([P, G, TOP]), ALU.mult).then_inc(b_w, 1)

            dve.wait_ge(b_hb, NT)
            multiply_qk(0, 0)
            multiply_qk(1, 1)
            n2 = n1 + own.n
            attend(0, 0, n2)
            n2 += own.n
            attend(1, 1, n2)
            n2 += own.n
            AG = 29
            with dve.Fori(1, (NG - 1) // 2) as k:
                attend(k * 2, 0, (k - 1) * 2 * AG + n2)
                assert own.n == AG, own.n
                attend(k * 2 + 1, 1, (k - 1) * 2 * AG + (n2 + AG))
            n3 = n2 + (NG - 3) * AG
            for c in range(NG - 1, NG + 2):
                attend(c, c % 2, n3)
                n3 += own.n
            own.step(n3)
            for n in range(5, 2 * G):
                one_hots(n, NG - 1)

            dve.wait_ge(b_inv, NG * G + 1)
            own(dve.tensor_scalar(tok2[:, :, :], bank[7][:, 0:2 * TOP * KEY].rearrange("p (c a k) -> p c a k", c=TOP, a=2)[:, :, 0, :],
                                  float(P), None, ALU.mult))
            own(dve.tensor_tensor(tok2[:, :, :], bank[7][:, 0:2 * TOP * KEY].rearrange("p (c a k) -> p c a k", c=TOP, a=2)[:, :, 1, :],
                                  tok2[:, :, :], ALU.add))
            dve.wait_ge(masks_ok, 1)
            own(dve.tensor_tensor(tok2[:, :, :], tok2[:, :, :], t01[:, :, :], ALU.mult))
            own(dve.tensor_tensor(ids[:, :], tok2[:, 0, :], tok2[:, 1, :], ALU.add))
            dve.tensor_copy(from_i[:, :], ids[:, :]).then_inc(tables, 1)
            own(dve.tensor_tensor(ids[:, :], ids[:, :], spill[:, :], ALU.add))
            dve.tensor_copy(to_i[:, :], ids[:, :]).then_inc(tables, 1)
            n4 = own.base + own.n

            def split_rows(e, s, g, js):
                u, v = e * CH + g, (s + g) % 2
                for j in js:
                    m = min(P, CAP - (g * ST + j) * P)
                    dve.wait_ge(e_xhi, u * ST + j + 1)
                    if j == 0:
                        after(dve, e_up, (u - 1) * NM)
                    dve.tensor_tensor(xt_l[:, v, :, j * P:j * P + m],
                                      bank[(s + g * ST + j) % 2][:, 0:D].rearrange("p (k n) -> p k n", k=ND)[:, :, 0:m],
                                      xt_h[:, v, :, j * P:j * P + m], ALU.subtract).then_inc(e_xlo, 1)

            def expert(e, s, last, base):
                own.step(base)
                for g in range(CH):
                    w = min(ST * P, CAP - g * ST * P)
                    u = e * CH + g
                    v = (s + g) % 2
                    nxt = (e, s, g + 1) if g + 1 < CH else None if last else (e + 1, 1 - s, 0)
                    for m in range(NM):
                        k = u * NM + m
                        dve.wait_ge(e_gelu, k + 1)
                        if m == 0:
                            after(dve, e_down, (u - 1) * ST)
                        dve.tensor_copy(hid_h[v][:, m, 0:w], hf[:, m % 2, 0:w]).then_inc(e_hhi, 1)
                        dve.wait_ge(e_hhi, k + 1)
                        dve.tensor_tensor(hid_l[v][:, m, 0:w], hf[:, m % 2, 0:w], hid_h[v][:, m, 0:w],
                                          ALU.subtract).then_inc(e_hlo, 1)
                    if nxt:
                        split_rows(*nxt, (0, 1))
                    if g == 0:
                        def cols(tab):
                            return tab[:, e * NS:(e + 1) * NS] if isinstance(e, int) else tab[:, bass.ds(e * NS, NS)]
                        for gg in range(CH):
                            dve.wait_ge(got[s][gg], gathered(e, s))
                        own(dve.tensor_tensor(ws[:, s, :], rows[s][:, :, D], cols(t0), ALU.mult))
                        own(dve.tensor_tensor(wtmp[:, s, :], rows[s][:, :, D + 1], cols(t1), ALU.mult))
                        own(dve.tensor_tensor(ws[:, s, :], ws[:, s, :], wtmp[:, s, :], ALU.add))
                        own(dve.tensor_scalar(wtmp[:, s, :], ws[:, s, :], 1.0 / SCALE, None, ALU.mult))
                        dve.wait_ge(b2_in, e * 16 + 16)
                    for j in range(ST):
                        jj = g * ST + j
                        m = min(P, w - j * P)
                        k = u * ST + j
                        own(dve.tensor_scalar(b2w[0:m, jj % 2, :], b2_b[0:m, s, :], ws[0:m, s, jj:jj + 1], None, ALU.mult))
                        dve.wait_ge(e_down, k + 1)
                        after(dve, added, (k - 2) * 16)
                        dve.scalar_tensor_tensor(y_sb[0:m, jj % 3, :], bank[5 + (s + jj) % 2][0:m, 0:D],
                                                 wtmp[0:m, s, jj:jj + 1], b2w[0:m, jj % 2, :],
                                                 ALU.mult, ALU.add).then_inc(e_y, 1)
                        if j == 0 and nxt:
                            split_rows(*nxt, (2,))
                        if j == 0 and g == 0 and not last:
                            split_w1(e + 1, 1 - s)
                        if j == 0 and g == 1 and not last:
                            split_w2(e + 1, 1 - s)

            EO = 4 + NS
            split_rows(0, 0, 0, range(ST))
            expert(0, 0, False, n4)
            assert own.n == EO
            with dve.Fori(0, (E - 2) // 2) as k:
                expert(k * 2 + 1, 1, False, k * 2 * EO + (n4 + EO))
                expert(k * 2 + 2, 0, False, k * 2 * EO + (n4 + 2 * EO))
            expert(E - 1, 1, True, n4 + (E - 1) * EO)

        @block.tensor
        def _(pe):
            def three(dst, lh, ll, rh, rl, start, stop):
                pe.matmul(dst, lh, rh, start=start, stop=False)
                pe.matmul(dst, lh, rl, start=False, stop=False)
                return pe.matmul(dst, ll, rh, start=False, stop=stop)

            def add_zeros(dst, n, start):
                return pe.matmul(dst, zero_h[:, 0:P], zero_h[:, 0:n], start=start, stop=not start, skip_group_check=True)

            pe.wait_ge(consts, 2)
            pe.wait_ge(raw_in, 16)

            def turn(f):
                step, part = f // 2, f % 2
                if f >= 4:
                    pe.wait_ge(tk_lo, f - 3)
                for k in range(3):
                    kt = 3 * part + k
                    if step < 2:
                        src = tokw_raw[:, step, kt * P:(kt + 1) * P]
                    else:
                        s = step - 2
                        if k == 0:
                            pe.wait_ge(tk_patch, s + 1)
                        src = patch[:, s % 2, kt * P:(kt + 1) * P]
                    last = pe.transpose(bank[f % 4][:, k * P:(k + 1) * P], src, ident[:, :])
                last.then_inc(tk_turned, 1)

            for f in range(4):
                turn(f)
            turn(4)
            turn(5)
            pe.wait_ge(tk_lo, 4)
            for s in range(NX):
                if s + 1 < NX:
                    turn(2 * (s + 1) + 4)
                    turn(2 * (s + 1) + 5)
                pe.wait_ge(tk_lo, 2 * s + 6)
                if s >= 2:
                    pe.wait_ge(tk_row, s - 1)
                for kt in range(NKT):
                    cut = slice(kt * P, (kt + 1) * P)
                    last = three(bank[4 + s % 2][:, 0:D], pat_h[:, s % 2, cut], pat_l[:, s % 2, cut],
                                 tokw_h[:, kt, :], tokw_l[:, kt, :], kt == 0, kt == NKT - 1)
                last.then_inc(tk_prod, 1)
            pe.wait_ge(raw2_in, 16 * 8)
            pe.transpose(bank[0][:, 0:E * NM], b1_raw, ident[0:E * NM, 0:E * NM]).then_inc(b1_turned, 1)
            pe.wait_ge(b1_ok, 1)
            pe.wait_ge(tk_row, NX)
            pe.wait_ge(qkv_lo, 2)
            pe.wait_ge(consts, 3)

            def turn_x(i, s):
                pe.wait_ge(a_xn, i + 1)
                after(pe, a_lo, i - 1)
                for k in range(ND):
                    last = pe.transpose(bank[s][:, k * P:(k + 1) * P], xn[:, s, k * P:(k + 1) * P], ident[:, :])
                last.then_inc(a_turned, 1)

            def sum_q(i, s):
                pe.wait_ge(a_qsq, i + 1)
                dst = bank[7][:, i:i + 1] if isinstance(i, int) else bank[7][:, bass.ds(i, 1)]
                for k in range(ND):
                    last = pe.matmul(dst, sq[:, s, k * P:(k + 1) * P], ones_f[:, :], start=k == 0, stop=k == ND - 1)
                last.then_inc(a_nq, 1)

            def sum_kv(i, s):
                pe.wait_ge(a_kvl, i + 1)
                lhs = ind[:, i + 1, :] if isinstance(i, int) else ind[:, bass.ds(i + 1, 1), :].rearrange("p a b -> p (a b)")
                first, final = isinstance(i, int) and i == 0, isinstance(i, int) and i == NT - 1
                pe.matmul(bank[6][:, 0:D], lhs, kvp_h[:, s, :], start=first, stop=False)
                pe.matmul(bank[6][:, 0:D], lhs, kvp_l[:, s, :], start=False, stop=final).then_inc(a_acc, 1)

            def project(c, half_0):
                for t in range(G):
                    i = c * G + t
                    s = (half_0 + t) % 2
                    pe.wait_ge(a_lo, i + 1)
                    after(pe, a_kvb, i - 1)
                    dst = bank[4 + s][:, 0:2 * D]
                    for k in range(ND):
                        cut = slice(k * P, (k + 1) * P)
                        last = three(dst, xh[:, s, cut], xl[:, s, cut], qkv_h[:, k, D:3 * D], qkv_l[:, k, D:3 * D],
                                     k == 0, k == ND - 1)
                    last.then_inc(a_kv, 1)
                    after(pe, a_qsq, i - 1)
                    for dh in range(ND):
                        dst = bank[2 + s][:, dh * P:(dh + 1) * P]
                        pe.matmul(dst, bq_hl[:, dh * P:(dh + 1) * P], ones_h[:, :], start=True, stop=False)
                        for k in range(ND):
                            cut = slice(k * P, (k + 1) * P)
                            last = three(dst, qkv_h[:, k, dh * P:(dh + 1) * P], qkv_l[:, k, dh * P:(dh + 1) * P],
                                         xh[:, s, cut], xl[:, s, cut], False, k == ND - 1)
                    last.then_inc(a_q, 1)
                    if there(i + 2):
                        turn_x(i + 2, s)
                    if there(i - 1):
                        sum_q(i - 1, 1 - s)
                    if there(i - 2):
                        sum_kv(i - 2, s)

            turn_x(0, 0)
            turn_x(1, 1)
            project(0, 0)
            with pe.Fori(0, (NG - 3) // 2) as k:
                project(k * 2 + 1, 1)
                project(k * 2 + 2, 0)
            project(NG - 2, 1)
            project(NG - 1, 0)
            sum_q(NT - 1, (NT - 1) % 2)
            sum_kv(NT - 2, NT % 2)
            sum_kv(NT - 1, (NT - 1) % 2)
            pe.wait_ge(a_nqc, 1)
            pe.wait_ge(kv_ready, 1)

            def spread(i, s):
                after(pe, b_qk, i - 1)
                rhs = ind_t[:, i * P:(i + 1) * P] if isinstance(i, int) else ind_t[:, bass.ds(i * P, P)]
                for k in range(ND):
                    last = pe.matmul(bank[s][:, k * P:(k + 1) * P], kv_hl[:, k * P:(k + 1) * P], rhs,
                                     start=True, stop=True)
                last.then_inc(b_kvb, 1)

            def ranks(c):
                pe.wait_ge(b_pick, c + 1)
                dst = bank[5][:, 0:G * TOP * E]
                pe.matmul(dst, upper[:, :], pick[:, :, :].rearrange("p t k -> p (t k)"), start=True, stop=False)
                pe.matmul(dst, ones_b[:, :], cum[:, 0:G, :].rearrange("p t k -> p (t k)"),
                          start=False, stop=True).then_inc(b_rank, 1)
                if isinstance(c, int) and c == NG - 1:
                    pe.matmul(bank[5][:, G * TOP * E:(G + 1) * TOP * E], ones_b[:, :], cum[:, G, :],
                              start=True, stop=True).then_inc(counted, 1)

            def invert(c, ts):
                for t in ts:
                    pe.wait_ge(b_key, c * G + t + 1)
                    for n in range(t * TOP, (t + 1) * TOP):
                        k = n % TOP
                        last = pe.matmul(bank[7][:, 2 * k * KEY:2 * (k + 1) * KEY], hot_lo[:, n, :],
                                         hot_token[:, n, :, :].rearrange("p a k -> p (a k)"),
                                         start=False, stop=False, skip_group_check=True)
                    if isinstance(c, int) and c == NG - 1 and t == G - 1:
                        last = add_zeros(bank[7][:, 0:2 * TOP * KEY], 2 * TOP * KEY, False)
                    last.then_inc(b_inv, 1)

            def attend(c, half_0):
                for t in range(G):
                    i = c * G + t
                    s = (half_0 + t) % 2
                    if there(i + 2):
                        spread(i + 2, s)
                    if there(i):
                        pe.wait_ge(b_qlo, i + 1)
                        after(pe, b_h2, i - 1)
                        for k in range(ND):
                            cut = slice(k * P, (k + 1) * P)
                            last = three(bank[2 + s][:, 0:D], xh[:, s, cut], xl[:, s, cut], wo_h[:, k, :], wo_l[:, k, :],
                                         k == 0, k == ND - 1)
                        last.then_inc(b_prod, 1)
                    if t == 1 and group_there(c - 2):
                        ranks(c - 2)
                    if there(i - 2):
                        pe.wait_ge(b_xn, i - 1)
                        after(pe, b_xt, i - 2)
                        src = x2[half_0 if t >= 2 else 1 - half_0]
                        for k in range(ND):
                            last = pe.transpose(bank[4][:, k * P:(k + 1) * P], src[:, (t - 2) % G, k * P:(k + 1) * P], ident[:, :])
                        last.then_inc(b_turned, 1)
                    if there(i - 3):
                        u = (t - 3) % G
                        pe.wait_ge(b_xt, i - 2)
                        if u == 0:
                            after(pe, b_lg, c)
                        for k in range(ND):
                            last = pe.matmul(bank[6][:, u * E:(u + 1) * E], xn[:, 1 - s, k * P:(k + 1) * P],
                                             wg_sb[:, k, :], start=k == 0, stop=k == ND - 1)
                        last.then_inc(b_logit, 1)
                    if t >= 3 and group_there(c - 2):
                        invert(c - 2, (0, 1) if t == 3 else (2, 3, 4))

            add_zeros(bank[7][:, 0:2 * TOP * KEY], 2 * TOP * KEY, True).then_inc(b_inv, 1)
            spread(0, 0)
            spread(1, 1)
            attend(0, 0)
            attend(1, 1)
            with pe.Fori(1, (NG - 1) // 2) as k:
                attend(k * 2, 0)
                attend(k * 2 + 1, 1)
            for c in range(NG - 1, NG + 2):
                attend(c, c % 2)

            pe.wait_ge(tables, 2)
            up = [2, 3, 4, 7]

            def turn_rows(e, s, g, js):
                for j in js:
                    m = min(P, CAP - (g * ST + j) * P)
                    k = (e * CH + g) * ST + j
                    if j == 0:
                        pe.wait_ge(got[s][g], gathered(e, s))
                    after(pe, e_xlo, k - 1)
                    for kk in range(ND):
                        last = pe.transpose(bank[(s + g * ST + j) % 2][:, kk * P:kk * P + m],
                                            rows[s][0:m, g * ST + j, kk * P:(kk + 1) * P], ident[0:m, 0:m])
                    last.then_inc(e_turned, 1)

            def expert(e, s, last_one):
                for g in range(CH):
                    w = min(ST * P, CAP - g * ST * P)
                    u = e * CH + g
                    v = (s + g) % 2
                    if g == 0:
                        pe.wait_ge(w1_lo, e + 1)
                    pe.wait_ge(e_xlo, u * ST + ST)
                    for m in range(NM):
                        after(pe, e_gelu, u * NM + m - 3)
                        for k in range(ND):
                            cut = slice(m * P, (m + 1) * P)
                            last = three(bank[up[m % 4]][:, 0:w], w1h[s][:, k, cut], w1l[s][:, k, cut],
                                         xt_h[:, v, k, 0:w], xt_l[:, v, k, 0:w], k == 0, k == ND - 1)
                        last.then_inc(e_up, 1)
                    nxt = (e, s, g + 1) if g + 1 < CH else None if last_one else (e + 1, 1 - s, 0)
                    if nxt:
                        turn_rows(*nxt, (0, 1))
                    if g == 0:
                        pe.wait_ge(w2_lo, e + 1)
                    for j in range(ST):
                        mj = min(P, w - j * P)
                        kj = u * ST + j
                        after(pe, e_y, kj - 1)
                        dst = bank[5 + (s + g * ST + j) % 2][0:mj, 0:D]
                        for m in range(NM):
                            if j == 0:
                                pe.wait_ge(e_hlo, u * NM + m + 1)
                            cut = slice(j * P, j * P + mj)
                            last = three(dst, hid_h[v][:, m, cut], hid_l[v][:, m, cut], w2h[s][:, m, :], w2l[s][:, m, :],
                                         m == 0, m == NM - 1)
                        last.then_inc(e_down, 1)
                        if j == 0 and nxt:
                            turn_rows(*nxt, (2,))

            turn_rows(0, 0, 0, range(ST))
            expert(0, 0, False)
            with pe.Fori(0, (E - 2) // 2) as k:
                expert(k * 2 + 1, 1, False)
                expert(k * 2 + 2, 0, False)
            expert(E - 1, 1, True)


_INS = ["x", "txt", "L0_tok_W", "L0_tok_b", "L0_tok_cls_token", "L0_tok_pos_embedding", "L0_attn_Wqkv", "L0_attn_bqkv",
        "L0_attn_Wout", "L0_attn_bout", "L0_ffn_wg", "L0_ffn_w1", "L0_ffn_b1", "L0_ffn_w2", "L0_ffn_b2"]


def kernel(**inputs):
    import concourse.bacc as bacc
    from concourse.bass_utils import run_bass_kernel_spmd

    nc = bacc.Bacc("TRN2", target_bir_lowering=False, num_devices=1)
    arrays, args = {}, []
    for name in _INS:
        a = np.ascontiguousarray(inputs[name])
        arrays[f"in_{name}"] = a
        args.append(nc.dram_tensor(f"in_{name}", a.shape, mybir.dt.from_np(a.dtype), kind="ExternalInput").ap())
    out = nc.dram_tensor("out_rows", (N + P, D), F32, kind="ExternalOutput").ap()
    build(nc, *args, out)
    r = run_bass_kernel_spmd(nc, [arrays], core_ids=[0])
    return r.results[0]["out_rows"][0:N].reshape(B, SEQ, D)
```
